# Optimizing a Trainium2 kernel written in Bass

```python
import numpy as np
import jax
import jax.numpy as jnp

def _softmax(x, axis=-1):
    return jax.nn.softmax(x, axis=axis)

def _gelu(x):
    return jax.nn.gelu(x, approximate=True)

def _silu(x):
    return jax.nn.silu(x)

def _sigmoid(x):
    return jax.nn.sigmoid(x)

def _layernorm(x, axis=-1, eps=1e-05):
    m = jnp.mean(x, axis=axis, keepdims=True)
    v = jnp.var(x, axis=axis, keepdims=True)
    return (x - m) / jnp.sqrt(v + eps)

def _scatter_add(tgt, idx, src, axis=0):
    return tgt.at[idx].add(src)

def _segment_sum(src, seg, n):
    return jax.ops.segment_sum(src, seg, n)
kernel_name = 'mk_gnn_ffn_d4_gnn_r32_0cc513'

def setup_inputs(seed: int=0):
    np.random.seed(seed)
    _w = jnp.asarray

    def _rec_inputs():
        import jax
        import jax.numpy as jnp
        _gk = jax.random.key(seed)
        x = -0.0003713 + 1 * jax.random.normal(jax.random.fold_in(_gk, 1), (3125, 256), jnp.float32)
        src = jax.random.randint(jax.random.fold_in(_gk, 2), (50000,), 0, 3125, jnp.int32)
        dst = jnp.minimum((3125 * jax.random.uniform(jax.random.fold_in(_gk, 3), (50000,)) ** 2.0).astype(jnp.int32), 99999)
        _o = jnp.argsort(dst, stable=True)
        src = src[_o]
        dst = dst[_o]
        edge_attr_3 = -1.09012e-05 + 0.99985 * jax.random.normal(jax.random.fold_in(_gk, 12), (50000, 3), jnp.float32)
        edge_attr_64 = 0.000279952 + 1.00013 * jax.random.normal(jax.random.fold_in(_gk, 13), (50000, 64), jnp.float32)
        edge_type_16 = jax.random.randint(jax.random.fold_in(_gk, 15), (50000,), 0, 16, jnp.int32)
        edge_weight = jax.random.uniform(jax.random.fold_in(_gk, 16), (50000,), jnp.float32, 0.0, 1)
        edge_weight1 = jax.random.uniform(jax.random.fold_in(_gk, 17), (50000, 1), jnp.float32, 0.0, 0.999998)
        return (x, src, dst, edge_attr_3, edge_attr_64, edge_type_16, edge_weight, edge_weight1)
    x, src, dst, edge_attr_3, edge_attr_64, edge_type_16, edge_weight, edge_weight1 = _rec_inputs()

    def _L0_gnn_setup():
        import jax, jax.numpy as jnp
        import numpy as np
        N, E, D, H, C = (50000, 50000, 256, 8, 32)
        key = jax.random.key(seed)
        ks = jax.random.split(key, 7)
        feat = jax.random.normal(ks[0], (N, D), dtype=jnp.float32)
        edge_weight = jax.random.uniform(ks[1], (E,), dtype=jnp.float32)
        W_lin = jax.random.normal(ks[2], (D, H * C), dtype=jnp.float32) * (1.0 / np.sqrt(D))
        att_l = jax.random.normal(ks[3], (1, H, C), dtype=jnp.float32) * (1.0 / np.sqrt(H))
        att_r = jax.random.normal(ks[4], (1, H, C), dtype=jnp.float32) * (1.0 / np.sqrt(H))
        W_res = jax.random.normal(ks[5], (D, H * C), dtype=jnp.float32) * (1.0 / np.sqrt(D))
        edge_index = jax.random.randint(ks[6], (2, E), 0, N, dtype=jnp.int32)
        return {'feat': feat, 'edge_weight': edge_weight, 'W_lin': W_lin, 'att_l': att_l, 'att_r': att_r, 'W_res': W_res, 'edge_index': edge_index}
    _L0_gnn_all = _L0_gnn_setup()
    _L0_gnn_in = {k: v for k, v in _L0_gnn_all.items() if k in ('W_lin', 'att_l', 'att_r', 'W_res')}
    del _L0_gnn_all

    def _L0_ffn_setup():
        import jax, jax.numpy as jnp
        import numpy as np
        B, N, D = (16, 128, 256)
        NUM_EXPERTS, TOP_K, HEADS = (4, 2, 4)
        N_EDGES = 32768
        LN_EPS = 1e-05

        def _layernorm(x, g, b):
            mu = x.mean(-1, keepdims=True)
            var = ((x - mu) ** 2).mean(-1, keepdims=True)
            return (x - mu) * jax.lax.rsqrt(var + LN_EPS) * g + b

        def _forward(x, edge_index, W_gat, att_src, att_dst, b_gat, ln_gamma, ln_beta, W1, b1, W2, b2):
            Bc, Nc, Dc = x.shape
            M = Bc * Nc
            x_flat = x.reshape(M, Dc)
            h = (x_flat @ W_gat).reshape(M, HEADS, NUM_EXPERTS)
            loops = jnp.arange(M, dtype=edge_index.dtype)
            src = jnp.concatenate([edge_index[0], loops])
            dst = jnp.concatenate([edge_index[1], loops])
            a_src = (h * att_src).sum(-1)
            a_dst = (h * att_dst).sum(-1)
            e = jax.nn.leaky_relu(a_src[src] + a_dst[dst], negative_slope=0.2)
            e_max = jax.ops.segment_max(e, dst, num_segments=M)
            ee = jnp.exp(e - e_max[dst])
            denom = jax.ops.segment_sum(ee, dst, num_segments=M)
            alpha = ee / (denom[dst] + 1e-16)
            msg = h[src] * alpha[:, :, None]
            agg = jax.ops.segment_sum(msg, dst, num_segments=M).reshape(M, HEADS * NUM_EXPERTS) + b_gat
            scores = _layernorm(agg, ln_gamma, ln_beta).reshape(M, HEADS, NUM_EXPERTS).mean(1)
            scores = scores.reshape(Bc, Nc, NUM_EXPERTS)
            topk_s, topk_i = jax.lax.top_k(scores, TOP_K)
            w = jax.nn.softmax(topk_s, axis=-1)
            out = jnp.zeros_like(x)
            for ei in range(NUM_EXPERTS):
                g = jnp.where(topk_i == ei, w, 0.0).sum(-1)
                hh = jax.nn.gelu(x @ W1[ei] + b1[ei], approximate=False)
                out = out + g[..., None] * (hh @ W2[ei] + b2[ei])
            return out
        key = jax.random.key(seed)
        ks = jax.random.split(key, 8)
        s = 0.05
        return {'x': jax.random.normal(ks[0], (B, N, D), jnp.float32), 'W_gat': jax.random.normal(ks[1], (D, HEADS * NUM_EXPERTS), jnp.float32) * s, 'att_src': jax.random.normal(ks[2], (HEADS, NUM_EXPERTS), jnp.float32) * s, 'att_dst': jax.random.normal(ks[3], (HEADS, NUM_EXPERTS), jnp.float32) * s, 'b_gat': jnp.zeros((HEADS * NUM_EXPERTS,), jnp.float32), 'ln_gamma': jnp.ones((HEADS * NUM_EXPERTS,), jnp.float32), 'ln_beta': jnp.zeros((HEADS * NUM_EXPERTS,), jnp.float32), 'W1': jax.random.normal(ks[4], (NUM_EXPERTS, D, 2 * D), jnp.float32) * s, 'b1': jnp.zeros((NUM_EXPERTS, 2 * D), jnp.float32), 'W2': jax.random.normal(ks[5], (NUM_EXPERTS, 2 * D, D), jnp.float32) * s, 'b2': jnp.zeros((NUM_EXPERTS, D), jnp.float32), 'edge_index': jax.random.randint(ks[6], (2, N_EDGES), 0, B * N, jnp.int32)}
    _L0_ffn_all = _L0_ffn_setup()
    _L0_ffn_in = {k: v for k, v in _L0_ffn_all.items() if k in ('W_gat', 'att_src', 'att_dst', 'b_gat', 'ln_gamma', 'ln_beta', 'W1', 'b1', 'W2', 'b2', 'edge_index')}
    del _L0_ffn_all

    def _L1_gnn_setup():
        import jax, jax.numpy as jnp
        import numpy as np
        N_NODES = 625
        N_EDGES = 10000
        H = 256
        R = 16
        B = 128
        SUB = H // B

        def _rel_graph_conv_bdd(x, src, dst, etype, norm, w, loop_w, bias):
            e = src.shape[0]
            n = x.shape[0]
            nb = w.shape[1]
            xs = x[src].reshape(e, nb, -1)
            we = w[etype]
            msg = jnp.einsum('ebi,ebio->ebo', xs, we)
            msg = msg.reshape(e, -1) * norm
            agg = jax.ops.segment_sum(msg, dst, num_segments=n)
            return agg + bias + x @ loop_w
        key = jax.random.key(seed)
        ks = jax.random.split(key, 11)
        scale = 1.0 / np.sqrt(H)
        return {'x': jax.random.normal(ks[0], (N_NODES, H), jnp.float32), 'src': jax.random.randint(ks[1], (N_EDGES,), 0, N_NODES), 'dst': jax.random.randint(ks[2], (N_EDGES,), 0, N_NODES), 'etype': jax.random.randint(ks[3], (N_EDGES,), 0, R), 'norm': jax.random.uniform(ks[4], (N_EDGES, 1), jnp.float32), 'w1': jax.random.normal(ks[5], (R, B, SUB, SUB), jnp.float32) * scale, 'loop_w1': jax.random.normal(ks[6], (H, H), jnp.float32) * scale, 'b1': jnp.zeros((H,), jnp.float32), 'w2': jax.random.normal(ks[7], (R, B, SUB, SUB), jnp.float32) * scale, 'loop_w2': jax.random.normal(ks[8], (H, H), jnp.float32) * scale, 'b2': jnp.zeros((H,), jnp.float32)}
    _L1_gnn_all = _L1_gnn_setup()
    _L1_gnn_in = {k: v for k, v in _L1_gnn_all.items() if k in ('w1', 'loop_w1', 'b1', 'w2', 'loop_w2', 'b2')}
    del _L1_gnn_all

    def _L1_ffn_setup():
        import jax, jax.numpy as jnp
        import numpy as np
        E = 8
        K = 2
        D = 256
        H = 512
        DOUT = 256
        EPS = 1e-05
        key = jax.random.key(seed)
        ks = jax.random.split(key, 9)
        s = 0.02
        return {'x': jax.random.normal(ks[0], (4, 256, D), jnp.float32), 'gamma': 1.0 + 0.05 * jax.random.normal(ks[1], (D,), jnp.float32), 'beta': 0.05 * jax.random.normal(ks[2], (D,), jnp.float32), 'Wr': 0.01 * jax.random.normal(ks[3], (D, E), jnp.float32), 'br': jnp.zeros((E,), jnp.float32), 'W1': s * jax.random.normal(ks[4], (E, D, H), jnp.float32), 'b1': s * jax.random.normal(ks[5], (E, H), jnp.float32), 'W2': s * jax.random.normal(ks[6], (E, H, DOUT), jnp.float32), 'b2': s * jax.random.normal(ks[7], (E, DOUT), jnp.float32)}
    _L1_ffn_all = _L1_ffn_setup()
    _L1_ffn_in = {k: v for k, v in _L1_ffn_all.items() if k in ('gamma', 'beta', 'Wr', 'br', 'W1', 'b1', 'W2', 'b2')}
    del _L1_ffn_all

    def _L2_gnn_setup():
        import jax, jax.numpy as jnp
        import numpy as np
        N = 50000
        E = 12500
        IN = 256
        H = 8
        D = 32
        EF = 3
        key = jax.random.key(seed)
        ks = jax.random.split(key, 8)
        x = jax.random.normal(ks[0], (N, IN), dtype=jnp.float32)
        edge_index = jax.random.randint(ks[1], (2, E), 0, N, dtype=jnp.int64)
        edge_attr = jax.random.normal(ks[2], (E, EF), dtype=jnp.float32)
        W = jax.random.normal(ks[3], (H * D, IN), dtype=jnp.float32) * np.float32(np.sqrt(2.0 / (IN + H * D)))
        a_src = jax.random.normal(ks[4], (H, D), dtype=jnp.float32) * np.float32(np.sqrt(2.0 / (H + D)))
        a_dst = jax.random.normal(ks[5], (H, D), dtype=jnp.float32) * np.float32(np.sqrt(2.0 / (H + D)))
        edge_W = jax.random.normal(ks[6], (H * D, EF), dtype=jnp.float32) * np.float32(np.sqrt(2.0 / (EF + H * D)))
        edge_b = jnp.zeros((H * D,), dtype=jnp.float32)
        bias = jnp.zeros((H * D,), dtype=jnp.float32)
        return {'x': x, 'W': W, 'a_src': a_src, 'a_dst': a_dst, 'edge_W': edge_W, 'edge_b': edge_b, 'bias': bias, 'edge_attr': edge_attr, 'edge_index': edge_index}
    _L2_gnn_all = _L2_gnn_setup()
    _L2_gnn_in = {k: v for k, v in _L2_gnn_all.items() if k in ('W', 'a_src', 'a_dst', 'edge_W', 'edge_b', 'bias')}
    del _L2_gnn_all

    def _L2_ffn_setup():
        import jax, jax.numpy as jnp
        import numpy as np
        B, A = (128, 8)
        IN, OUT = (256, 256)
        SH1, SH2 = (256, 128)
        EH1, EH2 = (128, 64)
        E, TOPK = (4, 2)

        def _shared_mlp(x, W1, b1, W2, b2, W3, b3):
            h = jax.nn.relu(x @ W1 + b1)
            h = jax.nn.relu(h @ W2 + b2)
            return h @ W3 + b3

        def _experts_mlp(x, eW1, eb1, eW2, eb2, eW3, eb3):
            h = jax.nn.relu(jnp.einsum('baf,efh->ebah', x, eW1) + eb1[:, None, None, :])
            h = jax.nn.relu(jnp.einsum('ebah,ehg->ebag', h, eW2) + eb2[:, None, None, :])
            o = jnp.einsum('ebag,ego->ebao', h, eW3) + eb3[:, None, None, :]
            return jnp.moveaxis(o, 0, -1)
        key = jax.random.key(seed)
        ks = jax.random.split(key, 16)
        s = 0.05
        return {'x': jax.random.normal(ks[0], (B, A, IN), jnp.float32), 'sW1': jax.random.normal(ks[1], (IN, SH1), jnp.float32) * s, 'sb1': jnp.zeros((SH1,), jnp.float32), 'sW2': jax.random.normal(ks[2], (SH1, SH2), jnp.float32) * s, 'sb2': jnp.zeros((SH2,), jnp.float32), 'sW3': jax.random.normal(ks[3], (SH2, OUT), jnp.float32) * s, 'sb3': jnp.zeros((OUT,), jnp.float32), 'eW1': jax.random.normal(ks[4], (E, IN, EH1), jnp.float32) * s, 'eb1': jnp.zeros((E, EH1), jnp.float32), 'eW2': jax.random.normal(ks[5], (E, EH1, EH2), jnp.float32) * s, 'eb2': jnp.zeros((E, EH2), jnp.float32), 'eW3': jax.random.normal(ks[6], (E, EH2, OUT), jnp.float32) * s, 'eb3': jnp.zeros((E, OUT), jnp.float32), 'gW': jax.random.normal(ks[7], (IN, E), jnp.float32) * s, 'gb': jnp.zeros((E,), jnp.float32)}
    _L2_ffn_all = _L2_ffn_setup()
    _L2_ffn_in = {k: v for k, v in _L2_ffn_all.items() if k in ('sW1', 'sb1', 'sW2', 'sb2', 'sW3', 'sb3', 'eW1', 'eb1', 'eW2', 'eb2', 'eW3', 'eb3', 'gW', 'gb')}
    del _L2_ffn_all

    def _L3_gnn_setup():
        import jax, jax.numpy as jnp
        import numpy as np
        N = 3125
        E = 10000
        CIN = 256
        EDIM = 64
        EEMB = 256
        H = 1024
        LN_EPS = 1e-05

        def _ln(x, g, b):
            m = jnp.mean(x, axis=-1, keepdims=True)
            v = jnp.var(x, axis=-1, keepdims=True)
            return (x - m) * jax.lax.rsqrt(v + LN_EPS) * g + b
        key = jax.random.key(seed)
        ks = jax.random.split(key, 16)

        def w(k, i, o):
            return (jax.random.normal(k, (i, o), jnp.float32) / np.sqrt(i)).astype(jnp.float32)
        return {'x': jax.random.normal(ks[0], (N, CIN), jnp.float32), 'edge_index': jax.random.randint(ks[1], (2, E), 0, N, dtype=jnp.int64), 'edge_attr': jax.random.normal(ks[2], (E, EDIM), jnp.float32), 'eps': jnp.float32(0.0), 'ee_w1': w(ks[3], EDIM, EEMB), 'ee_b1': jnp.zeros((EEMB,), jnp.float32), 'ee_w2': w(ks[4], EEMB, CIN), 'ee_b2': jnp.zeros((CIN,), jnp.float32), 'w1': w(ks[5], CIN, H), 'b1': jnp.zeros((H,), jnp.float32), 'g1': jnp.ones((H,), jnp.float32), 'be1': jnp.zeros((H,), jnp.float32), 'w2': w(ks[6], H, H), 'b2': jnp.zeros((H,), jnp.float32), 'g2': jnp.ones((H,), jnp.float32), 'be2': jnp.zeros((H,), jnp.float32), 'w3': w(ks[7], H, CIN), 'b3': jnp.zeros((CIN,), jnp.float32), 'bn_g': jnp.ones((CIN,), jnp.float32), 'bn_b': jnp.zeros((CIN,), jnp.float32)}
    _L3_gnn_all = _L3_gnn_setup()
    _L3_gnn_in = {k: v for k, v in _L3_gnn_all.items() if k in ('eps', 'ee_w1', 'ee_b1', 'ee_w2', 'ee_b2', 'w1', 'b1', 'g1', 'be1', 'w2', 'b2', 'g2', 'be2', 'w3', 'b3', 'bn_g', 'bn_b')}
    del _L3_gnn_all

    def _L3_ffn_setup():
        import jax, jax.numpy as jnp
        import numpy as np
        DIM = 256
        H = 8
        D = 64
        G = 64
        INNER = H * D
        SCALE = D ** (-0.5)
        key = jax.random.key(seed)
        ks = jax.random.split(key, 12)
        B, N = (4, 512)
        x = jax.random.normal(ks[0], (B, N, DIM), dtype=jnp.float32)
        s = lambda fan_in: 1.0 / np.sqrt(fan_in)
        W_fx = jax.random.normal(ks[1], (DIM, INNER), dtype=jnp.float32) * s(DIM)
        b_fx = jnp.zeros((INNER,), dtype=jnp.float32)
        W_x = jax.random.normal(ks[2], (DIM, INNER), dtype=jnp.float32) * s(DIM)
        b_x = jnp.zeros((INNER,), dtype=jnp.float32)
        A = jax.random.normal(ks[3], (G, D), dtype=jnp.float32)
        Q, _ = jnp.linalg.qr(A.T)
        W_slice = Q[:, :G].astype(jnp.float32)
        b_slice = jnp.zeros((G,), dtype=jnp.float32)
        W_q = jax.random.normal(ks[4], (D, D), dtype=jnp.float32) * s(D)
        W_k = jax.random.normal(ks[5], (D, D), dtype=jnp.float32) * s(D)
        W_v = jax.random.normal(ks[6], (D, D), dtype=jnp.float32) * s(D)
        W_out = jax.random.normal(ks[7], (INNER, DIM), dtype=jnp.float32) * s(INNER)
        b_out = jnp.zeros((DIM,), dtype=jnp.float32)
        temperature = jnp.ones((1, H, 1, 1), dtype=jnp.float32) * 0.5
        return {'x': x, 'W_fx': W_fx, 'b_fx': b_fx, 'W_x': W_x, 'b_x': b_x, 'W_slice': W_slice, 'b_slice': b_slice, 'W_q': W_q, 'W_k': W_k, 'W_v': W_v, 'W_out': W_out, 'b_out': b_out, 'temperature': temperature}
    _L3_ffn_all = _L3_ffn_setup()
    _L3_ffn_in = {k: v for k, v in _L3_ffn_all.items() if k in ('W_fx', 'b_fx', 'W_x', 'b_x', 'W_slice', 'b_slice', 'W_q', 'W_k', 'W_v', 'W_out', 'b_out', 'temperature')}
    del _L3_ffn_all
    return {'x': x, 'src': src, 'dst': dst, 'edge_attr_3': edge_attr_3, 'edge_attr_64': edge_attr_64, 'edge_type_16': edge_type_16, 'edge_weight': edge_weight, 'edge_weight1': edge_weight1, 'L0_gnn_W_lin': _L0_gnn_in['W_lin'], 'L0_gnn_att_l': _L0_gnn_in['att_l'], 'L0_gnn_att_r': _L0_gnn_in['att_r'], 'L0_gnn_W_res': _L0_gnn_in['W_res'], 'L0_ffn_W_gat': _L0_ffn_in['W_gat'], 'L0_ffn_att_src': _L0_ffn_in['att_src'], 'L0_ffn_att_dst': _L0_ffn_in['att_dst'], 'L0_ffn_b_gat': _L0_ffn_in['b_gat'], 'L0_ffn_ln_gamma': _L0_ffn_in['ln_gamma'], 'L0_ffn_ln_beta': _L0_ffn_in['ln_beta'], 'L0_ffn_W1': _L0_ffn_in['W1'], 'L0_ffn_b1': _L0_ffn_in['b1'], 'L0_ffn_W2': _L0_ffn_in['W2'], 'L0_ffn_b2': _L0_ffn_in['b2'], 'L0_ffn_edge_index': _L0_ffn_in['edge_index'], 'L1_gnn_w1': _L1_gnn_in['w1'], 'L1_gnn_loop_w1': _L1_gnn_in['loop_w1'], 'L1_gnn_b1': _L1_gnn_in['b1'], 'L1_gnn_w2': _L1_gnn_in['w2'], 'L1_gnn_loop_w2': _L1_gnn_in['loop_w2'], 'L1_gnn_b2': _L1_gnn_in['b2'], 'L1_ffn_gamma': _L1_ffn_in['gamma'], 'L1_ffn_beta': _L1_ffn_in['beta'], 'L1_ffn_Wr': _L1_ffn_in['Wr'], 'L1_ffn_br': _L1_ffn_in['br'], 'L1_ffn_W1': _L1_ffn_in['W1'], 'L1_ffn_b1': _L1_ffn_in['b1'], 'L1_ffn_W2': _L1_ffn_in['W2'], 'L1_ffn_b2': _L1_ffn_in['b2'], 'L2_gnn_W': _L2_gnn_in['W'], 'L2_gnn_a_src': _L2_gnn_in['a_src'], 'L2_gnn_a_dst': _L2_gnn_in['a_dst'], 'L2_gnn_edge_W': _L2_gnn_in['edge_W'], 'L2_gnn_edge_b': _L2_gnn_in['edge_b'], 'L2_gnn_bias': _L2_gnn_in['bias'], 'L2_ffn_sW1': _L2_ffn_in['sW1'], 'L2_ffn_sb1': _L2_ffn_in['sb1'], 'L2_ffn_sW2': _L2_ffn_in['sW2'], 'L2_ffn_sb2': _L2_ffn_in['sb2'], 'L2_ffn_sW3': _L2_ffn_in['sW3'], 'L2_ffn_sb3': _L2_ffn_in['sb3'], 'L2_ffn_eW1': _L2_ffn_in['eW1'], 'L2_ffn_eb1': _L2_ffn_in['eb1'], 'L2_ffn_eW2': _L2_ffn_in['eW2'], 'L2_ffn_eb2': _L2_ffn_in['eb2'], 'L2_ffn_eW3': _L2_ffn_in['eW3'], 'L2_ffn_eb3': _L2_ffn_in['eb3'], 'L2_ffn_gW': _L2_ffn_in['gW'], 'L2_ffn_gb': _L2_ffn_in['gb'], 'L3_gnn_eps': _L3_gnn_in['eps'], 'L3_gnn_ee_w1': _L3_gnn_in['ee_w1'], 'L3_gnn_ee_b1': _L3_gnn_in['ee_b1'], 'L3_gnn_ee_w2': _L3_gnn_in['ee_w2'], 'L3_gnn_ee_b2': _L3_gnn_in['ee_b2'], 'L3_gnn_w1': _L3_gnn_in['w1'], 'L3_gnn_b1': _L3_gnn_in['b1'], 'L3_gnn_g1': _L3_gnn_in['g1'], 'L3_gnn_be1': _L3_gnn_in['be1'], 'L3_gnn_w2': _L3_gnn_in['w2'], 'L3_gnn_b2': _L3_gnn_in['b2'], 'L3_gnn_g2': _L3_gnn_in['g2'], 'L3_gnn_be2': _L3_gnn_in['be2'], 'L3_gnn_w3': _L3_gnn_in['w3'], 'L3_gnn_b3': _L3_gnn_in['b3'], 'L3_gnn_bn_g': _L3_gnn_in['bn_g'], 'L3_gnn_bn_b': _L3_gnn_in['bn_b'], 'L3_ffn_W_fx': _L3_ffn_in['W_fx'], 'L3_ffn_b_fx': _L3_ffn_in['b_fx'], 'L3_ffn_W_x': _L3_ffn_in['W_x'], 'L3_ffn_b_x': _L3_ffn_in['b_x'], 'L3_ffn_W_slice': _L3_ffn_in['W_slice'], 'L3_ffn_b_slice': _L3_ffn_in['b_slice'], 'L3_ffn_W_q': _L3_ffn_in['W_q'], 'L3_ffn_W_k': _L3_ffn_in['W_k'], 'L3_ffn_W_v': _L3_ffn_in['W_v'], 'L3_ffn_W_out': _L3_ffn_in['W_out'], 'L3_ffn_b_out': _L3_ffn_in['b_out'], 'L3_ffn_temperature': _L3_ffn_in['temperature']}

def reference(x, src, dst, edge_attr_3, edge_attr_64, edge_type_16, edge_weight, edge_weight1, L0_gnn_W_lin, L0_gnn_att_l, L0_gnn_att_r, L0_gnn_W_res, L0_ffn_W_gat, L0_ffn_att_src, L0_ffn_att_dst, L0_ffn_b_gat, L0_ffn_ln_gamma, L0_ffn_ln_beta, L0_ffn_W1, L0_ffn_b1, L0_ffn_W2, L0_ffn_b2, L0_ffn_edge_index, L1_gnn_w1, L1_gnn_loop_w1, L1_gnn_b1, L1_gnn_w2, L1_gnn_loop_w2, L1_gnn_b2, L1_ffn_gamma, L1_ffn_beta, L1_ffn_Wr, L1_ffn_br, L1_ffn_W1, L1_ffn_b1, L1_ffn_W2, L1_ffn_b2, L2_gnn_W, L2_gnn_a_src, L2_gnn_a_dst, L2_gnn_edge_W, L2_gnn_edge_b, L2_gnn_bias, L2_ffn_sW1, L2_ffn_sb1, L2_ffn_sW2, L2_ffn_sb2, L2_ffn_sW3, L2_ffn_sb3, L2_ffn_eW1, L2_ffn_eb1, L2_ffn_eW2, L2_ffn_eb2, L2_ffn_eW3, L2_ffn_eb3, L2_ffn_gW, L2_ffn_gb, L3_gnn_eps, L3_gnn_ee_w1, L3_gnn_ee_b1, L3_gnn_ee_w2, L3_gnn_ee_b2, L3_gnn_w1, L3_gnn_b1, L3_gnn_g1, L3_gnn_be1, L3_gnn_w2, L3_gnn_b2, L3_gnn_g2, L3_gnn_be2, L3_gnn_w3, L3_gnn_b3, L3_gnn_bn_g, L3_gnn_bn_b, L3_ffn_W_fx, L3_ffn_b_fx, L3_ffn_W_x, L3_ffn_b_x, L3_ffn_W_slice, L3_ffn_b_slice, L3_ffn_W_q, L3_ffn_W_k, L3_ffn_W_v, L3_ffn_W_out, L3_ffn_b_out, L3_ffn_temperature):
    import jax
    import jax.numpy as jnp

    def _L0_gnn_ref(feat, edge_weight, W_lin, att_l, att_r, W_res, edge_index):
        import jax, jax.numpy as jnp
        import numpy as np
        N, E, D, H, C = (50000, 50000, 256, 8, 32)
        n_nodes = feat.shape[0]
        h, c = (att_l.shape[1], att_l.shape[2])
        src, dst = (edge_index[0], edge_index[1])
        x = (feat @ W_lin).reshape(n_nodes, h, c)
        alpha_l = (x * att_l).sum(-1)
        alpha_r = (x * att_r).sum(-1)
        alpha = alpha_l[src] + alpha_r[dst]
        alpha = edge_weight[:, None] * alpha
        alpha = jnp.where(alpha > 0, alpha, 0.2 * alpha)
        amax = jax.lax.stop_gradient(jax.ops.segment_max(alpha, dst, num_segments=n_nodes))
        ex = jnp.exp(alpha - amax[dst])
        denom = jax.ops.segment_sum(ex, dst, num_segments=n_nodes)
        coeff = ex / (denom[dst] + 1e-16)
        msg = x[src] * coeff[:, :, None]
        agg = jax.ops.segment_sum(msg, dst, num_segments=n_nodes)
        out = jax.nn.elu(agg).reshape(n_nodes, h * c)
        out = out + feat @ W_res
        return out

    def _L0_ffn_ref(x, W_gat, att_src, att_dst, b_gat, ln_gamma, ln_beta, W1, b1, W2, b2, edge_index):
        import jax, jax.numpy as jnp
        import numpy as np
        B, N, D = (16, 128, 256)
        NUM_EXPERTS, TOP_K, HEADS = (4, 2, 4)
        N_EDGES = 32768
        LN_EPS = 1e-05

        def _layernorm(x, g, b):
            mu = x.mean(-1, keepdims=True)
            var = ((x - mu) ** 2).mean(-1, keepdims=True)
            return (x - mu) * jax.lax.rsqrt(var + LN_EPS) * g + b

        def _forward(x, edge_index, W_gat, att_src, att_dst, b_gat, ln_gamma, ln_beta, W1, b1, W2, b2):
            Bc, Nc, Dc = x.shape
            M = Bc * Nc
            x_flat = x.reshape(M, Dc)
            h = (x_flat @ W_gat).reshape(M, HEADS, NUM_EXPERTS)
            loops = jnp.arange(M, dtype=edge_index.dtype)
            src = jnp.concatenate([edge_index[0], loops])
            dst = jnp.concatenate([edge_index[1], loops])
            a_src = (h * att_src).sum(-1)
            a_dst = (h * att_dst).sum(-1)
            e = jax.nn.leaky_relu(a_src[src] + a_dst[dst], negative_slope=0.2)
            e_max = jax.ops.segment_max(e, dst, num_segments=M)
            ee = jnp.exp(e - e_max[dst])
            denom = jax.ops.segment_sum(ee, dst, num_segments=M)
            alpha = ee / (denom[dst] + 1e-16)
            msg = h[src] * alpha[:, :, None]
            agg = jax.ops.segment_sum(msg, dst, num_segments=M).reshape(M, HEADS * NUM_EXPERTS) + b_gat
            scores = _layernorm(agg, ln_gamma, ln_beta).reshape(M, HEADS, NUM_EXPERTS).mean(1)
            scores = scores.reshape(Bc, Nc, NUM_EXPERTS)
            topk_s, topk_i = jax.lax.top_k(scores, TOP_K)
            w = jax.nn.softmax(topk_s, axis=-1)
            out = jnp.zeros_like(x)
            for ei in range(NUM_EXPERTS):
                g = jnp.where(topk_i == ei, w, 0.0).sum(-1)
                hh = jax.nn.gelu(x @ W1[ei] + b1[ei], approximate=False)
                out = out + g[..., None] * (hh @ W2[ei] + b2[ei])
            return out
        return _forward(x, edge_index, W_gat, att_src, att_dst, b_gat, ln_gamma, ln_beta, W1, b1, W2, b2)

    def _L1_gnn_ref(x, src, dst, etype, norm, w1, loop_w1, b1, w2, loop_w2, b2):
        import jax, jax.numpy as jnp
        import numpy as np
        N_NODES = 625
        N_EDGES = 10000
        H = 256
        R = 16
        B = 128
        SUB = H // B

        def _rel_graph_conv_bdd(x, src, dst, etype, norm, w, loop_w, bias):
            e = src.shape[0]
            n = x.shape[0]
            nb = w.shape[1]
            xs = x[src].reshape(e, nb, -1)
            we = w[etype]
            msg = jnp.einsum('ebi,ebio->ebo', xs, we)
            msg = msg.reshape(e, -1) * norm
            agg = jax.ops.segment_sum(msg, dst, num_segments=n)
            return agg + bias + x @ loop_w
        h = jax.nn.relu(_rel_graph_conv_bdd(x, src, dst, etype, norm, w1, loop_w1, b1))
        return _rel_graph_conv_bdd(h, src, dst, etype, norm, w2, loop_w2, b2)

    def _L1_ffn_ref(x, gamma, beta, Wr, br, W1, b1, W2, b2):
        import jax, jax.numpy as jnp
        import numpy as np
        E = 8
        K = 2
        D = 256
        H = 512
        DOUT = 256
        EPS = 1e-05
        mu = jnp.mean(x, axis=-1, keepdims=True)
        var = jnp.mean(jnp.square(x - mu), axis=-1, keepdims=True)
        xn = (x - mu) * jax.lax.rsqrt(var + EPS) * gamma + beta
        logits = jnp.einsum('bsd,de->bse', xn, Wr) + br
        top_vals, top_idx = jax.lax.top_k(logits, K)
        w = jax.nn.softmax(top_vals, axis=-1)
        w_full = jnp.einsum('bsk,bske->bse', w, jax.nn.one_hot(top_idx, E, dtype=w.dtype))
        y = jnp.zeros(x.shape[:-1] + (DOUT,), x.dtype)
        for e in range(E):
            h = jax.nn.gelu(jnp.einsum('bsd,dh->bsh', xn, W1[e]) + b1[e], approximate=False)
            y_e = jnp.einsum('bsh,hd->bsd', h, W2[e]) + b2[e]
            y = y + y_e * w_full[..., e, None]
        return y

    def _L2_gnn_ref(x, W, a_src, a_dst, edge_W, edge_b, bias, edge_attr, edge_index):
        import jax, jax.numpy as jnp
        import numpy as np
        N = 50000
        E = 12500
        IN = 256
        H = 8
        D = 32
        EF = 3
        n = x.shape[0]
        h = (x @ W.T).reshape(n, H, D)
        src, dst = (edge_index[0], edge_index[1])
        h_src = h[src]
        h_dst = h[dst]
        alpha = jnp.einsum('ehd,hd->eh', h_src, a_src) + jnp.einsum('ehd,hd->eh', h_dst, a_dst)
        enc = jax.nn.relu(edge_attr @ edge_W.T + edge_b).reshape(-1, H, D)
        alpha = alpha + jnp.sum(enc * h_dst, axis=-1)
        alpha = jnp.where(alpha >= 0, alpha, 0.2 * alpha)
        amax = jax.ops.segment_max(alpha, dst, num_segments=n)
        ex = jnp.exp(alpha - amax[dst])
        denom = jax.ops.segment_sum(ex, dst, num_segments=n)
        attn = ex / jnp.maximum(denom[dst], 1e-10)
        out = jax.ops.segment_sum(h_src * attn[..., None], dst, num_segments=n)
        return out.reshape(n, H * D) + bias

    def _L2_ffn_ref(x, sW1, sb1, sW2, sb2, sW3, sb3, eW1, eb1, eW2, eb2, eW3, eb3, gW, gb):
        import jax, jax.numpy as jnp
        import numpy as np
        B, A = (128, 8)
        IN, OUT = (256, 256)
        SH1, SH2 = (256, 128)
        EH1, EH2 = (128, 64)
        E, TOPK = (4, 2)

        def _shared_mlp(x, W1, b1, W2, b2, W3, b3):
            h = jax.nn.relu(x @ W1 + b1)
            h = jax.nn.relu(h @ W2 + b2)
            return h @ W3 + b3

        def _experts_mlp(x, eW1, eb1, eW2, eb2, eW3, eb3):
            h = jax.nn.relu(jnp.einsum('baf,efh->ebah', x, eW1) + eb1[:, None, None, :])
            h = jax.nn.relu(jnp.einsum('ebah,ehg->ebag', h, eW2) + eb2[:, None, None, :])
            o = jnp.einsum('ebag,ego->ebao', h, eW3) + eb3[:, None, None, :]
            return jnp.moveaxis(o, 0, -1)
        all_out = _experts_mlp(x, eW1, eb1, eW2, eb2, eW3, eb3)
        shared = _shared_mlp(x, sW1, sb1, sW2, sb2, sW3, sb3)
        gates = jax.nn.softmax(x @ gW + gb, axis=-1)
        topv, topi = jax.lax.top_k(gates, TOPK)
        topw = jax.nn.softmax(topv, axis=-1)
        sel = jnp.take_along_axis(all_out, topi[:, :, None, :], axis=-1)
        gated = jnp.sum(sel * topw[:, :, None, :], axis=-1)
        return shared + gated

    def _L3_gnn_ref(x, edge_index, edge_attr, eps, ee_w1, ee_b1, ee_w2, ee_b2, w1, b1, g1, be1, w2, b2, g2, be2, w3, b3, bn_g, bn_b):
        import jax, jax.numpy as jnp
        import numpy as np
        N = 3125
        E = 10000
        CIN = 256
        EDIM = 64
        EEMB = 256
        H = 1024
        LN_EPS = 1e-05

        def _ln(x, g, b):
            m = jnp.mean(x, axis=-1, keepdims=True)
            v = jnp.var(x, axis=-1, keepdims=True)
            return (x - m) * jax.lax.rsqrt(v + LN_EPS) * g + b
        n = x.shape[0]
        sl = jnp.arange(n, dtype=edge_index.dtype)
        ei = jnp.concatenate([edge_index, jnp.stack([sl, sl], axis=0)], axis=1)
        ea = jnp.concatenate([edge_attr, jnp.zeros((n, edge_attr.shape[1]), edge_attr.dtype)], axis=0)
        src, dst = (ei[0], ei[1])
        e = jax.nn.relu(ea @ ee_w1 + ee_b1) @ ee_w2 + ee_b2
        msg = x[src] + e
        agg = jax.ops.segment_sum(msg, dst, num_segments=n)
        h = (1.0 + eps) * x + agg
        h = jax.nn.relu(_ln(h @ w1 + b1, g1, be1))
        h = jax.nn.relu(_ln(h @ w2 + b2, g2, be2))
        y = h @ w3 + b3
        out = x + y
        out = _ln(out, bn_g, bn_b)
        return jax.nn.relu(out)

    def _L3_ffn_ref(x, W_fx, b_fx, W_x, b_x, W_slice, b_slice, W_q, W_k, W_v, W_out, b_out, temperature):
        import jax, jax.numpy as jnp
        import numpy as np
        DIM = 256
        H = 8
        D = 64
        G = 64
        INNER = H * D
        SCALE = D ** (-0.5)
        B, N, _ = x.shape
        fx_mid = (x @ W_fx + b_fx).reshape(B, N, H, D).transpose(0, 2, 1, 3)
        x_mid = (x @ W_x + b_x).reshape(B, N, H, D).transpose(0, 2, 1, 3)
        temp = jnp.clip(temperature, 0.1, 5.0)
        slice_weights = jax.nn.softmax((x_mid @ W_slice + b_slice) / temp, axis=-1)
        slice_norm = slice_weights.sum(axis=2)
        slice_token = jnp.einsum('bhnc,bhng->bhgc', fx_mid, slice_weights)
        slice_token = slice_token / (slice_norm[..., None] + 1e-05)
        q = slice_token @ W_q
        k = slice_token @ W_k
        v = slice_token @ W_v
        attn = jax.nn.softmax(jnp.einsum('bhgc,bhkc->bhgk', q, k) * SCALE, axis=-1)
        out_slice = jnp.einsum('bhgk,bhkc->bhgc', attn, v)
        out_x = jnp.einsum('bhgc,bhng->bhnc', out_slice, slice_weights)
        out_x = out_x.transpose(0, 2, 1, 3).reshape(B, N, INNER)
        return out_x @ W_out + b_out
    edge_index = jnp.stack([src, dst])
    x = x + _L0_gnn_ref(_layernorm(x, axis=-1), edge_weight, L0_gnn_W_lin, L0_gnn_att_l, L0_gnn_att_r, L0_gnn_W_res, edge_index)
    x = x + _L0_ffn_ref(_layernorm(x, axis=-1)[None], L0_ffn_W_gat, L0_ffn_att_src, L0_ffn_att_dst, L0_ffn_b_gat, L0_ffn_ln_gamma, L0_ffn_ln_beta, L0_ffn_W1, L0_ffn_b1, L0_ffn_W2, L0_ffn_b2, L0_ffn_edge_index)[0]
    x = x + _L1_gnn_ref(_layernorm(x, axis=-1), src, dst, edge_type_16, edge_weight1, L1_gnn_w1, L1_gnn_loop_w1, L1_gnn_b1, L1_gnn_w2, L1_gnn_loop_w2, L1_gnn_b2)
    x = x + _L1_ffn_ref(_layernorm(x, axis=-1)[None], L1_ffn_gamma, L1_ffn_beta, L1_ffn_Wr, L1_ffn_br, L1_ffn_W1, L1_ffn_b1, L1_ffn_W2, L1_ffn_b2)[0]
    x = x + _L2_gnn_ref(_layernorm(x, axis=-1), L2_gnn_W, L2_gnn_a_src, L2_gnn_a_dst, L2_gnn_edge_W, L2_gnn_edge_b, L2_gnn_bias, edge_attr_3, edge_index)
    x = x + _L2_ffn_ref(_layernorm(x, axis=-1)[None], L2_ffn_sW1, L2_ffn_sb1, L2_ffn_sW2, L2_ffn_sb2, L2_ffn_sW3, L2_ffn_sb3, L2_ffn_eW1, L2_ffn_eb1, L2_ffn_eW2, L2_ffn_eb2, L2_ffn_eW3, L2_ffn_eb3, L2_ffn_gW, L2_ffn_gb)[0]
    x = x + _L3_gnn_ref(_layernorm(x, axis=-1), edge_index, edge_attr_64, L3_gnn_eps, L3_gnn_ee_w1, L3_gnn_ee_b1, L3_gnn_ee_w2, L3_gnn_ee_b2, L3_gnn_w1, L3_gnn_b1, L3_gnn_g1, L3_gnn_be1, L3_gnn_w2, L3_gnn_b2, L3_gnn_g2, L3_gnn_be2, L3_gnn_w3, L3_gnn_b3, L3_gnn_bn_g, L3_gnn_bn_b)
    x = x + _L3_ffn_ref(_layernorm(x, axis=-1)[None], L3_ffn_W_fx, L3_ffn_b_fx, L3_ffn_W_x, L3_ffn_b_x, L3_ffn_W_slice, L3_ffn_b_slice, L3_ffn_W_q, L3_ffn_W_k, L3_ffn_W_v, L3_ffn_W_out, L3_ffn_b_out, L3_ffn_temperature)[0]
    return x

_drawn_inputs = setup_inputs


def setup_inputs(seed=0):
    import zlib

    import numpy as np

    out = dict(_drawn_inputs(seed))
    spreads = {'L0_ffn_b_gat': (0.0, 0.1),
     'L0_ffn_ln_gamma': (1.0, 0.2),
     'L0_ffn_ln_beta': (0.0, 0.1),
     'L0_ffn_b1': (0.0, 0.1),
     'L0_ffn_b2': (0.0, 0.1),
     'L1_gnn_b1': (0.0, 0.1),
     'L1_gnn_b2': (0.0, 0.1),
     'L1_ffn_br': (0.0, 0.339),
     'L2_gnn_edge_b': (0.0, 0.1),
     'L2_gnn_bias': (0.0, 0.1),
     'L2_ffn_sb1': (0.0, 0.639),
     'L2_ffn_sb2': (0.0, 0.293),
     'L2_ffn_sb3': (0.0, 0.1),
     'L2_ffn_eb1': (0.0, 0.8),
     'L2_ffn_eb2': (0.0, 0.785),
     'L2_ffn_eb3': (0.0, 0.1),
     'L2_ffn_gb': (0.0, 0.525),
     'L3_gnn_ee_b1': (0.0, 0.508),
     'L3_gnn_ee_b2': (0.0, 0.283),
     'L3_gnn_b1': (0.0, 0.8),
     'L3_gnn_g1': (1.0, 0.2),
     'L3_gnn_be1': (0.0, 0.429),
     'L3_gnn_b2': (0.0, 0.298),
     'L3_gnn_g2': (1.0, 0.2),
     'L3_gnn_be2': (0.0, 0.456),
     'L3_gnn_b3': (0.0, 0.291),
     'L3_gnn_bn_g': (1.0, 0.2),
     'L3_gnn_bn_b': (0.0, 0.1),
     'L3_ffn_b_fx': (0.0, 0.1),
     'L3_ffn_b_x': (0.0, 0.8),
     'L3_ffn_b_slice': (0.0, 0.8),
     'L3_ffn_b_out': (0.0, 0.1),
     'L3_ffn_temperature': (0.5, 0.6)}
    factors = {'L1_ffn_gamma': 8.0,
     'L1_ffn_beta': 7.417,
     'L1_ffn_b1': 8.0,
     'L1_ffn_b2': 6.135,
     'L3_ffn_W_x': 8.0,
     'L3_ffn_W_slice': 8.0,
     'L3_ffn_W_q': 8.0,
     'L3_ffn_W_k': 8.0}
    for name, (base, spread) in spreads.items():
        noise = np.random.default_rng([zlib.crc32(name.encode()), seed]).standard_normal(out[name].shape)
        drawn = base * np.exp(spread * noise) if base else spread * noise
        out[name] = jnp.asarray(drawn.astype(out[name].dtype))
    for name, factor in factors.items():
        out[name] = (out[name] * factor).astype(out[name].dtype)
    return out
```

```python
from contextlib import ExitStack

import concourse.bass as bass
from concourse import mybir

ALU = mybir.AluOpType
ACT = mybir.ActivationFunctionType
AX = mybir.AxisListType
F32 = mybir.dt.float32
BF16 = mybir.dt.bfloat16
I32 = mybir.dt.int32

P = 128
N = 3125
NT = (N + P - 1) // P
NP = NT * P
D = 256
PAD = NP - 1
BIG = 1.0e30
EPS = 1.0e-5

E = 50000
EF = 64
EJ = 392
FE = 32768
FEJ = 288
REC = 9 + EF
R_SRC, R_DST, R_TYPE, R_EW, R_EW1, R_EA3, R_ONE, R_EA = 0, 1, 2, 3, 4, 5, 8, 9
NCH = 416
FNC = 320
LOW = 64
HIGH = NP // LOW


class Steps:

    def __init__(self, sem, names):
        self.sem, self.names, self.n = sem, names.split(), 0
        self.base = len(self.names)

    def step(self, name):
        assert self.names[self.n % len(self.names)] == name, (name, self.names[self.n % len(self.names)])
        self.n += 1
        return self.sem, 1

    def at(self, name, i=0):
        return self.sem, i * len(self.names) + (self.base + self.names.index(name) + 1)

    def ended(self, i):
        return self.sem, i * len(self.names) + self.base


class Kit:

    free = [None]
    rows = [None, 0]

    def __init__(self, nc, ctx, tag):
        self.nc, self.ctx, self.tag, self.counted = nc, ctx, tag, []
        if not tag:
            Kit.free[0] = min(nc.free_semaphores)
        self.first = Kit.free[0]
        ctx.callback(self.close)

    def close(self):
        if Kit.free[0] > self.first:
            self.nc.all_engine_barrier(sems_to_clear=range(self.first, Kit.free[0]))
        Kit.free[0] = self.first

    def sb(self, name, shape, dt=F32):
        return self.ctx.enter_context(self.nc.sbuf_tensor(self.tag + name, shape, dt))

    def ps(self, name, shape, dt=F32):
        words = 512 if dt == F32 else 1024
        size = 1
        for n in shape[1:]:
            size *= n
        t = self.ctx.enter_context(self.nc.psum_tensor(self.tag + name, [P, -(-size // words) * words], dt))
        a = t[0:shape[0], 0:size]
        if len(shape) == 2:
            return a
        names = "abcd"[:len(shape) - 1]
        return a.rearrange(f"p ({' '.join(names)}) -> p {' '.join(names)}", **dict(zip(names, shape[1:])))

    def sem(self, name):
        Kit.free[0] += 1
        return self.ctx.enter_context(self.nc.semaphore(self.tag + name, num=Kit.free[0] - 1))

    def row_sems(self, rounds=0):
        if not self.tag:
            Kit.rows[:] = [[self.sem(f"rows_moved{u}_") for u in range(8)], 0]
        before = Kit.rows[1]
        Kit.rows[1] += 16 * rounds
        return Kit.rows[0], before

    def steps(self, name, names):
        self.counted.append(Steps(self.sem(name), names))
        return self.counted[-1]

    def open(self, eng):
        for steps in self.counted:
            eng.sem_inc(steps.sem, steps.base)


def constants(nc, K, G):
    G.iota = K.sb("iota", [P, P])
    G.part = K.sb("part", [P, 1])
    G.ident = K.sb("ident", [P, P])
    G.identb = K.sb("identb", [P, P], BF16)
    G.ones = K.sb("ones", [P, P])
    G.earlier = K.sb("earlier", [P, P])
    filled = K.sem("filled")
    made = K.sem("made")
    block = nc.Block()
    with block:
        @block.gpsimd
        def _(pool):
            pool.iota(G.iota[:], [[1, P]], base=0, channel_multiplier=0,
                      allow_small_or_imprecise_dtypes=True).then_inc(filled, 1)
            pool.iota(G.part[:], [[0, 1]], base=0, channel_multiplier=1,
                      allow_small_or_imprecise_dtypes=True).then_inc(filled, 1)

        @block.vector
        def _(dve):
            dve.memset(G.ones[:], 1.0).then_inc(made, 1)
            dve.wait_ge(filled, 2)
            dve.tensor_scalar(G.ident[:], G.iota[:], G.part[:, 0:1], None, ALU.is_equal).then_inc(made, 1)
            dve.tensor_scalar(G.identb[:], G.iota[:], G.part[:, 0:1], None, ALU.is_equal).then_inc(made, 1)
            dve.tensor_scalar(G.earlier[:], G.iota[:], G.part[:, 0:1], None, ALU.is_gt).then_inc(made, 1)


def rank_pass(nc, K, G, tag, cols, digit, buckets, tiled, pos_i, tile_of=None, tile_i=None, chunks=0):
    with ExitStack() as ctx:
        L = Kit(nc, ctx, tag)
        eq = L.sb("eq", [P, cols])
        run = L.sb("run", [P, cols])
        hit = L.sb("hit", [P, cols])
        pos = L.sb("pos", [P, cols])
        tot = L.sb("tot", [P, LOW])
        total = L.sb("total", [P, LOW])
        ends = L.sb("ends", [P, LOW])
        base = L.sb("base", [P, LOW])
        zero = L.sb("zero", [P, cols])
        cnt_i = L.sb("cnt_i", [P, NT], I32)
        row_i = L.sb("row_i", [P, cols], I32)
        col_i = L.sb("col_i", [P, cols], I32)
        after = L.sb("after", [P, chunks, NT - 1]) if tiled else None
        sums = L.ps("sums", [P, 2, LOW])
        B = buckets
        V = L.steps("dve_rank", "eq run total hit pos")
        W = L.steps("dve_base", "hit pos")
        chain = L.sem("dve_chain")
        counted = L.sem("counted")
        summed = L.sem("summed")
        with nc.Block() as block:
            @block.sync
            def _(sp):
                L.open(sp)

            @block.vector
            def _(dve):
                dve.memset(pos[:], 0.0).then_inc(chain, 1)
                dve.memset(zero[:], 0.0).then_inc(chain, 1)
                dve.wait_ge(chain, 2)
                with dve.Fori(0, B) as b:
                    dve.wait_ge(*V.ended(b))
                    dve.tensor_scalar(eq[:], digit[:], G.iota[:, bass.ds(b, 1)], None,
                                      ALU.is_equal).then_inc(*V.step("eq"))
                    dve.wait_ge(*V.at("eq", b))
                    dve.tensor_tensor_scan(run[:], zero[:], eq[:], 0.0, ALU.add, ALU.add).then_inc(*V.step("run"))
                    dve.wait_ge(*V.at("run", b))
                    dve.tensor_copy(tot[:, bass.ds(b, 1)], run[:, cols - 1:cols]).then_inc(*V.step("total"))
                    dve.tensor_tensor(hit[:], eq[:], run[:], ALU.mult).then_inc(*V.step("hit"))
                    dve.wait_ge(*V.at("hit", b))
                    dve.tensor_tensor(pos[:], pos[:], hit[:], ALU.add).then_inc(*V.step("pos"))
                dve.wait_ge(*V.ended(B))
                dve.sem_inc(counted, 1)
                dve.wait_ge(summed, 1)
                dve.tensor_copy(total[:, 0:B], sums[:, 1, 0:B]).then_inc(chain, 1)
                dve.wait_ge(chain, 3)
                n = 3
                if not tiled:
                    dve.tensor_tensor_scan(ends[:, 0:B], zero[:, 0:B], total[:, 0:B], 0.0, ALU.add,
                                           ALU.add).then_inc(chain, 1)
                    dve.wait_ge(chain, 4)
                    dve.tensor_tensor(base[:, 0:B], ends[:, 0:B], total[:, 0:B], ALU.subtract).then_inc(chain, 1)
                    n = 5
                else:
                    pair = total[:, 0:B].rearrange("p (t h) -> p t h", h=2)
                    bpair = base[:, 0:B].rearrange("p (t h) -> p t h", h=2)
                    dve.tensor_tensor(hit[:, 0:NT], pair[:, :, 0], pair[:, :, 1], ALU.add).then_inc(chain, 1)
                    dve.wait_ge(chain, 4)
                    dve.tensor_scalar(cnt_i[:], hit[:, 0:NT], float(P - 1), None, ALU.add).then_inc(chain, 1)
                    dve.wait_ge(chain, 5)
                    dve.tensor_scalar(cnt_i[:], cnt_i[:], 7, None, ALU.arith_shift_right).then_inc(chain, 1)
                    dve.wait_ge(chain, 6)
                    dve.tensor_copy(hit[:, 0:NT], cnt_i[:]).then_inc(chain, 1)
                    dve.wait_ge(chain, 7)
                    dve.tensor_tensor_scan(ends[:, 0:NT], zero[:, 0:NT], hit[:, 0:NT], 0.0, ALU.add,
                                           ALU.add).then_inc(chain, 1)
                    dve.wait_ge(chain, 8)
                    dve.tensor_tensor(hit[:, NT:2 * NT], ends[:, 0:NT], hit[:, 0:NT], ALU.subtract).then_inc(chain, 1)
                    dve.wait_ge(chain, 9)
                    dve.tensor_scalar(bpair[:, :, 0], hit[:, NT:2 * NT], float(P), None, ALU.mult).then_inc(chain, 1)
                    dve.wait_ge(chain, 10)
                    dve.tensor_tensor(bpair[:, :, 1], bpair[:, :, 0], pair[:, :, 0], ALU.add).then_inc(chain, 1)
                    dve.tensor_tensor(after[:, :, 0:NT - 1],
                                      G.chunk[:, 0:chunks].unsqueeze(2).broadcast_to([P, chunks, NT - 1]),
                                      ends[:, 0:NT - 1].unsqueeze(1).broadcast_to([P, chunks, NT - 1]),
                                      ALU.is_ge).then_inc(chain, 1)
                    dve.wait_ge(chain, 12)
                    dve.tensor_reduce(tile_of[:], after[:, :, 0:NT - 1], AX.X, ALU.add).then_inc(chain, 1)
                    dve.wait_ge(chain, 13)
                    dve.tensor_copy(tile_i[:], tile_of[:]).then_inc(chain, 1)
                    n = 14
                dve.wait_ge(chain, n)
                dve.scalar_tensor_tensor(base[:, 0:B], base[:, 0:B], -1.0, sums[:, 0, 0:B], ALU.add,
                                         ALU.add).then_inc(chain, 1)
                dve.wait_ge(chain, n + 1)
                with dve.Fori(0, B) as b:
                    dve.wait_ge(*W.ended(b))
                    dve.tensor_scalar(hit[:], digit[:], G.iota[:, bass.ds(b, 1)], base[:, bass.ds(b, 1)],
                                      ALU.is_equal, ALU.mult).then_inc(*W.step("hit"))
                    dve.wait_ge(*W.at("hit", b))
                    dve.tensor_tensor(pos[:], pos[:], hit[:], ALU.add).then_inc(*W.step("pos"))
                dve.wait_ge(*W.ended(B))
                n += 2
                dve.tensor_copy(pos_i[:] if not tiled else row_i[:], pos[:]).then_inc(chain, 1)
                dve.wait_ge(chain, n)
                if tiled:
                    dve.tensor_scalar(col_i[:], row_i[:], 7, None, ALU.arith_shift_right).then_inc(chain, 1)
                    dve.tensor_scalar(row_i[:], row_i[:], P - 1, None, ALU.bitwise_and).then_inc(chain, 1)
                    dve.wait_ge(chain, n + 2)
                    dve.tensor_copy(eq[:], col_i[:]).then_inc(chain, 1)
                    dve.tensor_copy(run[:], row_i[:]).then_inc(chain, 1)
                    dve.wait_ge(chain, n + 4)
                    dve.scalar_tensor_tensor(pos[:], run[:], float(chunks), eq[:], ALU.mult,
                                             ALU.add).then_inc(chain, 1)
                    dve.wait_ge(chain, n + 5)
                    dve.tensor_copy(pos_i[:], pos[:]).then_inc(chain, 1)

            @block.tensor
            def _(pe):
                pe.wait_ge(counted, 1)
                pe.matmul(sums[:, 0, 0:B], G.earlier[:], tot[:, 0:B], start=True, stop=True)
                pe.matmul(sums[:, 1, 0:B], G.ones[:], tot[:, 0:B], start=True, stop=True).then_inc(summed, 1)


def scatter_records(nc, K, tag, cols, words, rec, pos_i, dram):
    U = 4
    with ExitStack() as ctx:
        L = Kit(nc, ctx, tag)
        row = L.sb("row", [P, 2 * U, words])
        at = L.sb("at", [P, 2, U], I32)
        A = L.steps("act_staged", "row0 at0 row1 at1")
        sent, before = L.row_sems(cols // (2 * U))
        go = L.sem("go")
        with nc.Block() as block:
            @block.sync
            def _(sp):
                L.open(sp)

            @block.scalar
            def _(act):
                with act.Fori(0, cols // (2 * U)) as i:
                    for h in range(2):
                        for u in range(U):
                            act.wait_ge(sent[h * U + u], i * 16 + before)
                        act.copy(row[:, h * U:(h + 1) * U, :],
                                 rec[:, bass.ds(i * (2 * U) + h * U, U), :]).then_inc(*A.step(f"row{h}"))
                        act.copy(at[:, h, :], pos_i[:, bass.ds(i * (2 * U) + h * U, U)]).then_inc(*A.step(f"at{h}"))

            @block.gpsimd
            def _(pool):
                with pool.Fori(0, cols // (2 * U)) as i:
                    for h in range(2):
                        pool.wait_ge(*A.at(f"at{h}", i))
                        pool.sem_inc(go, 1)
                        for u in range(U):
                            pool.indirect_dma_start(
                                out=dram, out_offset=bass.IndirectOffsetOnAxis(ap=at[:, h, u:u + 1], axis=0),
                                in_=row[:, h * U + u, :], in_offset=None).then_inc(sent[h * U + u], 16)
                for u in range(2 * U):
                    pool.wait_ge(sent[u], 16 * (cols // (2 * U)) + before)


def digits(nc, tag, keys, cols, low, digit):
    with ExitStack() as ctx:
        L = Kit(nc, ctx, tag)
        key_i = L.sb("key_i", [P, cols], I32)
        chain = L.sem("chain")
        with nc.Block() as block:
            @block.vector
            def _(dve):
                dve.tensor_copy(key_i[:], keys).then_inc(chain, 1)
                dve.wait_ge(chain, 1)
                if low:
                    dve.tensor_scalar(key_i[:], key_i[:], LOW - 1, None, ALU.bitwise_and).then_inc(chain, 1)
                else:
                    dve.tensor_scalar(key_i[:], key_i[:], 6, None, ALU.arith_shift_right).then_inc(chain, 1)
                dve.wait_ge(chain, 2)
                dve.tensor_copy(digit[:], key_i[:]).then_inc(chain, 1)


def sort_edges(nc, K, G, tag, cols, words, fill, first_dram, last_dram, chunks, out):
    with ExitStack() as ctx:
        L = Kit(nc, ctx, tag)
        rec = L.sb("rec", [P, cols, words])
        digit = L.sb("digit", [P, cols])
        pos_i = L.sb("pos_i", [P, cols], I32)
        fill(rec)
        digits(nc, tag + "lo", rec[:, :, R_DST], cols, True, digit)
        rank_pass(nc, L, G, tag + "ra", cols, digit, LOW, False, pos_i)
        scatter_records(nc, L, tag + "sa", cols, words, rec, pos_i, first_dram)
        loaded = L.sem("loaded")
        step = 32
        padrow = L.sb("padrow", [P, step, words])
        padded = L.sem("padded")
        stored = L.sem("stored")
        with nc.Block() as block:
            @block.vector
            def _(dve):
                dve.memset(padrow[:], 0.0).then_inc(padded, 1)
                dve.wait_ge(padded, 1)
                dve.memset(padrow[:, :, R_DST:R_DST + 1], float(PAD)).then_inc(padded, 1)

            @block.sync
            def _(sp):
                sp.dma_start(rec[:], first_dram.rearrange("(p j) w -> p j w", j=cols)).then_inc(loaded, 16)
                sp.wait_ge(padded, 2)
                last = last_dram.rearrange("(p c) w -> p c w", c=chunks)
                for c in range(0, chunks, step):
                    sp.dma_start(last[:, c:c + step, :], padrow[:]).then_inc(stored, 16)
                sp.wait_ge(stored, 16 * (chunks // step))
                sp.wait_ge(loaded, 16)
        digits(nc, tag + "hi", rec[:, :, R_DST], cols, False, digit)
        rank_pass(nc, L, G, tag + "rb", cols, digit, HIGH, True, pos_i, out[0], out[1], chunks)
        scatter_records(nc, L, tag + "sb", cols, words, rec, pos_i, last_dram)


def fill_graph(nc, G, I):
    full = E // EJ
    rest = E - full * EJ

    def fill(rec):
        with ExitStack() as ctx:
            L = Kit(nc, ctx, "fg")
            ints = L.sb("ints", [P, 3, EJ], I32)
            scal = L.sb("scal", [P, 2, EJ])
            attr = L.sb("attr", [P, EJ, 3])
            cleared = L.sem("cleared")
            loaded = L.sem("loaded")
            ready = L.sem("ready")
            with nc.Block() as block:
                @block.vector
                def _(dve):
                    dve.memset(ints[:], 0).then_inc(cleared, 1)
                    dve.memset(rec[:], 0.0).then_inc(cleared, 1)
                    dve.memset(scal[:], 0.0).then_inc(cleared, 1)
                    dve.memset(attr[:], 0.0).then_inc(cleared, 1)
                    dve.wait_ge(cleared, 4)
                    dve.memset(ints[:, 1, :], PAD).then_inc(cleared, 1)
                    dve.memset(rec[:, :, R_ONE:R_ONE + 1], 1.0).then_inc(cleared, 1)
                    dve.wait_ge(loaded, 16 * 14)
                    for f, row in ((0, R_SRC), (1, R_DST), (2, R_TYPE)):
                        dve.tensor_copy(rec[:, :, row], ints[:, f, :]).then_inc(ready, 1)
                    dve.tensor_copy(rec[:, :, R_EW], scal[:, 0, :]).then_inc(ready, 1)
                    dve.tensor_copy(rec[:, :, R_EW1], scal[:, 1, :]).then_inc(ready, 1)
                    dve.tensor_copy(rec[:, :, R_EA3:R_EA3 + 3], attr[:]).then_inc(ready, 1)

                @block.sync
                def _(sp):
                    sp.wait_ge(cleared, 6)
                    for f, name in ((0, "src"), (1, "dst"), (2, "edge_type_16")):
                        a = I[name]
                        sp.dma_start(ints[0:full, f, :], a[0:full * EJ].rearrange("(p j) -> p j", j=EJ)).then_inc(loaded, 16)
                        sp.dma_start(ints[full:full + 1, f, 0:rest],
                                     a[full * EJ:E].rearrange("(p j) -> p j", j=rest)).then_inc(loaded, 16)
                    for f, a in ((0, I["edge_weight"]), (1, I["edge_weight1"].rearrange("e w -> (e w)"))):
                        sp.dma_start(scal[0:full, f, :], a[0:full * EJ].rearrange("(p j) -> p j", j=EJ)).then_inc(loaded, 16)
                        sp.dma_start(scal[full:full + 1, f, 0:rest],
                                     a[full * EJ:E].rearrange("(p j) -> p j", j=rest)).then_inc(loaded, 16)
                    for a, to in ((I["edge_attr_3"], attr[:]), (I["edge_attr_64"], rec[:, :, R_EA:REC])):
                        sp.dma_start(to[0:full],
                                     a[0:full * EJ, :].rearrange("(p j) w -> p j w", j=EJ)).then_inc(loaded, 16)
                        sp.dma_start(to[full:full + 1, 0:rest],
                                     a[full * EJ:E, :].rearrange("(p j) w -> p j w", j=rest)).then_inc(loaded, 16)
    return fill


def fill_router(nc, G, I):
    cols = FE // P

    def fill(rec):
        with ExitStack() as ctx:
            L = Kit(nc, ctx, "fr")
            ints = L.sb("ints", [P, 2, cols], I32)
            cleared = L.sem("cleared")
            loaded = L.sem("loaded")
            ready = L.sem("ready")
            with nc.Block() as block:
                @block.vector
                def _(dve):
                    dve.memset(rec[:, cols + NT:, :], float(PAD)).then_inc(ready, 1)
                    for f in range(2):
                        for t in range(NT):
                            dve.tensor_scalar(rec[:, cols + t, f:f + 1], G.part[:, 0:1], float(t * P), None,
                                              ALU.add).then_inc(ready, 1)
                    dve.wait_ge(loaded, 32)
                    for f in range(2):
                        dve.tensor_copy(rec[:, 0:cols, f], ints[:, f, :]).then_inc(ready, 1)

                @block.sync
                def _(sp):
                    for f in range(2):
                        sp.dma_start(ints[:, f, :], I["L0_ffn_edge_index"][f, :].rearrange(
                            "(p j) -> p j", j=cols)).then_inc(loaded, 16)
    return fill


class Globals:
    pass


class Edges:

    def __init__(self, K, tag, chunks):
        self.chunks = chunks
        self.tile_of = K.sb(tag + "tile_of", [P, chunks])
        self.tile = K.sb(tag + "tile", [P, chunks], I32)
        self.src = K.sb(tag + "src", [P, chunks], I32)
        self.dst = K.sb(tag + "dst", [P, chunks])
        self.local = K.sb(tag + "local", [P, chunks])


def load_edges(nc, tag, X, rows, words, small=None):
    with ExitStack() as ctx:
        L = Kit(nc, ctx, tag)
        ch = X.chunks
        w = 8 if small is not None else words
        part = L.sb("part", [P, ch, w]) if small is None else small
        loaded = L.sem("loaded")
        chain = L.sem("chain")
        with nc.Block() as block:
            @block.sync
            def _(sp):
                with nc.allow_non_contiguous_dma(reason="fields of records"):
                    sp.dma_start(part[:, :, 0:w] if small is None else part[:],
                                 rows.rearrange("(p c) w -> p c w", c=ch)[:, :, 0:(w if small is None else 9)]
                                 ).then_inc(loaded, 16)

            @block.vector
            def _(dve):
                dve.wait_ge(loaded, 16)
                dve.tensor_copy(X.src[:], part[:, :, R_SRC]).then_inc(chain, 1)
                dve.tensor_copy(X.dst[:], part[:, :, R_DST]).then_inc(chain, 1)
                dve.wait_ge(chain, 2)
                dve.scalar_tensor_tensor(X.local[:], X.tile_of[:], -float(P), X.dst[:], ALU.mult,
                                         ALU.add).then_inc(chain, 1)


GT = 5
NG = NT // GT
U = 4
IT = 2 * U


class Norm:

    def __init__(self, L, G, affine=None, relu_of=None):
        self.G, self.affine, self.relu_of = G, affine, relu_of
        self.stats = L.sb("n_stats", [P, GT, 6])
        self.mv = L.sb("n_mv", [P, GT, 2])
        self.rstd = L.sb("n_rstd", [P, GT])
        self.std = L.sb("n_std", [P, GT])
        self.xn = L.sb("n_xn", [P, GT, D])
        self.raw = L.sb("n_raw", [P, GT, D]) if affine else None
        self.xT = L.sb("n_xT", [P, 2, GT * P])
        self.tr = [L.ps(f"n_tr{s}", [P, 2, P]) for s in range(2)]
        self.took = L.sem("n_took")
        self.V = L.steps("dve_norm", "norm" if relu_of is not None else "stats aggr eps rstd norm" + (" stats2 aggr2 eps2 rstd2 norm2 gamma beta" if affine else ""))
        self.Q = L.steps("act_std", "std" + (" std2" if affine else ""))
        self.T = L.steps("pe_turned", "tr0 tr1 tr2 tr3 tr4")
        self.C = L.steps("act_turned", "cp0 cp1 cp2 cp3 cp4")
        self.last = "beta" if affine else "norm"

    def dve(self, dve, i, xn_free=()):
        V, Q, G = self.V, self.Q, self.G
        dve.wait_ge(*V.ended(i))
        if self.relu_of is not None:
            dve.wait_ge(*self.T.ended(i))
            for w in xn_free:
                dve.wait_ge(*w)
            dve.tensor_scalar(self.xn[:], self.relu_of[:, bass.ds(i * GT, GT), :], 0.0, None,
                              ALU.max).then_inc(*V.step("norm"))
            return
        for u in range(GT):
            ins = dve.bn_stats(self.stats[:, u, :], G.x[:, bass.ds(i * GT + u, 1), :].rearrange("p a d -> p (a d)"))
        ins.then_inc(*V.step("stats"))
        dve.wait_ge(*V.at("stats", i))
        dve.sem_inc(self.took, 1)
        for u in range(GT):
            ins = dve.bn_aggr(self.mv[:, u, :], self.stats[:, u, :])
        ins.then_inc(*V.step("aggr"))
        dve.wait_ge(*V.at("aggr", i))
        dve.tensor_scalar(self.rstd[:], self.mv[:, :, 1], EPS, None, ALU.add).then_inc(*V.step("eps"))
        dve.wait_ge(*Q.at("std", i))
        dve.reciprocal(self.rstd[:], self.std[:]).then_inc(*V.step("rstd"))
        dve.wait_ge(*V.at("rstd", i))
        dve.wait_ge(*self.T.ended(i))
        for w in xn_free:
            dve.wait_ge(*w)
        to = self.raw if self.affine else self.xn
        for u in range(GT):
            ins = dve.tensor_scalar(to[:, u, :], G.x[:, bass.ds(i * GT + u, 1), :].rearrange("p a d -> p (a d)"),
                                    self.mv[:, u, 0:1], self.rstd[:, u:u + 1], ALU.subtract, ALU.mult)
        ins.then_inc(*V.step("norm"))
        if self.affine:
            gamma, beta = self.affine
            dve.wait_ge(*V.at("norm", i))
            for u in range(GT):
                ins = dve.bn_stats(self.stats[:, u, :], self.raw[:, u, :])
            ins.then_inc(*V.step("stats2"))
            dve.wait_ge(*V.at("stats2", i))
            dve.sem_inc(self.took, 1)
            for u in range(GT):
                ins = dve.bn_aggr(self.mv[:, u, :], self.stats[:, u, :])
            ins.then_inc(*V.step("aggr2"))
            dve.wait_ge(*V.at("aggr2", i))
            dve.tensor_scalar(self.rstd[:], self.mv[:, :, 1], EPS, None, ALU.add).then_inc(*V.step("eps2"))
            dve.wait_ge(*Q.at("std2", i))
            dve.reciprocal(self.rstd[:], self.std[:]).then_inc(*V.step("rstd2"))
            dve.wait_ge(*V.at("rstd2", i))
            for u in range(GT):
                ins = dve.tensor_scalar(self.raw[:, u, :], self.raw[:, u, :], self.mv[:, u, 0:1],
                                        self.rstd[:, u:u + 1], ALU.subtract, ALU.mult)
            ins.then_inc(*V.step("norm2"))
            dve.wait_ge(*V.at("norm2", i))
            dve.tensor_tensor(self.raw[:], self.raw[:], gamma[:].unsqueeze(1).broadcast_to([P, GT, D]),
                              ALU.mult).then_inc(*V.step("gamma"))
            dve.wait_ge(*V.at("gamma", i))
            dve.tensor_tensor(self.xn[:], self.raw[:], beta[:].unsqueeze(1).broadcast_to([P, GT, D]),
                              ALU.add).then_inc(*V.step("beta"))

    def pe(self, pe, i):
        pe.wait_ge(*self.V.at(self.last, i))
        pe.wait_ge(*self.C.ended(i))
        for u in range(GT):
            if u >= 2:
                pe.wait_ge(*self.C.at(f"cp{u - 2}", i))
            for k in range(2):
                ins = pe.transpose(self.tr[u % 2][:, k, :], self.xn[:, u, k * P:(k + 1) * P], self.G.ident[:])
            ins.then_inc(*self.T.step(f"tr{u}"))

    def act(self, act, i, xT_free):
        for n in () if self.relu_of is not None else ("", "2") if self.affine else ("",):
            act.wait_ge(*self.V.at("eps" + n, i))
            act.activation(self.std[:], self.rstd[:], ACT.Sqrt).then_inc(*self.Q.step("std" + n))
        act.wait_ge(*xT_free)
        for u in range(GT):
            act.wait_ge(*self.T.at(f"tr{u}", i))
            act.copy(self.xT[:, :, u * P:(u + 1) * P], self.tr[u % 2]).then_inc(*self.C.step(f"cp{u}"))


def rows_of(dram, i):
    return dram.rearrange("(t p) w -> p t w", p=P)[:, bass.ds(i * GT, GT), :]


def spread(a, n):
    return a.rearrange("(o n) -> o n", o=1).broadcast_to([P, n])


def gat_nodes(nc, G, I, tag, W, Wres, att_l, att_r, table, al_dram, ar, keep=None, transposed=False):
    H, C = 8, 32
    with ExitStack() as ctx:
        L = Kit(nc, ctx, tag)
        nrm = Norm(L, G)
        wide = 2 * D if Wres is not None else D
        w = L.sb("w", [P, 2, wide])
        wn = L.sb("wn", [P, 2, D]) if transposed else None
        att = L.sb("att", [P, 2, D])
        tab = L.sb("tab", [P, GT, D])
        prod = L.sb("prod", [P, GT, D])
        al = L.sb("al", [P, GT, H])
        y = [L.ps(f"y{s}", [P, 512]) for s in range(2)]
        loaded = L.sem("loaded")
        turned = L.sem("turned")
        wready = L.sem("wready")
        stored = L.sem("stored")
        M = L.steps("pe_h", "mm0 mm1 mm2 mm3 mm4")
        A = L.steps("act_h", "tab0 tab1 tab2 tab3 tab4")
        V = L.steps("dve_h", ("res0 res1 res2 res3 res4 " if Wres is not None else "") + "pl al pr ar")

        def rows(i):
            return keep[:, bass.ds(i * GT, GT), 0:D] if keep is not None else tab[:]

        with nc.Block() as block:
            @block.sync
            def _(sp):
                L.open(sp)
                sp.dma_start((wn if transposed else w)[:, :, 0:D], W.rearrange("(k p) n -> p k n", p=P)).then_inc(loaded, 16)
                if Wres is not None:
                    sp.dma_start(w[:, :, D:2 * D], Wres.rearrange("(k p) n -> p k n", p=P)).then_inc(loaded, 16)
                sp.dma_start(att[:, 0, :], spread(att_l, D)).then_inc(loaded, 16)
                sp.dma_start(att[:, 1, :], spread(att_r, D)).then_inc(loaded, 16)
                with sp.Fori(0, NG) as i:
                    sp.wait_ge(*V.at("al", i))
                    sp.dma_start(rows_of(table, i), rows(i)).then_inc(stored, 16)
                    sp.dma_start(rows_of(al_dram, i), al[:]).then_inc(stored, 16)
                    sp.wait_ge(stored, i * 32 + 32)
                    sp.sem_inc(turned, 1)

            @block.vector
            def _(dve):
                if transposed:
                    dve.wait_ge(wready, 2)
                    for k in range(2):
                        for n in range(2):
                            ins = dve.tensor_copy(w[:, k, n * P:(n + 1) * P], y[k][:, n * P:(n + 1) * P])
                    ins.then_inc(wready, 1)
                dve.wait_ge(loaded, 64 if Wres is not None else 48)
                with dve.Fori(0, NG) as i:
                    nrm.dve(dve, i)
                    if Wres is not None:
                        for u in range(GT):
                            dve.wait_ge(*M.at(f"mm{u}", i))
                            xt = G.x[:, bass.ds(i * GT + u, 1), :].rearrange("p a d -> p (a d)")
                            dve.tensor_tensor(xt, xt, y[u % 2][:, D:2 * D], ALU.add).then_inc(*V.step(f"res{u}"))
                    dve.wait_ge(*V.ended(i))
                    dve.wait_ge(*A.at("tab4", i))
                    dve.wait_ge(turned, i)
                    dve.tensor_tensor(prod[:], rows(i), att[:, 0, :].unsqueeze(1).broadcast_to([P, GT, D]),
                                      ALU.mult).then_inc(*V.step("pl"))
                    dve.wait_ge(*V.at("pl", i))
                    dve.tensor_reduce(al[:], prod[:].rearrange("p t (h c) -> p t h c", h=H), AX.X,
                                      ALU.add).then_inc(*V.step("al"))
                    dve.wait_ge(*V.at("al", i))
                    dve.tensor_tensor(prod[:], rows(i), att[:, 1, :].unsqueeze(1).broadcast_to([P, GT, D]),
                                      ALU.mult).then_inc(*V.step("pr"))
                    dve.wait_ge(*V.at("pr", i))
                    dve.tensor_reduce(ar(i), prod[:].rearrange("p t (h c) -> p t h c", h=H), AX.X,
                                      ALU.add).then_inc(*V.step("ar"))

            @block.scalar
            def _(act):
                with act.Fori(0, NG) as i:
                    nrm.act(act, i, M.ended(i))
                    if keep is None:
                        act.wait_ge(turned, i)
                        act.wait_ge(*V.ended(i))
                    for u in range(GT):
                        act.wait_ge(*(M.at(f"mm{u}", i) if Wres is None else V.at(f"res{u}", i)))
                        to = tab[:, u, :] if keep is None else keep[:, bass.ds(i * GT + u, 1), 0:D].rearrange("p a d -> p (a d)")
                        act.copy(to, y[u % 2][:, 0:D]).then_inc(*A.step(f"tab{u}"))

            @block.tensor
            def _(pe):
                pe.wait_ge(loaded, 64 if Wres is not None else 48)
                if transposed:
                    for k in range(2):
                        for n in range(2):
                            ins = pe.transpose(y[k][:, n * P:(n + 1) * P], wn[:, n, k * P:(k + 1) * P], G.ident[:])
                        ins.then_inc(wready, 1)
                    pe.wait_ge(wready, 3)
                with pe.Fori(0, NG) as i:
                    nrm.pe(pe, i)
                    pe.wait_ge(*A.ended(i))
                    for u in range(GT):
                        pe.wait_ge(*nrm.C.at(f"cp{u}", i))
                        if u >= 2:
                            pe.wait_ge(*A.at(f"tab{u - 2}", i))
                        for k in range(2):
                            ins = pe.matmul(y[u % 2][:, 0:wide], nrm.xT[:, k, u * P:(u + 1) * P], w[:, k, :],
                                            start=(k == 0), stop=(k == 1))
                        ins.then_inc(*M.step(f"mm{u}"))


def one_hots(dve, G, X, oh, c, chunks=U, scale=None):
    return dve.tensor_tensor(oh, G.iota[:].unsqueeze(1).broadcast_to([P, chunks, P]),
                             X.local[:, bass.ds(c, chunks)].unsqueeze(2).broadcast_to([P, chunks, P]), ALU.is_equal)


def attention_pass(nc, G, tag, X, H, al_dram, width, al_at, ar, alpha, weight=None, keep=None):
    with ExitStack() as ctx:
        L = Kit(nc, ctx, tag)
        row = L.sb("row", [P, IT, width])
        at = L.sb("at", [P, 2, U], I32)
        oh = L.sb("oh", [P, 2, U, P])
        ohT = L.sb("ohT", [P, 2, U * P])
        s = L.sb("s", [P, 2, U, H])
        turn = [L.ps(f"turn{h}", [P, U, P]) for h in range(2)]
        atdst = [L.ps(f"atdst{h}", [P, U, H]) for h in range(2)]
        got, before = L.row_sems(X.chunks // IT)
        took = L.sem("took")
        V = L.steps("dve_alpha", "oh0 oh1 " + " ".join(f"sum{h} " + (f"w{h} " if weight is not None else "") + f"alpha{h}" for h in range(2)))
        A = L.steps("act_turned", "at0 at1 T0 T1" + (" keep0 keep1" if keep is not None else ""))
        M = L.steps("pe_dst", "tr0 tr1 dst0 dst1")
        n = X.chunks // IT
        with nc.Block() as block:
            @block.sync
            def _(sp):
                L.open(sp)

            @block.gpsimd
            def _(pool):
                with pool.Fori(0, n) as i:
                    for h in range(2):
                        pool.wait_ge(*A.at(f"at{h}", i))
                        pool.sem_inc(took, 1)
                        for u in range(U):
                            pool.indirect_dma_start(
                                out=row[:, h * U + u, :], out_offset=None, in_=al_dram,
                                in_offset=bass.IndirectOffsetOnAxis(ap=at[:, h, u:u + 1], axis=0)
                            ).then_inc(got[h * U + u], 16)

            @block.scalar
            def _(act):
                with act.Fori(0, n) as i:
                    for h in range(2):
                        act.wait_ge(*V.at(f"sum{h}", i - 1))
                        if keep is not None:
                            act.wait_ge(*A.at(f"keep{h}", i - 1))
                        act.copy(at[:, h, :], X.src[:, bass.ds(i * IT + h * U, U)]).then_inc(*A.step(f"at{h}"))
                    for h in range(2):
                        act.wait_ge(*M.at(f"tr{h}", i))
                        act.wait_ge(*M.at(f"dst{h}", i - 1))
                        act.copy(ohT[:, h, :], turn[h][:].rearrange("p u e -> p (u e)")).then_inc(*A.step(f"T{h}"))
                    if keep is not None:
                        for h in range(2):
                            for u in range(U):
                                act.wait_ge(got[h * U + u], i * 16 + (16 + before))
                            act.copy(keep[:, bass.ds(i * IT + h * U, U), :],
                                     row[:, h * U:(h + 1) * U, 0:al_at]).then_inc(*A.step(f"keep{h}"))

            @block.vector
            def _(dve):
                with dve.Fori(0, n) as i:
                    for h in range(2):
                        dve.wait_ge(*M.at(f"tr{h}", i - 1))
                        one_hots(dve, G, X, oh[:, h], i * IT + h * U).then_inc(*V.step(f"oh{h}"))
                    for h in range(2):
                        c = i * IT + h * U
                        for u in range(U):
                            dve.wait_ge(got[h * U + u], i * 16 + (16 + before))
                        dve.wait_ge(*M.at(f"dst{h}", i))
                        dve.wait_ge(*V.at(f"alpha{h}", i - 1))
                        dve.tensor_tensor(s[:, h], row[:, h * U:(h + 1) * U, al_at:al_at + H], atdst[h][:],
                                          ALU.add).then_inc(*V.step(f"sum{h}"))
                        if weight is not None:
                            dve.wait_ge(*V.at(f"sum{h}", i))
                            dve.tensor_tensor(s[:, h], s[:, h],
                                              weight[:, bass.ds(c, U)].unsqueeze(2).broadcast_to([P, U, H]),
                                              ALU.mult).then_inc(*V.step(f"w{h}"))
                        dve.wait_ge(*V.at(f"w{h}" if weight is not None else f"sum{h}", i))
                        flat = s[:, h].rearrange("p u h -> p (u h)")
                        dve.scalar_tensor_tensor(alpha[:, bass.ds(c, U), :].rearrange("p u h -> p (u h)"), flat, 0.2,
                                                 flat, ALU.mult, ALU.max).then_inc(*V.step(f"alpha{h}"))

            @block.tensor
            def _(pe):
                with pe.Fori(0, n) as i:
                    for h in range(2):
                        pe.wait_ge(*V.at(f"oh{h}", i))
                        pe.wait_ge(*A.at(f"T{h}", i - 1))
                        for u in range(U):
                            ins = pe.transpose(turn[h][:, u, :], oh[:, h, u, :], G.ident[:])
                        ins.then_inc(*M.step(f"tr{h}"))
                    for h in range(2):
                        pe.wait_ge(*A.at(f"T{h}", i))
                        pe.wait_ge(*V.at(f"sum{h}", i - 1))
                        for u in range(U):
                            t = pe.value_load(X.tile[0:1, bass.ds(i * IT + h * U + u, 1)], min_val=0, max_val=NT - 1)
                            ins = pe.matmul(atdst[h][:, u, :], ohT[:, h, u * P:(u + 1) * P],
                                            ar[:, bass.ds(t, 1), :].rearrange("p a h -> p (a h)"), start=True, stop=True)
                        ins.then_inc(*M.step(f"dst{h}"))


def softmax_pass(nc, G, tag, X, H, alpha):
    S = P // H
    g = X.chunks // S
    W = g * P
    with ExitStack() as ctx:
        L = Kit(nc, ctx, tag)
        dst8 = L.sb("dst8", [P, X.chunks, H])
        slot = L.sb("slot", [P, 2, 2, P])
        aT = L.sb("aT", [P, W])
        dT = L.sb("dT", [P, W])
        cut = L.sb("cut", [P, W + 1])
        top = L.sb("top", [P, W])
        ends = L.sb("ends", [P, 4])
        rhs = L.sb("rhs", [P, 4, S])
        vk = L.sb("vk", [P, 4, S])
        hit = L.sb("hit", [P, 2, 2 * S])
        both = L.sb("both", [P, 2])
        key_i = L.sb("key_i", [P, 3, P], I32)
        keyf = L.sb("keyf", [P, 3, P])
        same = L.sb("same", [P, P])
        seg = L.sb("seg", [P, S])
        turn = [L.ps(f"turn{s}", [P, 2, P]) for s in range(2)]
        pj = L.ps("pj", [P, 4, S])
        bits = {8: 3, 4: 2}[H]
        chain = L.sem("chain")
        expd = L.sem("expd")
        joined = L.sem("joined")
        ready2 = L.sem("pool_out")
        M = L.steps("pe_in", "in0 in1")
        A = L.steps("act_in", "sa0 sd0 sa1 sd1")
        V = L.steps("dve_in", "a0 d0 a1 d1")
        M2 = L.steps("pe_out", "out0 out1")
        A2 = L.steps("act_out", "out0 out1")
        aview = alpha.rearrange("p (s g) h -> p g s h", g=g)
        dview = dst8[:].rearrange("p (s g) h -> p g s h", g=g)
        with nc.Block() as block:
            @block.sync
            def _(sp):
                L.open(sp)

            @block.vector
            def _(dve):
                k = [0]

                def link(ins):
                    k[0] += 1
                    ins.then_inc(chain, 1)
                    dve.wait_ge(chain, k[0])

                link(dve.tensor_copy(dst8[:], X.dst[:].unsqueeze(2).broadcast_to([P, X.chunks, H])))
                link(dve.tensor_copy(key_i[:, 0, :], G.iota[:]))
                link(dve.tensor_copy(key_i[:, 1, :], G.part[:, 0:1].broadcast_to([P, P])))
                link(dve.tensor_scalar(key_i[:, 2, :], key_i[:, 1, :], bits, None, ALU.arith_shift_right))
                link(dve.tensor_scalar(key_i[:, 0:2, :], key_i[:, 0:2, :], H - 1, None, ALU.bitwise_and))
                link(dve.tensor_copy(keyf[:], key_i[:]))
                link(dve.tensor_tensor(same[:], keyf[:, 0, :], keyf[:, 1, :], ALU.is_equal))
                link(dve.tensor_tensor(seg[:], G.iota[:, 0:S], keyf[:, 2, 0:S], ALU.is_equal))
                with dve.Fori(0, g // 2) as i:
                    for s in range(2):
                        dve.wait_ge(*M.at(f"in{s}", i))
                        dve.tensor_copy(aT[:, bass.ds((i * 2 + s) * P, P)], turn[s][:, 0, :]).then_inc(*V.step(f"a{s}"))
                        dve.tensor_copy(dT[:, bass.ds((i * 2 + s) * P, P)], turn[s][:, 1, :]).then_inc(*V.step(f"d{s}"))
                dve.wait_ge(*V.ended(g // 2))
                link(dve.memset(cut[:], 0.0))
                link(dve.tensor_tensor(cut[:, 1:W], dT[:, 1:W], dT[:, 0:W - 1], ALU.not_equal))
                link(dve.tensor_scalar(cut[:, 1:W], cut[:, 1:W], -BIG, None, ALU.mult))
                link(dve.tensor_tensor_scan(top[:], cut[:, 0:W], aT[:], -BIG, ALU.add, ALU.max))
                link(dve.tensor_tensor_scan(top[:, ::-1], cut[:, W:0:-1], top[:, ::-1], -BIG, ALU.add, ALU.max))
                link(dve.tensor_copy(ends[:, 0:1], top[:, 0:1]))
                link(dve.tensor_copy(ends[:, 1:2], top[:, W - 1:W]))
                link(dve.tensor_copy(ends[:, 2:3], dT[:, 0:1]))
                link(dve.tensor_copy(ends[:, 3:4], dT[:, W - 1:W]))
                for q in range(4):
                    link(dve.tensor_scalar(rhs[:, q, :], seg[:], ends[:, q:q + 1], None, ALU.mult))
                dve.wait_ge(joined, 1)
                link(dve.tensor_copy(vk[:], pj[:]))
                val = vk[:, 0:2, :].rearrange("p a s -> p (a s)")
                key = vk[:, 2:4, :].rearrange("p a s -> p (a s)")
                for q in range(2):
                    link(dve.tensor_scalar(hit[:, q, :], key, ends[:, 2 + q:3 + q], -BIG, ALU.not_equal, ALU.mult))
                    link(dve.tensor_tensor(hit[:, q, :], hit[:, q, :], val, ALU.add))
                    link(dve.tensor_reduce(both[:, q:q + 1], hit[:, q, :], AX.X, ALU.max))
                for q in range(2):
                    link(dve.tensor_scalar(cut[:, 0:W], dT[:], ends[:, 2 + q:3 + q], -BIG, ALU.not_equal, ALU.mult))
                    link(dve.scalar_tensor_tensor(top[:], cut[:, 0:W], both[:, q:q + 1], top[:], ALU.add, ALU.max))
                link(dve.tensor_tensor(aT[:], aT[:], top[:], ALU.subtract))
                dve.sem_inc(joined, 1)

            @block.scalar
            def _(act):
                act.wait_ge(chain, 1)
                with act.Fori(0, g // 2) as i:
                    for s in range(2):
                        act.wait_ge(*M.ended(i))
                        v = slot[:, s, 0, :].rearrange("p (s h) -> p s h", h=H)
                        w = slot[:, s, 1, :].rearrange("p (s h) -> p s h", h=H)
                        act.copy(v, aview[:, bass.ds(i * 2 + s, 1)].rearrange("p a s h -> p (a s) h")).then_inc(*A.step(f"sa{s}"))
                        act.copy(w, dview[:, bass.ds(i * 2 + s, 1)].rearrange("p a s h -> p (a s) h")).then_inc(*A.step(f"sd{s}"))
                act.wait_ge(joined, 2)
                act.activation(top[:], aT[:], ACT.Exp).then_inc(expd, 1)
                act.wait_ge(expd, 1)
                with act.Fori(0, g // 2) as i:
                    for s in range(2):
                        act.wait_ge(*M2.at(f"out{s}", i))
                        act.copy(aview[:, bass.ds(i * 2 + s, 1)].rearrange("p a s h -> p (a s) h"),
                                 turn[s][:, 0, :].rearrange("p (s h) -> p s h", h=H)).then_inc(*A2.step(f"out{s}"))

            @block.tensor
            def _(pe):
                with pe.Fori(0, g // 2) as i:
                    for s in range(2):
                        pe.wait_ge(*A.at(f"sd{s}", i))
                        pe.wait_ge(*V.ended(i))
                        pe.transpose(turn[s][:, 0, :], slot[:, s, 0, :], G.ident[:])
                        pe.transpose(turn[s][:, 1, :], slot[:, s, 1, :], G.ident[:]).then_inc(*M.step(f"in{s}"))
                pe.wait_ge(chain, 21)
                pe.matmul(pj[:], same[:], rhs[:], start=True, stop=True).then_inc(joined, 1)
                pe.wait_ge(expd, 2)
                with pe.Fori(0, g // 2) as i:
                    for s in range(2):
                        pe.wait_ge(ready2, i * 2 + s + 1)
                        pe.wait_ge(*A2.ended(i))
                        pe.transpose(turn[s][:, 0, :], slot[:, s, 0, :], G.ident[:]).then_inc(*M2.step(f"out{s}"))

            @block.gpsimd
            def _(pool):
                pool.wait_ge(expd, 1)
                pool.sem_inc(expd, 1)
                with pool.Fori(0, g // 2) as i:
                    for s in range(2):
                        pool.wait_ge(*M2.ended(i))
                        pool.sem_inc(joined, 1)
                        pool.tensor_copy(slot[:, s, 0, :], top[:, bass.ds((i * 2 + s) * P, P)]).then_inc(ready2, 1)


def message_pass(nc, G, tag, X, H, C, table, ex, acc, rows=None):
    W = H * C
    AW = W + H
    with ExitStack() as ctx:
        L = Kit(nc, ctx, tag)
        row = L.sb("row", [P, IT, W]) if rows is None else None
        at = L.sb("at", [P, 2, U], I32)
        oh = L.sb("oh", [P, 2, U, P])
        msg = L.sb("msg", [P, 2, U, AW])
        banks = [[L.ps(f"sum{h}_{u}", [P, 512]) for u in range(U)] for h in range(2)]
        got, before = L.row_sems(X.chunks // IT if rows is None else 0)
        took = L.sem("took")
        V = L.steps("dve_msg", "oh0 ex0 msg0 oh1 ex1 msg1 " + " ".join(f"acc{u}" for u in range(IT)))
        A = L.steps("act_at", "at0 at1")
        M = L.steps("pe_sum", " ".join(f"sum{u}" for u in range(IT)))
        n = X.chunks // IT
        with nc.Block() as block:
            @block.sync
            def _(sp):
                L.open(sp)

            if rows is None:
                @block.gpsimd
                def _(pool):
                    with pool.Fori(0, n) as i:
                        for h in range(2):
                            pool.wait_ge(*A.at(f"at{h}", i))
                            pool.sem_inc(took, 1)
                            for u in range(U):
                                pool.indirect_dma_start(
                                    out=row[:, h * U + u, :], out_offset=None, in_=table,
                                    in_offset=bass.IndirectOffsetOnAxis(ap=at[:, h, u:u + 1], axis=0)
                                ).then_inc(got[h * U + u], 16)

                @block.scalar
                def _(act):
                    with act.Fori(0, n) as i:
                        for h in range(2):
                            act.wait_ge(*V.at(f"msg{h}", i - 1))
                            act.copy(at[:, h, :], X.src[:, bass.ds(i * IT + h * U, U)]).then_inc(*A.step(f"at{h}"))

            @block.vector
            def _(dve):
                with dve.Fori(0, n) as i:
                    for h in range(2):
                        c = i * IT + h * U
                        dve.wait_ge(*M.at(f"sum{h * U + U - 1}", i - 1))
                        one_hots(dve, G, X, oh[:, h], c).then_inc(*V.step(f"oh{h}"))
                        dve.tensor_copy(msg[:, h, :, W:AW], ex[:, bass.ds(c, U), :]).then_inc(*V.step(f"ex{h}"))
                        if rows is None:
                            for u in range(U):
                                dve.wait_ge(got[h * U + u], i * 16 + (16 + before))
                            r = row[:, h * U:(h + 1) * U, :]
                        else:
                            r = rows[:, bass.ds(c, U), :]
                        dve.tensor_tensor(msg[:, h, :, 0:W].rearrange("p u (h c) -> p u h c", h=H),
                                          r.rearrange("p u (h c) -> p u h c", h=H),
                                          ex[:, bass.ds(c, U), :].unsqueeze(3).broadcast_to([P, U, H, C]),
                                          ALU.mult).then_inc(*V.step(f"msg{h}"))
                    for u in range(IT):
                        t = dve.value_load(X.tile[0:1, bass.ds(i * IT + u, 1)], min_val=0, max_val=NT - 1)
                        a = acc[:, bass.ds(t, 1), :].rearrange("p a w -> p (a w)")
                        dve.wait_ge(*M.at(f"sum{u}", i))
                        dve.wait_ge(*(V.at(f"acc{u - 1}", i) if u else V.at(f"acc{IT - 1}", i - 1)))
                        dve.tensor_tensor(a, a, banks[u // U][u % U][:, 0:AW], ALU.add).then_inc(*V.step(f"acc{u}"))

            @block.tensor
            def _(pe):
                with pe.Fori(0, n) as i:
                    for h in range(2):
                        pe.wait_ge(*V.at(f"msg{h}", i))
                        for u in range(U):
                            pe.wait_ge(*V.at(f"acc{h * U + u}", i - 1))
                            pe.matmul(banks[h][u][:, 0:AW], oh[:, h, u, :], msg[:, h, u, :],
                                      start=True, stop=True).then_inc(*M.step(f"sum{h * U + u}"))


def clear(nc, tag, t, value=0.0):
    with ExitStack() as ctx:
        L = Kit(nc, ctx, tag)
        done = L.sem("done")
        with nc.Block() as block:
            @block.vector
            def _(dve):
                dve.memset(t, value).then_inc(done, 1)


def finish_l0_gnn(nc, G, acc):
    H, C = 8, 32
    with ExitStack() as ctx:
        L = Kit(nc, ctx, "f0")
        den = L.sb("den", [P, NT, H])
        z = L.sb("z", [P, GT, D])
        low = L.sb("low", [P, GT, D])
        ready = L.sem("ready")
        V = L.steps("dve_elu", "z low x1 x2")
        A = L.steps("act_elu", "exp")
        with nc.Block() as block:
            @block.sync
            def _(sp):
                L.open(sp)

            @block.vector
            def _(dve):
                dve.tensor_scalar(den[:], acc[:, :, D:D + H], 1e-16, None, ALU.add).then_inc(ready, 1)
                dve.wait_ge(ready, 1)
                dve.reciprocal(den[:], den[:]).then_inc(ready, 1)
                dve.wait_ge(ready, 2)
                with dve.Fori(0, NG) as i:
                    dve.wait_ge(*V.ended(i))
                    dve.tensor_tensor(z[:].rearrange("p t (h c) -> p t h c", h=H),
                                      acc[:, bass.ds(i * GT, GT), 0:D].rearrange("p t (h c) -> p t h c", h=H),
                                      den[:, bass.ds(i * GT, GT), :].unsqueeze(3).broadcast_to([P, GT, H, C]),
                                      ALU.mult).then_inc(*V.step("z"))
                    dve.wait_ge(*V.at("z", i))
                    dve.tensor_scalar(low[:], z[:], 0.0, None, ALU.min).then_inc(*V.step("low"))
                    xg = G.x[:, bass.ds(i * GT, GT), :].rearrange("p t d -> p (t d)")
                    dve.scalar_tensor_tensor(xg, z[:].rearrange("p t d -> p (t d)"), 0.0, xg, ALU.max,
                                             ALU.add).then_inc(*V.step("x1"))
                    dve.wait_ge(*V.at("x1", i))
                    dve.wait_ge(*A.at("exp", i))
                    dve.scalar_tensor_tensor(xg, low[:].rearrange("p t d -> p (t d)"), -1.0, xg, ALU.add,
                                             ALU.add).then_inc(*V.step("x2"))

            @block.scalar
            def _(act):
                with act.Fori(0, NG) as i:
                    act.wait_ge(*V.at("low", i))
                    act.activation(low[:], low[:], ACT.Exp).then_inc(*A.step("exp"))


def router_nodes(nc, G, I, table, ad):
    HE = 16
    with ExitStack() as ctx:
        L = Kit(nc, ctx, "rn")
        nrm = Norm(L, G)
        w = L.sb("w", [P, 2, HE])
        att = L.sb("att", [P, 2, HE])
        rows = L.sb("rows", [P, GT, HE + 4])
        prod = L.sb("prod", [P, GT, HE])
        y = [L.ps(f"y{s}", [P, HE]) for s in range(2)]
        loaded = L.sem("loaded")
        stored = L.sem("stored")
        M = L.steps("pe_h", "mm0 mm1 mm2 mm3 mm4")
        V = L.steps("dve_h", "h0 h1 h2 h3 h4 ps as pd ad")
        with nc.Block() as block:
            @block.sync
            def _(sp):
                L.open(sp)
                with nc.allow_non_contiguous_dma(reason="a small weight"):
                    sp.dma_start(w[:], I["L0_ffn_W_gat"].rearrange("(k p) n -> p k n", p=P)).then_inc(loaded, 16)
                sp.dma_start(att[:, 0, :], spread(I["L0_ffn_att_src"].rearrange("h e -> (h e)"), HE)).then_inc(loaded, 16)
                sp.dma_start(att[:, 1, :], spread(I["L0_ffn_att_dst"].rearrange("h e -> (h e)"), HE)).then_inc(loaded, 16)
                with sp.Fori(0, NG) as i:
                    sp.wait_ge(*V.at("as", i))
                    sp.dma_start(rows_of(table, i), rows[:]).then_inc(stored, 16)
                sp.wait_ge(stored, 16 * NG)

            @block.vector
            def _(dve):
                dve.wait_ge(loaded, 48)
                with dve.Fori(0, NG) as i:
                    nrm.dve(dve, i)
                    dve.wait_ge(stored, i * 16)
                    for u in range(GT):
                        dve.wait_ge(*M.at(f"mm{u}", i))
                        dve.tensor_copy(rows[:, u, 0:HE], y[u % 2]).then_inc(*V.step(f"h{u}"))
                    dve.wait_ge(*V.at("h4", i))
                    for q, (p, a) in enumerate((("ps", "as"), ("pd", "ad"))):
                        if q:
                            dve.wait_ge(*V.at("as", i))
                        dve.tensor_tensor(prod[:], rows[:, :, 0:HE],
                                          att[:, q, :].unsqueeze(1).broadcast_to([P, GT, HE]), ALU.mult).then_inc(*V.step(p))
                        dve.wait_ge(*V.at(p, i))
                        to = rows[:, :, HE:HE + 4] if q == 0 else ad[:, bass.ds(i * GT, GT), :]
                        dve.tensor_reduce(to, prod[:].rearrange("p t (h e) -> p t h e", h=4), AX.X,
                                          ALU.add).then_inc(*V.step(a))

            @block.scalar
            def _(act):
                with act.Fori(0, NG) as i:
                    nrm.act(act, i, M.ended(i))

            @block.tensor
            def _(pe):
                pe.wait_ge(loaded, 48)
                with pe.Fori(0, NG) as i:
                    nrm.pe(pe, i)
                    for u in range(GT):
                        pe.wait_ge(*nrm.C.at(f"cp{u}", i))
                        pe.wait_ge(*(V.at(f"h{u - 2}", i) if u >= 2 else V.ended(i)))
                        for k in range(2):
                            ins = pe.matmul(y[u % 2], nrm.xT[:, k, u * P:(u + 1) * P], w[:, k, :],
                                            start=(k == 0), stop=(k == 1))
                        ins.then_inc(*M.step(f"mm{u}"))


def top2(L, G, dve, link, score, gates, n):
    rank = L.sb("t_rank", [P, NT, n])
    pair = L.sb("t_pair", [P, NT, n, n])
    tie = L.sb("t_tie", [P, NT, n, n])
    first = L.sb("t_first", [P, n, n])
    big = L.sb("t_big", [P, 4, NT])
    one = L.sb("t_one", [P, 2, NT, n])
    pick = L.sb("t_pick", [P, NT, n])
    other = score.unsqueeze(2).broadcast_to([P, NT, n, n])
    own = score.unsqueeze(3).broadcast_to([P, NT, n, n])
    for e in range(n):
        link(dve.tensor_scalar(first[:, e, :], G.iota[:, 0:n], float(e), None, ALU.is_lt))
    link(dve.tensor_tensor(tie[:], other, own, ALU.is_equal))
    for t in range(NT):
        link(dve.tensor_tensor(tie[:, t], tie[:, t], first[:], ALU.mult))
    link(dve.tensor_tensor(pair[:], other, own, ALU.is_gt))
    link(dve.tensor_tensor(pair[:], pair[:], tie[:], ALU.add))
    link(dve.tensor_reduce(rank[:], pair[:], AX.X, ALU.add))
    for r in range(2):
        link(dve.tensor_scalar(one[:, r], rank[:], float(r), None, ALU.is_equal))
        link(dve.tensor_tensor(pick[:], one[:, r], score, ALU.mult))
        link(dve.tensor_reduce(big[:, r, :], pick[:], AX.X, ALU.add))
    link(dve.tensor_tensor(big[:, 2, :], big[:, 1, :], big[:, 0, :], ALU.subtract))

    def after_exp():
        link(dve.tensor_scalar(big[:, 3, :], big[:, 2, :], 1.0, None, ALU.add))
        link(dve.reciprocal(big[:, 3, :], big[:, 3, :]))
        link(dve.tensor_tensor(big[:, 2, :], big[:, 2, :], big[:, 3, :], ALU.mult))
        link(dve.tensor_tensor(one[:, 0], one[:, 0], big[:, 3, :].unsqueeze(2).broadcast_to([P, NT, n]), ALU.mult))
        link(dve.tensor_tensor(one[:, 1], one[:, 1], big[:, 2, :].unsqueeze(2).broadcast_to([P, NT, n]), ALU.mult))
        link(dve.tensor_tensor(gates, one[:, 0], one[:, 1], ALU.add))
    return big[:, 2, :], after_exp


def chained(eng, sem):
    k = [0]

    def link(ins):
        k[0] += 1
        ins.then_inc(sem, 1)
        eng.wait_ge(sem, k[0])
    return link


def router_gates(nc, G, I, acc, gates):
    HE = 16
    with ExitStack() as ctx:
        L = Kit(nc, ctx, "rg")
        par = L.sb("par", [P, 3, HE])
        z = L.sb("z", [P, NT, HE])
        sq = L.sb("sq", [P, NT, HE])
        den = L.sb("den", [P, NT, 4])
        mean = L.sb("mean", [P, NT])
        var = L.sb("var", [P, NT])
        score = L.sb("score", [P, NT, 4])
        loaded, chain, ask, done = L.sem("loaded"), L.sem("chain"), L.sem("ask"), L.sem("done")
        second = {}
        with nc.Block() as block:
            @block.sync
            def _(sp):
                for q, name in enumerate(("L0_ffn_b_gat", "L0_ffn_ln_gamma", "L0_ffn_ln_beta")):
                    sp.dma_start(par[:, q, :], spread(I[name], HE)).then_inc(loaded, 16)

            @block.vector
            def _(dve):
                link = chained(dve, chain)

                def row(q):
                    return par[:, q, :].unsqueeze(1).broadcast_to([P, NT, HE])

                def per_token(a):
                    return a.unsqueeze(2).broadcast_to([P, NT, HE])

                link(dve.tensor_scalar(den[:], acc[:, :, HE:HE + 4], 1e-16, None, ALU.add))
                link(dve.reciprocal(den[:], den[:]))
                link(dve.tensor_tensor(z[:].rearrange("p t (h e) -> p t h e", h=4),
                                       acc[:, :, 0:HE].rearrange("p t (h e) -> p t h e", h=4),
                                       den[:].unsqueeze(3).broadcast_to([P, NT, 4, 4]), ALU.mult))
                dve.wait_ge(loaded, 48)
                link(dve.tensor_tensor(z[:], z[:], row(0), ALU.add))
                link(dve.tensor_reduce(mean[:], z[:], AX.X, ALU.add))
                link(dve.tensor_scalar(mean[:], mean[:], 1.0 / HE, None, ALU.mult))
                link(dve.tensor_tensor(z[:], z[:], per_token(mean[:]), ALU.subtract))
                link(dve.tensor_tensor(sq[:], z[:], z[:], ALU.mult))
                link(dve.tensor_reduce(var[:], sq[:], AX.X, ALU.add))
                link(dve.tensor_scalar(var[:], var[:], 1.0 / HE, EPS, ALU.mult, ALU.add))
                dve.sem_inc(ask, 1)
                dve.wait_ge(done, 1)
                link(dve.reciprocal(var[:], mean[:]))
                link(dve.tensor_tensor(z[:], z[:], per_token(var[:]), ALU.mult))
                link(dve.tensor_tensor(z[:], z[:], row(1), ALU.mult))
                link(dve.tensor_tensor(z[:], z[:], row(2), ALU.add))
                link(dve.tensor_reduce(score[:], z[:].rearrange("p t (h e) -> p t e h", h=4), AX.X, ALU.add))
                link(dve.tensor_scalar(score[:], score[:], 0.25, None, ALU.mult))
                second["ap"], after = top2(L, G, dve, link, score[:], gates[:], 4)
                dve.sem_inc(ask, 1)
                dve.wait_ge(done, 2)
                after()

            @block.scalar
            def _(act):
                act.wait_ge(ask, 1)
                act.activation(mean[:], var[:], ACT.Sqrt).then_inc(done, 1)
                act.wait_ge(ask, 2)
                act.activation(second["ap"], second["ap"], ACT.Exp).then_inc(done, 1)


def gate_bias(nc, G, tag, gates, n, bias):
    with ExitStack() as ctx:
        L = Kit(nc, ctx, tag)
        gs = L.sb("gs", [P, GT, n])
        gT = L.sb("gT", [n, GT, P])
        tr = [L.ps(f"tr{s}", [n, P]) for s in range(2)]
        y = [L.ps(f"y{s}", [P, D]) for s in range(2)]
        M = L.steps("pe_bias", "tr0 tr1 tr2 tr3 tr4 mm0 mm1 mm2 mm3 mm4")
        A = L.steps("act_bias", "gs cp0 cp1 cp2 cp3 cp4")
        V = L.steps("dve_bias", "x0 x1 x2 x3 x4")
        with nc.Block() as block:
            @block.sync
            def _(sp):
                L.open(sp)

            @block.scalar
            def _(act):
                with act.Fori(0, NG) as i:
                    act.wait_ge(*M.ended(i))
                    act.copy(gs[:], gates[:, bass.ds(i * GT, GT), :]).then_inc(*A.step("gs"))
                    for u in range(GT):
                        act.wait_ge(*M.at(f"tr{u}", i))
                        act.copy(gT[:, u, :], tr[u % 2]).then_inc(*A.step(f"cp{u}"))

            @block.tensor
            def _(pe):
                with pe.Fori(0, NG) as i:
                    pe.wait_ge(*A.at("gs", i))
                    for u in range(GT):
                        if u >= 2:
                            pe.wait_ge(*A.at(f"cp{u - 2}", i))
                        pe.transpose(tr[u % 2], gs[:, u, :], G.ident[:]).then_inc(*M.step(f"tr{u}"))
                    for u in range(GT):
                        pe.wait_ge(*A.at(f"cp{u}", i))
                        pe.wait_ge(*(V.at(f"x{u - 2}", i) if u >= 2 else V.ended(i)))
                        pe.matmul(y[u % 2], gT[:, u, :], bias[:], start=True, stop=True).then_inc(*M.step(f"mm{u}"))

            @block.vector
            def _(dve):
                with dve.Fori(0, NG) as i:
                    for u in range(GT):
                        dve.wait_ge(*M.at(f"mm{u}", i))
                        xt = G.x[:, bass.ds(i * GT + u, 1), :].rearrange("p a d -> p (a d)")
                        dve.tensor_tensor(xt, xt, y[u % 2], ALU.add).then_inc(*V.step(f"x{u}"))


def gelu_experts(nc, G, tag, W1, b1, W2, gates, n, affine_of=None):
    F = 512
    HC = F // P
    HALF = GT * P // 2
    with ExitStack() as ctx:
        L = Kit(nc, ctx, tag)
        affine = (L.sb("gamma", [P, D]), L.sb("beta", [P, D])) if affine_of else None
        nrm = Norm(L, G, affine)
        w1 = L.sb("w1", [P, n, 2, F])
        w2 = L.sb("w2", [P, n, HC, D])
        b1T = L.sb("b1T", [P, n, HC])
        hT = L.sb("hT", [P, 2, HC, GT * P])
        hp = [[L.ps(f"hp{s}{f}", [P, HALF]) for f in range(2)] for s in range(2)]
        y = [L.ps(f"y{s}", [P, D]) for s in range(2)]
        loaded = L.sem("loaded")
        names = ""
        for e in range(n + 1):
            if e < n:
                names += " ".join(f"h{e}_{c}" for c in range(HC)) + " "
            if e:
                names += " ".join(f"y{e - 1}_{u}" for u in range(GT)) + " "
        M = L.steps("pe_ffn", names)
        A = L.steps("act_gelu", " ".join(f"g{e}_{c}" for e in range(n) for c in range(HC)))
        V = L.steps("dve_gated", " ".join(f"x{e}_{u}" for e in range(n) for u in range(GT)))
        loads = 16 * (3 + (2 if affine_of else 0))
        with nc.Block() as block:
            @block.sync
            def _(sp):
                L.open(sp)
                if affine_of:
                    sp.dma_start(affine[0][:], spread(affine_of[0], D)).then_inc(loaded, 16)
                    sp.dma_start(affine[1][:], spread(affine_of[1], D)).then_inc(loaded, 16)
                with nc.allow_non_contiguous_dma(reason="biases, hidden units to partitions"):
                    sp.dma_start(b1T[:], b1.rearrange("e (c p) -> p e c", p=P)).then_inc(loaded, 16)
                sp.dma_start(w1[:], W1.rearrange("e (k p) f -> p e k f", p=P)).then_inc(loaded, 16)
                sp.dma_start(w2[:], W2.rearrange("e (c p) d -> p e c d", p=P)).then_inc(loaded, 16)

            @block.vector
            def _(dve):
                dve.wait_ge(loaded, loads)
                with dve.Fori(0, NG) as i:
                    nrm.dve(dve, i)
                    for e in range(n):
                        for u in range(GT):
                            dve.wait_ge(*M.at(f"y{e}_{u}", i))
                            if e:
                                dve.wait_ge(*V.at(f"x{e - 1}_{u}", i))
                            xt = G.x[:, bass.ds(i * GT + u, 1), :].rearrange("p a d -> p (a d)")
                            dve.scalar_tensor_tensor(
                                xt, y[u % 2], gates[:, bass.ds(i * GT + u, 1), e:e + 1].rearrange("p a e -> p (a e)"),
                                xt, ALU.mult, ALU.add).then_inc(*V.step(f"x{e}_{u}"))

            @block.scalar
            def _(act):
                act.wait_ge(loaded, loads)
                with act.Fori(0, NG) as i:
                    nrm.act(act, i, M.ended(i))
                    for e in range(n):
                        for c in range(HC):
                            if c == 0:
                                act.wait_ge(*(M.at(f"y{e - 2}_{GT - 1}", i) if e >= 2 else M.ended(i)))
                            act.wait_ge(*M.at(f"h{e}_{c}", i))
                            for f in range(2):
                                ins = act.activation(hT[:, e % 2, c, f * HALF:(f + 1) * HALF],
                                                     hp[c % 2][f], ACT.Gelu, bias=b1T[:, e, c:c + 1])
                            ins.then_inc(*A.step(f"g{e}_{c}"))

            @block.tensor
            def _(pe):
                pe.wait_ge(loaded, loads)
                with pe.Fori(0, NG) as i:
                    nrm.pe(pe, i)
                    pe.wait_ge(*nrm.C.at(f"cp{GT - 1}", i))
                    for e in range(n + 1):
                        if e < n:
                            for c in range(HC):
                                q = e * HC + c - 2
                                pe.wait_ge(*(A.at(f"g{q // HC}_{q % HC}", i) if q >= 0 else A.ended(i)))
                                for f in range(2):
                                    for k in range(2):
                                        ins = pe.matmul(hp[c % 2][f], w1[:, e, k, c * P:(c + 1) * P],
                                                        nrm.xT[:, k, f * HALF:(f + 1) * HALF],
                                                        start=(k == 0), stop=(k == 1))
                                ins.then_inc(*M.step(f"h{e}_{c}"))
                        if e:
                            pe.wait_ge(*A.at(f"g{e - 1}_{HC - 1}", i))
                            for u in range(GT):
                                q = (e - 1) * GT + u
                                if u >= 2:
                                    pe.wait_ge(*V.at(f"x{e - 1}_{u - 2}", i))
                                else:
                                    pe.wait_ge(*(V.at(f"x{e - 2}_{GT - 1}", i) if e >= 2 else V.ended(i)))
                                for c in range(HC):
                                    ins = pe.matmul(y[u % 2], hT[:, (e - 1) % 2, c, u * P:(u + 1) * P],
                                                    w2[:, e - 1, c, :], start=(c == 0), stop=(c == HC - 1))
                                ins.then_inc(*M.step(f"y{e - 1}_{u}"))


def load(nc, tag, *pairs):
    with ExitStack() as ctx:
        L = Kit(nc, ctx, tag)
        loaded = L.sem("loaded")
        with nc.Block() as block:
            @block.sync
            def _(sp):
                for to, a in zip(pairs[::2], pairs[1::2]):
                    sp.dma_start(to, a).then_inc(loaded, 16)
                sp.wait_ge(loaded, 16 * (len(pairs) // 2))


def conv_nodes(nc, G, tag, W, bias, table, acc, relu_of=None):
    with ExitStack() as ctx:
        L = Kit(nc, ctx, tag)
        nrm = Norm(L, G, relu_of=relu_of)
        w = L.sb("w", [P, 2, D])
        b = L.sb("b", [P, D])
        y = [L.ps(f"y{s}", [P, D]) for s in range(2)]
        loaded = L.sem("loaded")
        stored = L.sem("stored")
        M = L.steps("pe_loop", "mm0 mm1 mm2 mm3 mm4")
        V = L.steps("dve_loop", "b0 b1 b2 b3 b4")
        with nc.Block() as block:
            @block.sync
            def _(sp):
                L.open(sp)
                sp.dma_start(w[:], W.rearrange("(k p) n -> p k n", p=P)).then_inc(loaded, 16)
                sp.dma_start(b[:], spread(bias, D)).then_inc(loaded, 16)
                with sp.Fori(0, NG) as i:
                    sp.wait_ge(*nrm.V.at(nrm.last, i))
                    sp.dma_start(rows_of(table, i), nrm.xn[:]).then_inc(stored, 16)
                sp.wait_ge(stored, 16 * NG)

            @block.vector
            def _(dve):
                dve.wait_ge(loaded, 32)
                with dve.Fori(0, NG) as i:
                    nrm.dve(dve, i, [(stored, i * 16)])
                    for u in range(GT):
                        dve.wait_ge(*M.at(f"mm{u}", i))
                        dve.tensor_tensor(acc[:, bass.ds(i * GT + u, 1), :].rearrange("p a d -> p (a d)"), y[u % 2],
                                          b[:], ALU.add).then_inc(*V.step(f"b{u}"))

            @block.scalar
            def _(act):
                with act.Fori(0, NG) as i:
                    nrm.act(act, i, M.ended(i))

            @block.tensor
            def _(pe):
                pe.wait_ge(loaded, 32)
                with pe.Fori(0, NG) as i:
                    nrm.pe(pe, i)
                    for u in range(GT):
                        pe.wait_ge(*nrm.C.at(f"cp{u}", i))
                        pe.wait_ge(*(V.at(f"b{u - 2}", i) if u >= 2 else V.ended(i)))
                        for k in range(2):
                            ins = pe.matmul(y[u % 2], nrm.xT[:, k, u * P:(u + 1) * P], w[:, k, :],
                                            start=(k == 0), stop=(k == 1))
                        ins.then_inc(*M.step(f"mm{u}"))


def conv_pass(nc, G, tag, X, table, types, weight, W, acc):
    R, B2 = 16, 512
    KP = 96
    with ExitStack() as ctx:
        L = Kit(nc, ctx, tag)
        wf = L.sb("wf", [KP, B2])
        rest = L.sb("rest", [KP, B2])
        parts = L.sb("parts", [KP, B2], BF16)
        kind = L.sb("kind", [P, KP])
        kind_i = L.sb("kind_i", [P, KP], I32)
        row = L.sb("row", [P, IT, D])
        at = L.sb("at", [P, 2, U], I32)
        oh = L.sb("oh", [P, 2, U, P])
        et = L.sb("et", [P, 2, U, KP], BF16)
        etT = L.sb("etT", [KP, 2, U * P], BF16)
        prod = L.sb("prod", [P, 2, U, B2])
        turn = L.ps("turn", [KP, U, P], BF16)
        wide = [L.ps(f"wide{u}", [P, B2]) for u in range(U)]
        sums = [L.ps(f"sums{q}", [P, 2, D]) for q in range(2)]
        got, before = L.row_sems(X.chunks // IT)
        took, loaded, chain = L.sem("took"), L.sem("loaded"), L.sem("chain")
        V = L.steps("dve_conv", "oh0 et0 oh1 et1 " + " ".join(f"prod{u}" for u in range(IT)) + " " +
                    " ".join(f"acc{u}" for u in range(IT)))
        A = L.steps("act_conv", "at0 at1 T0 T1")
        M = L.steps("pe_conv", "tr0 " + " ".join(f"w{u}" for u in range(U)) + " tr1 " +
                    " ".join(f"w{u}" for u in range(U, IT)) + " " + " ".join(f"sum{u}" for u in range(IT)))
        n = X.chunks // IT
        with nc.Block() as block:
            @block.sync
            def _(sp):
                L.open(sp)
                sp.wait_ge(chain, 2)
                for q in range(3):
                    sp.dma_start(wf[32 * q:32 * q + R, :], W.rearrange("r b i o -> r (b i o)")).then_inc(loaded, 16)

            @block.gpsimd
            def _(pool):
                with pool.Fori(0, n) as i:
                    for h in range(2):
                        pool.wait_ge(*A.at(f"at{h}", i))
                        pool.sem_inc(took, 1)
                        for u in range(U):
                            pool.indirect_dma_start(
                                out=row[:, h * U + u, :], out_offset=None, in_=table,
                                in_offset=bass.IndirectOffsetOnAxis(ap=at[:, h, u:u + 1], axis=0)
                            ).then_inc(got[h * U + u], 16)

            @block.scalar
            def _(act):
                with act.Fori(0, n) as i:
                    for h in range(2):
                        act.wait_ge(*V.at(f"prod{h * U + U - 1}", i - 1))
                        act.copy(at[:, h, :], X.src[:, bass.ds(i * IT + h * U, U)]).then_inc(*A.step(f"at{h}"))
                    for h in range(2):
                        act.wait_ge(*M.at(f"tr{h}", i))
                        act.wait_ge(*M.at(f"w{h * U + U - 1}", i - 1))
                        act.copy(etT[:, h, :], turn.rearrange("p u e -> p (u e)")).then_inc(*A.step(f"T{h}"))

            @block.vector
            def _(dve):
                link = chained(dve, chain)
                link(dve.memset(wf[:], 0.0))
                link(dve.memset(parts[:], 0.0))
                link(dve.tensor_copy(kind_i[:], G.iota[:, 0:KP]))
                link(dve.tensor_scalar(kind_i[:], kind_i[:], 31, None, ALU.bitwise_and))
                link(dve.tensor_copy(kind[:], kind_i[:]))
                dve.wait_ge(loaded, 48)
                link(dve.tensor_copy(parts[:], wf[:]))
                link(dve.tensor_tensor(rest[:], wf[:], parts[:], ALU.subtract))
                link(dve.tensor_copy(parts[32:64, :], rest[32:64, :]))
                link(dve.tensor_copy(parts[64:KP, :], rest[64:KP, :]))
                link(dve.tensor_tensor(rest[64:KP, :], rest[64:KP, :], parts[64:KP, :], ALU.subtract))
                link(dve.tensor_copy(parts[64:KP, :], rest[64:KP, :]))
                with dve.Fori(0, n) as i:
                    for h in range(2):
                        c = i * IT + h * U
                        dve.wait_ge(*M.at(f"sum{h * U + U - 1}", i - 1))
                        for u in range(U):
                            ins = dve.tensor_scalar(oh[:, h, u, :], G.iota[:], X.local[:, bass.ds(c + u, 1)],
                                                    weight[:, bass.ds(c + u, 1)], ALU.is_equal, ALU.mult)
                        ins.then_inc(*V.step(f"oh{h}"))
                        dve.tensor_tensor(et[:, h], kind[:].unsqueeze(1).broadcast_to([P, U, KP]),
                                          types[:, bass.ds(c, U)].unsqueeze(2).broadcast_to([P, U, KP]),
                                          ALU.is_equal).then_inc(*V.step(f"et{h}"))
                    for u in range(IT):
                        h = u // U
                        dve.wait_ge(got[u], i * 16 + (16 + before))
                        dve.wait_ge(*M.at(f"w{u}", i))
                        dve.tensor_tensor(prod[:, h, u % U, :].rearrange("p (c o) -> p c o", o=2),
                                          wide[u % U].rearrange("p (c o) -> p c o", o=2),
                                          row[:, u, :].unsqueeze(2).broadcast_to([P, D, 2]), ALU.mult
                                          ).then_inc(*V.step(f"prod{u}"))
                    for u in range(IT):
                        t = dve.value_load(X.tile[0:1, bass.ds(i * IT + u, 1)], min_val=0, max_val=NT - 1)
                        a = acc[:, bass.ds(t, 1), :].rearrange("p a w -> p (a w)")
                        dve.wait_ge(*M.at(f"sum{u | 1}", i))
                        dve.wait_ge(*(V.at(f"acc{u - 1}", i) if u else V.at(f"acc{IT - 1}", i - 1)))
                        dve.tensor_tensor(a, a, sums[u % U // 2][:, u % 2, :], ALU.add).then_inc(*V.step(f"acc{u}"))

            @block.tensor
            def _(pe):
                pe.wait_ge(chain, 11)
                with pe.Fori(0, n) as i:
                    for h in range(2):
                        pe.wait_ge(*V.at(f"et{h}", i))
                        pe.wait_ge(*(A.at("T0", i) if h else A.at("T1", i - 1)))
                        for u in range(U):
                            ins = pe.transpose(turn[:, u, :], et[:, h, u, :], G.identb[:])
                        ins.then_inc(*M.step(f"tr{h}"))
                        pe.wait_ge(*A.at(f"T{h}", i))
                        for u in range(U):
                            pe.wait_ge(*(V.at(f"prod{u}", i) if h else V.at(f"prod{U + u}", i - 1)))
                            pe.matmul(wide[u], etT[:, h, u * P:(u + 1) * P], parts[:], start=True,
                                      stop=True).then_inc(*M.step(f"w{h * U + u}"))
                    for u in range(IT):
                        h = u // U
                        pe.wait_ge(*V.at(f"prod{u}", i))
                        pe.wait_ge(*(V.at(f"acc{(u | 1) - U}", i) if h else V.at(f"acc{(u | 1) + U}", i - 1)))
                        p4 = prod[:, h, u % U, :].rearrange("p (b i o) -> p i b o", i=2, o=2)
                        for q in range(2):
                            ins = pe.matmul(sums[u % U // 2][:, u % 2, :].rearrange("p (b o) -> p b o", o=2),
                                            oh[:, h, u % U, :], p4[:, q], start=(q == 0), stop=(q == 1))
                        ins.then_inc(*M.step(f"sum{u}"))


def scores_of(nc, G, tag, W, n, bias, gates, affine_of=None, soft=False):
    with ExitStack() as ctx:
        L = Kit(nc, ctx, tag)
        score = L.sb("score", [P, NT, n])
        with ExitStack() as inner:
            L1 = Kit(nc, inner, tag + "n")
            affine = (L1.sb("gamma", [P, D]), L1.sb("beta", [P, D])) if affine_of else None
            nrm = Norm(L1, G, affine)
            w = L1.sb("w", [P, 2, n])
            b = L1.sb("b", [P, n])
            y = [L1.ps(f"y{s}", [P, n]) for s in range(2)]
            loaded = L1.sem("loaded")
            M = L1.steps("pe_score", "mm0 mm1 mm2 mm3 mm4")
            V = L1.steps("dve_score", "b0 b1 b2 b3 b4")
            loads = 16 * (4 if affine_of else 2)
            with nc.Block() as block:
                @block.sync
                def _(sp):
                    L1.open(sp)
                    with nc.allow_non_contiguous_dma(reason="a small weight"):
                        sp.dma_start(w[:], W.rearrange("(k p) n -> p k n", p=P)).then_inc(loaded, 16)
                    sp.dma_start(b[:], spread(bias, n)).then_inc(loaded, 16)
                    if affine_of:
                        sp.dma_start(affine[0][:], spread(affine_of[0], D)).then_inc(loaded, 16)
                        sp.dma_start(affine[1][:], spread(affine_of[1], D)).then_inc(loaded, 16)

                @block.vector
                def _(dve):
                    dve.wait_ge(loaded, loads)
                    with dve.Fori(0, NG) as i:
                        nrm.dve(dve, i)
                        for u in range(GT):
                            dve.wait_ge(*M.at(f"mm{u}", i))
                            dve.tensor_tensor(score[:, bass.ds(i * GT + u, 1), :].rearrange("p a d -> p (a d)"),
                                              y[u % 2], b[:], ALU.add).then_inc(*V.step(f"b{u}"))

                @block.scalar
                def _(act):
                    with act.Fori(0, NG) as i:
                        nrm.act(act, i, M.ended(i))

                @block.tensor
                def _(pe):
                    pe.wait_ge(loaded, loads)
                    with pe.Fori(0, NG) as i:
                        nrm.pe(pe, i)
                        for u in range(GT):
                            pe.wait_ge(*nrm.C.at(f"cp{u}", i))
                            pe.wait_ge(*(V.at(f"b{u - 2}", i) if u >= 2 else V.ended(i)))
                            for k in range(2):
                                ins = pe.matmul(y[u % 2], nrm.xT[:, k, u * P:(u + 1) * P], w[:, k, :],
                                                start=(k == 0), stop=(k == 1))
                            ins.then_inc(*M.step(f"mm{u}"))
        top = L.sb("top", [P, NT])
        chain, ask, done = L.sem("chain"), L.sem("ask"), L.sem("done")
        second = {}
        with nc.Block() as block:
            @block.vector
            def _(dve):
                link = chained(dve, chain)
                if soft:
                    link(dve.tensor_reduce(top[:], score[:], AX.X, ALU.max))
                    link(dve.tensor_tensor(score[:], score[:], top[:].unsqueeze(2).broadcast_to([P, NT, n]),
                                           ALU.subtract))
                    dve.sem_inc(ask, 1)
                    dve.wait_ge(done, 1)
                    link(dve.tensor_reduce(top[:], score[:], AX.X, ALU.add))
                    link(dve.reciprocal(top[:], top[:]))
                    link(dve.tensor_tensor(score[:], score[:], top[:].unsqueeze(2).broadcast_to([P, NT, n]), ALU.mult))
                second["ap"], after = top2(L, G, dve, link, score[:], gates[:, :, 0:n], n)
                dve.sem_inc(ask, 1)
                dve.wait_ge(done, 2 if soft else 1)
                after()

            @block.scalar
            def _(act):
                if soft:
                    act.wait_ge(ask, 1)
                    act.activation(score[:], score[:], ACT.Exp).then_inc(done, 1)
                act.wait_ge(ask, 2 if soft else 1)
                act.activation(second["ap"], second["ap"], ACT.Exp).then_inc(done, 1)


def add_to_x(nc, G, tag, t):
    with ExitStack() as ctx:
        L = Kit(nc, ctx, tag)
        done = L.sem("done")
        with nc.Block() as block:
            @block.vector
            def _(dve):
                dve.tensor_tensor(G.x[:], G.x[:], t, ALU.add).then_inc(done, 1)


def edge_attention_pass(nc, G, tag, X, al_dram, hh, edges, ew, alpha):
    H = 8
    with ExitStack() as ctx:
        L = Kit(nc, ctx, tag)
        row = L.sb("row", [P, IT, H])
        at = L.sb("at", [P, 2, U], I32)
        oh = L.sb("oh", [P, 2, U, P])
        ohT = L.sb("ohT", [P, 2, U * P])
        ea = L.sb("ea", [P, 2, U, 4])
        eaT = L.sb("eaT", [4, 2, U * P])
        enc = L.sb("enc", [P, 2, U, D])
        prod = L.sb("prod", [P, U, D])
        s = L.sb("s", [P, U, H])
        dot = L.sb("dot", [P, U, H])
        turn = L.ps("turn", [P, U, P])
        eturn = L.ps("eturn", [4, U, P])
        encp = [L.ps(f"encp{q}", [P, 2, D]) for q in range(2)]
        atdst = L.ps("atdst", [P, U, 512])
        got, before = L.row_sems(X.chunks // IT)
        took = L.sem("took")
        V = L.steps("dve_alpha", "oh0 oh1 " + " ".join(f"prod{h} dot{h} sum{h} add{h} alpha{h}" for h in range(2)))
        A = L.steps("act_alpha", "at0 at1 ea0 ea1 " + " ".join(f"T{h} ET{h} r{h}_0 r{h}_1" for h in range(2)))
        M = L.steps("pe_alpha", " ".join(f"tr{h} te{h} enc{h}_0 enc{h}_1 dst{h}" for h in range(2)))
        n = X.chunks // IT
        with nc.Block() as block:
            @block.sync
            def _(sp):
                L.open(sp)

            @block.gpsimd
            def _(pool):
                with pool.Fori(0, n) as i:
                    for h in range(2):
                        pool.wait_ge(*A.at(f"at{h}", i))
                        pool.sem_inc(took, 1)
                        for u in range(U):
                            pool.indirect_dma_start(
                                out=row[:, h * U + u, :], out_offset=None, in_=al_dram,
                                in_offset=bass.IndirectOffsetOnAxis(ap=at[:, h, u:u + 1], axis=0)
                            ).then_inc(got[h * U + u], 16)

            @block.scalar
            def _(act):
                with act.Fori(0, n) as i:
                    for h in range(2):
                        act.wait_ge(*V.at(f"sum{h}", i - 1))
                        act.copy(at[:, h, :], X.src[:, bass.ds(i * IT + h * U, U)]).then_inc(*A.step(f"at{h}"))
                    for h in range(2):
                        act.wait_ge(*M.at(f"te{h}", i - 1))
                        act.copy(ea[:, h], edges[:, bass.ds(i * IT + h * U, U), :]).then_inc(*A.step(f"ea{h}"))
                    for h in range(2):
                        act.wait_ge(*M.at(f"tr{h}", i))
                        act.wait_ge(*M.at(f"dst{h}", i - 1))
                        act.copy(ohT[:, h, :], turn.rearrange("p u e -> p (u e)")).then_inc(*A.step(f"T{h}"))
                        act.wait_ge(*M.at(f"te{h}", i))
                        act.wait_ge(*M.at(f"enc{h}_1", i - 1))
                        act.copy(eaT[:, h, :], eturn.rearrange("p u e -> p (u e)")).then_inc(*A.step(f"ET{h}"))
                        for q in range(2):
                            act.wait_ge(*M.at(f"enc{h}_{q}", i))
                            act.wait_ge(*V.at(f"prod{h}", i - 1))
                            act.activation(enc[:, h, 2 * q:2 * q + 2, :], encp[q], ACT.Relu).then_inc(*A.step(f"r{h}_{q}"))

            @block.vector
            def _(dve):
                with dve.Fori(0, n) as i:
                    for h in range(2):
                        dve.wait_ge(*M.at(f"tr{h}", i - 1))
                        one_hots(dve, G, X, oh[:, h], i * IT + h * U).then_inc(*V.step(f"oh{h}"))
                    for h in range(2):
                        c = i * IT + h * U
                        dve.wait_ge(*A.at(f"r{h}_1", i))
                        dve.wait_ge(*M.at(f"dst{h}", i))
                        dve.wait_ge(*(V.at("dot0", i) if h else V.at("dot1", i - 1)))
                        dve.tensor_tensor(prod[:], enc[:, h], atdst[:, :, 0:D], ALU.mult).then_inc(*V.step(f"prod{h}"))
                        dve.wait_ge(*V.at(f"prod{h}", i))
                        dve.tensor_reduce(dot[:], prod[:].rearrange("p u (h c) -> p u h c", h=H), AX.X,
                                          ALU.add).then_inc(*V.step(f"dot{h}"))
                        for u in range(U):
                            dve.wait_ge(got[h * U + u], i * 16 + (16 + before))
                        dve.wait_ge(*(V.at("alpha0", i) if h else V.at("alpha1", i - 1)))
                        dve.tensor_tensor(s[:], row[:, h * U:(h + 1) * U, :], atdst[:, :, D:D + H],
                                          ALU.add).then_inc(*V.step(f"sum{h}"))
                        dve.wait_ge(*V.at(f"sum{h}", i))
                        dve.tensor_tensor(s[:], s[:], dot[:], ALU.add).then_inc(*V.step(f"add{h}"))
                        dve.wait_ge(*V.at(f"add{h}", i))
                        flat = s[:].rearrange("p u h -> p (u h)")
                        dve.scalar_tensor_tensor(alpha[:, bass.ds(c, U), :].rearrange("p u h -> p (u h)"), flat, 0.2,
                                                 flat, ALU.mult, ALU.max).then_inc(*V.step(f"alpha{h}"))

            @block.tensor
            def _(pe):
                with pe.Fori(0, n) as i:
                    for h in range(2):
                        pe.wait_ge(*V.at(f"oh{h}", i))
                        pe.wait_ge(*(A.at("T0", i) if h else A.at("T1", i - 1)))
                        for u in range(U):
                            ins = pe.transpose(turn[:, u, :], oh[:, h, u, :], G.ident[:])
                        ins.then_inc(*M.step(f"tr{h}"))
                        pe.wait_ge(*A.at(f"ea{h}", i))
                        pe.wait_ge(*(A.at("ET0", i) if h else A.at("ET1", i - 1)))
                        for u in range(U):
                            ins = pe.transpose(eturn[:, u, :], ea[:, h, u, :], G.ident[:])
                        ins.then_inc(*M.step(f"te{h}"))
                        pe.wait_ge(*A.at(f"ET{h}", i))
                        for q in range(2):
                            pe.wait_ge(*(A.at(f"r0_{q}", i) if h else A.at(f"r1_{q}", i - 1)))
                            for u in range(2 * q, 2 * q + 2):
                                ins = pe.matmul(encp[q][:, u % 2, :], eaT[:, h, u * P:(u + 1) * P], ew[:],
                                                start=True, stop=True)
                            ins.then_inc(*M.step(f"enc{h}_{q}"))
                        pe.wait_ge(*(V.at("sum0", i) if h else V.at("sum1", i - 1)))
                        for u in range(U):
                            t = pe.value_load(X.tile[0:1, bass.ds(i * IT + h * U + u, 1)], min_val=0, max_val=NT - 1)
                            ins = pe.matmul(atdst[:, u, 0:D + H], ohT[:, h, u * P:(u + 1) * P],
                                            hh[:, bass.ds(t, 1), :].rearrange("p a h -> p (a h)"), start=True, stop=True)
                        ins.then_inc(*M.step(f"dst{h}"))


def finish_l2_gnn(nc, G, acc, bias):
    H, C = 8, 32
    with ExitStack() as ctx:
        L = Kit(nc, ctx, "f2")
        den = L.sb("den", [P, NT, H])
        b = L.sb("b", [P, D])
        loaded, ready = L.sem("loaded"), L.sem("ready")
        V = L.steps("dve_out", "z x1 x2")
        with nc.Block() as block:
            @block.sync
            def _(sp):
                L.open(sp)
                sp.dma_start(b[:], spread(bias, D)).then_inc(loaded, 16)

            @block.vector
            def _(dve):
                link = chained(dve, ready)
                link(dve.tensor_scalar(den[:], acc[:, :, D:D + H], 1e-10, None, ALU.max))
                link(dve.reciprocal(den[:], den[:]))
                dve.wait_ge(loaded, 16)
                with dve.Fori(0, NG) as i:
                    z = acc[:, bass.ds(i * GT, GT), 0:D]
                    zh = z.rearrange("p t (h c) -> p t h c", h=H)
                    xg = G.x[:, bass.ds(i * GT, GT), :]
                    dve.tensor_tensor(zh, zh, den[:, bass.ds(i * GT, GT), :].unsqueeze(3).broadcast_to([P, GT, H, C]),
                                      ALU.mult).then_inc(*V.step("z"))
                    dve.tensor_tensor(xg, xg, b[:].unsqueeze(1).broadcast_to([P, GT, D]), ALU.add).then_inc(*V.step("x1"))
                    dve.wait_ge(*V.at("x1", i))
                    dve.tensor_tensor(xg, xg, z, ALU.add).then_inc(*V.step("x2"))


def relu_experts(nc, G, I, gates):
    n, HALF = 4, GT * P // 2
    S1, S2, E1, E2 = 256, 128, 128, 64
    C1 = S1 // P + n
    with ExitStack() as ctx:
        L = Kit(nc, ctx, "x2")
        nrm = Norm(L, G)
        w1 = L.sb("w1", [P, 2, C1 * P])
        b1 = L.sb("b1", [P, C1])
        w2s = L.sb("w2s", [P, 2, S2])
        w2e = L.sb("w2e", [P, n, E2])
        b2s = L.sb("b2s", [P, 1])
        b2e = L.sb("b2e", [E2, n])
        w3s = L.sb("w3s", [P, D])
        w3e = L.sb("w3e", [E2, n, D])
        h1 = L.sb("h1", [P, C1, GT * P])
        h2s = L.sb("h2s", [P, GT * P])
        h2e = L.sb("h2e", [E2, n, GT * P])
        hp = [[L.ps(f"hp{s}{f}", [P, HALF]) for f in range(2)] for s in range(2)]
        y = [L.ps(f"y{s}", [P, D]) for s in range(2)]
        loaded = L.sem("loaded")
        JOBS = C1 + 1 + n
        M = L.steps("pe_mlp", " ".join(f"j{j}" for j in range(JOBS)) + " " +
                    " ".join(f"y{e}_{u}" for e in range(n + 1) for u in range(GT)))
        A = L.steps("act_relu", " ".join(f"j{j}" for j in range(JOBS)))
        V = L.steps("dve_sum", " ".join(f"x{e}_{u}" for e in range(n + 1) for u in range(GT)))
        with nc.Block() as block:
            @block.sync
            def _(sp):
                L.open(sp)
                with nc.allow_non_contiguous_dma(reason="biases, hidden units to partitions"):
                    for to, a in (
                            (w1[:, :, 0:S1], I["L2_ffn_sW1"].rearrange("(k p) n -> p k n", p=P)),
                            (b1[:, 0:2], I["L2_ffn_sb1"].rearrange("(c p) -> p c", p=P)),
                            (b1[:, 2:C1], I["L2_ffn_eb1"].rearrange("e p -> p e")),
                            (w2s[:], I["L2_ffn_sW2"].rearrange("(k p) n -> p k n", p=P)),
                            (w2e[:], I["L2_ffn_eW2"].rearrange("e p n -> p e n")),
                            (b2s[:], I["L2_ffn_sb2"].rearrange("(p o) -> p o", o=1)),
                            (b2e[:], I["L2_ffn_eb2"].rearrange("e p -> p e")),
                            (w3s[:], I["L2_ffn_sW3"]),
                            (w3e[:], I["L2_ffn_eW3"].rearrange("e p n -> p e n"))):
                        sp.dma_start(to, a).then_inc(loaded, 16)
                    for e in range(n):
                        sp.dma_start(w1[:, :, S1 + e * E1:S1 + (e + 1) * E1],
                                     I["L2_ffn_eW1"][e].rearrange("(k p) n -> p k n", p=P)).then_inc(loaded, 16)

            @block.vector
            def _(dve):
                dve.wait_ge(loaded, 16 * 13)
                with dve.Fori(0, NG) as i:
                    nrm.dve(dve, i)
                    for e in range(n + 1):
                        for u in range(GT):
                            dve.wait_ge(*M.at(f"y{e}_{u}", i))
                            if e:
                                dve.wait_ge(*V.at(f"x{e - 1}_{u}", i))
                            xt = G.x[:, bass.ds(i * GT + u, 1), :].rearrange("p a d -> p (a d)")
                            q = (e * GT + u) % 2
                            if e == 0:
                                dve.tensor_tensor(xt, xt, y[q], ALU.add).then_inc(*V.step(f"x{e}_{u}"))
                            else:
                                g = gates[:, bass.ds(i * GT + u, 1), e - 1:e].rearrange("p a e -> p (a e)")
                                dve.scalar_tensor_tensor(xt, y[q], g, xt, ALU.mult, ALU.add).then_inc(*V.step(f"x{e}_{u}"))

            @block.scalar
            def _(act):
                act.wait_ge(loaded, 16 * 13)
                with act.Fori(0, NG) as i:
                    nrm.act(act, i, M.ended(i))
                    for j in range(JOBS):
                        act.wait_ge(*M.at(f"j{j}", i))
                        for f in range(2):
                            c = slice(f * HALF, (f + 1) * HALF)
                            if j < C1:
                                to, b, rows = h1[:, j, c], b1[:, j:j + 1], P
                            elif j == C1:
                                to, b, rows = h2s[:, c], b2s[:, 0:1], P
                            else:
                                e = j - C1 - 1
                                to, b, rows = h2e[:, e, c], b2e[:, e:e + 1], E2
                            ins = act.activation(to, hp[j % 2][f][0:rows, :], ACT.Relu, bias=b)
                        ins.then_inc(*A.step(f"j{j}"))

            @block.tensor
            def _(pe):
                pe.wait_ge(loaded, 16 * 13)
                with pe.Fori(0, NG) as i:
                    nrm.pe(pe, i)
                    pe.wait_ge(*nrm.C.at(f"cp{GT - 1}", i))
                    for j in range(JOBS):
                        pe.wait_ge(*(A.at(f"j{j - 2}", i) if j >= 2 else A.ended(i)))
                        e = j - C1 - 1
                        if j == C1:
                            pe.wait_ge(*A.at("j1", i))
                        elif j > C1:
                            pe.wait_ge(*A.at(f"j{2 + e}", i))
                        for f in range(2):
                            c = slice(f * HALF, (f + 1) * HALF)
                            if j < C1:
                                for k in range(2):
                                    ins = pe.matmul(hp[j % 2][f], w1[:, k, j * P:(j + 1) * P], nrm.xT[:, k, c],
                                                    start=(k == 0), stop=(k == 1))
                            elif j == C1:
                                for k in range(2):
                                    ins = pe.matmul(hp[j % 2][f], w2s[:, k, :], h1[:, k, c],
                                                    start=(k == 0), stop=(k == 1))
                            else:
                                ins = pe.matmul(hp[j % 2][f][0:E2, :], w2e[:, e, :], h1[:, 2 + e, c],
                                                start=True, stop=True)
                        ins.then_inc(*M.step(f"j{j}"))
                    for e in range(n + 1):
                        pe.wait_ge(*A.at(f"j{C1 + e}", i))
                        for u in range(GT):
                            q = e * GT + u
                            pe.wait_ge(*(V.at(f"x{(q - 2) // GT}_{(q - 2) % GT}", i) if q >= 2 else V.ended(i)))
                            c = slice(u * P, (u + 1) * P)
                            if e == 0:
                                ins = pe.matmul(y[q % 2], h2s[:, c], w3s[:], start=True, stop=True)
                            else:
                                ins = pe.matmul(y[q % 2], h2e[:, e - 1, c], w3e[:, e - 1, :], start=True, stop=True)
                            ins.then_inc(*M.step(f"y{e}_{u}"))


HID = 1024


def counted_nodes(nc, G, table):
    with ExitStack() as ctx:
        L = Kit(nc, ctx, "cn")
        nrm = Norm(L, G)
        rows = L.sb("rows", [P, GT, D + 1])
        ones_set, stored = L.sem("ones_set"), L.sem("stored")
        V = L.steps("dve_rows", "rows")
        with nc.Block() as block:
            @block.sync
            def _(sp):
                L.open(sp)
                with sp.Fori(0, NG) as i:
                    sp.wait_ge(*V.at("rows", i))
                    sp.dma_start(rows_of(table, i), rows[:]).then_inc(stored, 16)
                sp.wait_ge(stored, 16 * NG)

            @block.vector
            def _(dve):
                dve.memset(rows[:], 1.0).then_inc(ones_set, 1)
                dve.wait_ge(ones_set, 1)
                with dve.Fori(0, NG) as i:
                    nrm.dve(dve, i)
                    dve.wait_ge(*nrm.V.at("norm", i))
                    dve.wait_ge(stored, i * 16)
                    dve.tensor_copy(rows[:, :, 0:D], nrm.xn[:]).then_inc(*V.step("rows"))

            @block.scalar
            def _(act):
                with act.Fori(0, NG) as i:
                    nrm.act(act, i, nrm.C.ended(i))

            @block.tensor
            def _(pe):
                with pe.Fori(0, NG) as i:
                    nrm.pe(pe, i)


def gine_pass(nc, G, I, tag, X, table, g_rows, acc):
    K1, W = EF + 1, D + 1
    with ExitStack() as ctx:
        L = Kit(nc, ctx, tag)
        w1 = L.sb("w1", [K1, D])
        row = L.sb("row", [P, IT, W])
        at = L.sb("at", [P, 2, U], I32)
        ea = L.sb("ea", [P, 2, U, K1])
        eaT = L.sb("eaT", [K1, 2, U * P])
        enc = L.sb("enc", [P, 2, U, W])
        oh = L.sb("oh", [P, 2, U, P])
        eturn = L.ps("eturn", [K1, U, P])
        encp = [L.ps(f"encp{q}", [P, 2, D]) for q in range(2)]
        sums = [L.ps(f"sums{q}", [P, 2, 512]) for q in range(2)]
        got, before = L.row_sems(X.chunks // IT)
        took, loaded, ones_set = L.sem("took"), L.sem("loaded"), L.sem("ones_set")
        attrs = [L.sem(f"attrs{h}_") for h in range(2)]
        V = L.steps("dve_gine", "oh0 oh1 " + " ".join(f"acc{u}" for u in range(IT)))
        A = L.steps("act_gine", "at0 at1 " + " ".join(f"ET{h} r{h}_0 r{h}_1" for h in range(2)))
        M = L.steps("pe_gine", " ".join(f"te{h} enc{h}_0 enc{h}_1" for h in range(2)) + " " +
                    " ".join(f"sum{u}" for u in range(IT)))
        n = X.chunks // IT
        attr_rows = g_rows.rearrange("(p c) w -> p c w", c=X.chunks)
        with nc.Block() as block:
            @block.sync
            def _(sp):
                L.open(sp)
                sp.dma_start(w1[0:1, :], I["L3_gnn_ee_b1"].rearrange("(o n) -> o n", o=1)).then_inc(loaded, 16)
                sp.dma_start(w1[1:K1, :], I["L3_gnn_ee_w1"]).then_inc(loaded, 16)
                with sp.Fori(0, n) as i:
                    for h in range(2):
                        sp.wait_ge(*M.at(f"te{h}", i - 1))
                        sp.dma_start(ea[:, h], attr_rows[:, bass.ds(i * IT + h * U, U), R_ONE:REC]).then_inc(attrs[h], 16)

            @block.gpsimd
            def _(pool):
                with pool.Fori(0, n) as i:
                    for h in range(2):
                        pool.wait_ge(*A.at(f"at{h}", i))
                        pool.sem_inc(took, 1)
                        for u in range(U):
                            pool.indirect_dma_start(
                                out=row[:, h * U + u, :], out_offset=None, in_=table,
                                in_offset=bass.IndirectOffsetOnAxis(ap=at[:, h, u:u + 1], axis=0)
                            ).then_inc(got[h * U + u], 16)

            @block.scalar
            def _(act):
                act.wait_ge(ones_set, 1)
                with act.Fori(0, n) as i:
                    for h in range(2):
                        act.wait_ge(*M.at(f"sum{h * U + U - 1}", i - 1))
                        act.copy(at[:, h, :], X.src[:, bass.ds(i * IT + h * U, U)]).then_inc(*A.step(f"at{h}"))
                    for h in range(2):
                        act.wait_ge(*M.at(f"te{h}", i))
                        act.wait_ge(*M.at(f"enc{h}_1", i - 1))
                        act.copy(eaT[:, h, :], eturn.rearrange("p u e -> p (u e)")).then_inc(*A.step(f"ET{h}"))
                        for q in range(2):
                            act.wait_ge(*M.at(f"enc{h}_{q}", i))
                            act.wait_ge(*M.at(f"sum{h * U + 2 * q + 1}", i - 1))
                            act.activation(enc[:, h, 2 * q:2 * q + 2, 0:D], encp[q], ACT.Relu).then_inc(*A.step(f"r{h}_{q}"))

            @block.vector
            def _(dve):
                dve.memset(enc[:], 1.0).then_inc(ones_set, 1)
                with dve.Fori(0, n) as i:
                    for h in range(2):
                        dve.wait_ge(*M.at(f"sum{h * U + U - 1}", i - 1))
                        one_hots(dve, G, X, oh[:, h], i * IT + h * U).then_inc(*V.step(f"oh{h}"))
                    for u in range(IT):
                        t = dve.value_load(X.tile[0:1, bass.ds(i * IT + u, 1)], min_val=0, max_val=NT - 1)
                        a = acc[:, bass.ds(t, 1), :, :].rearrange("p a q w -> p (a q) w")
                        dve.wait_ge(*M.at(f"sum{u}", i))
                        dve.wait_ge(*(V.at(f"acc{u - 1}", i) if u else V.at(f"acc{IT - 1}", i - 1)))
                        dve.tensor_tensor(a, a, sums[u % 2][:, :, 0:W], ALU.add).then_inc(*V.step(f"acc{u}"))

            @block.tensor
            def _(pe):
                pe.wait_ge(loaded, 32)
                pe.wait_ge(ones_set, 1)
                with pe.Fori(0, n) as i:
                    for h in range(2):
                        pe.wait_ge(attrs[h], i * 16 + 16)
                        pe.wait_ge(*(A.at("ET0", i) if h else A.at("ET1", i - 1)))
                        for u in range(U):
                            ins = pe.transpose(eturn[:, u, :], ea[:, h, u, :], G.ident[:])
                        ins.then_inc(*M.step(f"te{h}"))
                        pe.wait_ge(*A.at(f"ET{h}", i))
                        for q in range(2):
                            pe.wait_ge(*(A.at(f"r0_{q}", i) if h else A.at(f"r1_{q}", i - 1)))
                            for u in range(2 * q, 2 * q + 2):
                                ins = pe.matmul(encp[q][:, u % 2, :], eaT[:, h, u * P:(u + 1) * P], w1[:],
                                                start=True, stop=True)
                            ins.then_inc(*M.step(f"enc{h}_{q}"))
                    for u in range(IT):
                        h = u // U
                        pe.wait_ge(*V.at(f"oh{h}", i))
                        pe.wait_ge(got[u], i * 16 + (16 + before))
                        pe.wait_ge(*A.at(f"r{h}_{u % U // 2}", i))
                        pe.wait_ge(*(V.at(f"acc{u - 2}", i) if u >= 2 else V.at(f"acc{IT - 2 + u}", i - 1)))
                        pe.matmul(sums[u % 2][:, 0, 0:W], oh[:, h, u % U, :], row[:, u, :], start=True, stop=True)
                        pe.matmul(sums[u % 2][:, 1, 0:W], oh[:, h, u % U, :], enc[:, h, u % U, :], start=True,
                                  stop=True).then_inc(*M.step(f"sum{u}"))


def gine_nodes(nc, G, I, table, acc, h0):
    with ExitStack() as ctx:
        L = Kit(nc, ctx, "gn")
        w2 = L.sb("w2", [P, 2, D])
        self1 = L.sb("self1", [P, D])
        b2 = L.sb("b2", [P, D])
        eps2 = L.sb("eps2", [P, 1])
        cnt = L.sb("cnt", [P, NT])
        xn = L.sb("xn", [P, GT, D])
        e = L.sb("e", [P, GT, D])
        eT = L.sb("eT", [P, GT, 2, P])
        h = L.sb("h", [P, GT, D])
        tr = [L.ps(f"tr{s}", [P, 2, P]) for s in range(2)]
        y = [L.ps(f"y{s}", [P, D]) for s in range(2)]
        loaded, ready, rows_in = L.sem("loaded"), L.sem("ready"), L.sem("rows_in")
        V = L.steps("dve_h", "e h " + " ".join(f"c{u} x{u}" for u in range(GT)))
        A = L.steps("act_h", " ".join(f"cp{u}" for u in range(GT)))
        M = L.steps("pe_h", " ".join(f"tr{u}" for u in range(GT)) + " " + " ".join(f"mm{u}" for u in range(GT)))
        with nc.Block() as block:
            @block.sync
            def _(sp):
                L.open(sp)
                sp.dma_start(w2[:], I["L3_gnn_ee_w2"].rearrange("(k p) n -> p k n", p=P)).then_inc(loaded, 16)
                sp.dma_start(self1[:], spread(I["L3_gnn_ee_b1"], D)).then_inc(loaded, 16)
                sp.dma_start(b2[:], spread(I["L3_gnn_ee_b2"], D)).then_inc(loaded, 16)
                sp.dma_start(eps2[:], spread(I["L3_gnn_eps"], 1)).then_inc(loaded, 16)
                with sp.Fori(0, NG) as i:
                    sp.wait_ge(*V.ended(i))
                    sp.dma_start(xn[:], rows_of(table, i)[:, :, 0:D]).then_inc(rows_in, 16)

            @block.vector
            def _(dve):
                link = chained(dve, ready)
                dve.wait_ge(loaded, 64)
                link(dve.tensor_scalar(self1[:], self1[:], 0.0, None, ALU.max))
                link(dve.tensor_scalar(eps2[:], eps2[:], 1.0, 1.0, ALU.add, ALU.add))
                link(dve.tensor_scalar(cnt[:], acc[:, :, 0, D], 1.0, None, ALU.add))
                with dve.Fori(0, NG) as i:
                    g = bass.ds(i * GT, GT)
                    dve.wait_ge(*M.ended(i))
                    dve.tensor_tensor(e[:], acc[:, g, 1, 0:D], self1[:].unsqueeze(1).broadcast_to([P, GT, D]),
                                      ALU.add).then_inc(*V.step("e"))
                    dve.wait_ge(rows_in, i * 16 + 16)
                    dve.wait_ge(*V.ended(i))
                    dve.scalar_tensor_tensor(h[:], xn[:], eps2[:, 0:1], acc[:, g, 0, 0:D], ALU.mult,
                                             ALU.add).then_inc(*V.step("h"))
                    dve.wait_ge(*V.at("h", i))
                    for u in range(GT):
                        dve.scalar_tensor_tensor(h[:, u, :], b2[:], cnt[:, bass.ds(i * GT + u, 1)], h[:, u, :],
                                                 ALU.mult, ALU.add).then_inc(*V.step(f"c{u}"))
                        dve.wait_ge(*V.at(f"c{u}", i))
                        dve.wait_ge(*M.at(f"mm{u}", i))
                        dve.tensor_tensor(h0[:, bass.ds(i * GT + u, 1), :].rearrange("p a d -> p (a d)"), h[:, u, :],
                                          y[u % 2], ALU.add).then_inc(*V.step(f"x{u}"))

            @block.scalar
            def _(act):
                with act.Fori(0, NG) as i:
                    act.wait_ge(*M.ended(i))
                    for u in range(GT):
                        act.wait_ge(*M.at(f"tr{u}", i))
                        act.copy(eT[:, u], tr[u % 2]).then_inc(*A.step(f"cp{u}"))

            @block.tensor
            def _(pe):
                pe.wait_ge(loaded, 64)
                with pe.Fori(0, NG) as i:
                    pe.wait_ge(*V.at("e", i))
                    pe.wait_ge(*A.ended(i))
                    for u in range(GT):
                        if u >= 2:
                            pe.wait_ge(*A.at(f"cp{u - 2}", i))
                        for k in range(2):
                            ins = pe.transpose(tr[u % 2][:, k, :], e[:, u, k * P:(k + 1) * P], G.ident[:])
                        ins.then_inc(*M.step(f"tr{u}"))
                    for u in range(GT):
                        pe.wait_ge(*A.at(f"cp{u}", i))
                        pe.wait_ge(*(V.at(f"x{u - 2}", i) if u >= 2 else V.ended(i)))
                        for k in range(2):
                            ins = pe.matmul(y[u % 2], eT[:, u, k, :], w2[:, k, :], start=(k == 0), stop=(k == 1))
                        ins.then_inc(*M.step(f"mm{u}"))


def gine_mlp(nc, G, I, table, h0):
    KH = HID // P
    with ExitStack() as ctx:
        L = Kit(nc, ctx, "gm")
        w1 = L.sb("w1", [P, 2, HID])
        w2 = L.sb("w2", [P, KH, HID])
        w3 = L.sb("w3", [P, KH, D])
        par = L.sb("par", [P, 6, HID])
        last = L.sb("last", [P, 3, D])
        xn = L.sb("xn", [P, GT, D])
        hs = L.sb("hs", [P, GT, D])
        inT = L.sb("inT", [P, 2, KH, P])
        z = L.sb("z", [P, GT, HID])
        stats = L.sb("stats", [P, GT, 2, 6])
        mv = L.sb("mv", [P, GT, 2])
        var = L.sb("var", [P, GT])
        std = L.sb("std", [P, GT])
        rstd = L.sb("rstd", [P, GT])
        tr = [L.ps(f"tr{s}", [P, 4, P]) for s in range(2)]
        big = [L.ps(f"big{s}", [P, HID]) for s in range(2)]
        small = [L.ps(f"small{s}", [P, D]) for s in range(2)]
        loaded, rows_in, took = L.sem("loaded"), L.sem("rows_in"), L.sem("took")
        PEN, ACN, DVN = "", "hs ", ""
        for l in range(3):
            for u in range(GT):
                for b in range(1 if l == 0 else 2):
                    PEN += f"tr{l}_{u}_{b} "
                    ACN += f"T{l}_{u}_{b} "
                PEN += f"mm{l}_{u} "
                DVN += f"b{l}_{u} " + ("xn%d " % u if l == 2 else "") + f"st{l}_{u} ag{l}_{u} ep{l}_{u} rs{l}_{u} g{l}_{u} be{l}_{u} "
                if l < 2:
                    ACN += f"sq{l}_{u} relu{l}_{u} "
                else:
                    ACN += f"sq{l}_{u} "
                    DVN += f"x{u} "
        M = L.steps("pe_mlp", PEN)
        A = L.steps("act_mlp", ACN)
        V = L.steps("dve_mlp", DVN)
        with nc.Block() as block:
            @block.sync
            def _(sp):
                L.open(sp)
                sp.dma_start(w1[:], I["L3_gnn_w1"].rearrange("(k p) n -> p k n", p=P)).then_inc(loaded, 16)
                sp.dma_start(w2[:], I["L3_gnn_w2"].rearrange("(k p) n -> p k n", p=P)).then_inc(loaded, 16)
                sp.dma_start(w3[:], I["L3_gnn_w3"].rearrange("(k p) n -> p k n", p=P)).then_inc(loaded, 16)
                for q, name in enumerate(("b1", "g1", "be1", "b2", "g2", "be2")):
                    sp.dma_start(par[:, q, :], spread(I["L3_gnn_" + name], HID)).then_inc(loaded, 16)
                for q, name in enumerate(("b3", "bn_g", "bn_b")):
                    sp.dma_start(last[:, q, :], spread(I["L3_gnn_" + name], D)).then_inc(loaded, 16)
                with sp.Fori(0, NG) as i:
                    sp.wait_ge(*V.ended(i))
                    sp.dma_start(xn[:], rows_of(table, i)[:, :, 0:D]).then_inc(rows_in, 16)

            @block.vector
            def _(dve):
                dve.wait_ge(loaded, 16 * 12)
                with dve.Fori(0, NG) as i:
                    for l in range(3):
                        for u in range(GT):
                            zt = z[:, u, 0:HID if l < 2 else D]
                            b, g, be = ((par[:, 3 * l + q, :] for q in range(3)) if l < 2 else
                                        (last[:, q, :] for q in range(3)))
                            src = big[u % 2] if l < 2 else small[u % 2]
                            dve.wait_ge(*M.at(f"mm{l}_{u}", i))
                            if l == 0:
                                dve.wait_ge(*V.ended(i))
                            dve.tensor_tensor(zt, src, b, ALU.add).then_inc(*V.step(f"b{l}_{u}"))
                            dve.wait_ge(*V.at(f"b{l}_{u}", i))
                            if l == 2:
                                dve.wait_ge(rows_in, i * 16 + 16)
                                dve.tensor_tensor(zt, zt, xn[:, u, :], ALU.add).then_inc(*V.step(f"xn{u}"))
                                dve.wait_ge(*V.at(f"xn{u}", i))
                                ins = dve.bn_stats(stats[:, u, 0, :], zt)
                            else:
                                for f in range(2):
                                    ins = dve.bn_stats(stats[:, u, f, :], z[:, u, f * 512:(f + 1) * 512])
                            ins.then_inc(*V.step(f"st{l}_{u}"))
                            dve.wait_ge(*V.at(f"st{l}_{u}", i))
                            dve.sem_inc(took, 1)
                            if l < 2:
                                ins = dve.bn_aggr(mv[:, u, :], stats[:, u].rearrange("p f s -> p (f s)"))
                            else:
                                ins = dve.bn_aggr(mv[:, u, :], stats[:, u, 0, :])
                            ins.then_inc(*V.step(f"ag{l}_{u}"))
                            dve.wait_ge(*V.at(f"ag{l}_{u}", i))
                            dve.tensor_scalar(var[:, u:u + 1], mv[:, u, 1:2], EPS, None, ALU.add).then_inc(*V.step(f"ep{l}_{u}"))
                            dve.wait_ge(*A.at(f"sq{l}_{u}", i))
                            dve.reciprocal(rstd[:, u:u + 1], std[:, u:u + 1]).then_inc(*V.step(f"rs{l}_{u}"))
                            dve.wait_ge(*V.at(f"rs{l}_{u}", i))
                            dve.scalar_tensor_tensor(zt, zt, mv[:, u, 0:1], g, ALU.subtract, ALU.mult).then_inc(*V.step(f"g{l}_{u}"))
                            dve.wait_ge(*V.at(f"g{l}_{u}", i))
                            dve.scalar_tensor_tensor(zt, zt, rstd[:, u:u + 1], be, ALU.mult, ALU.add).then_inc(*V.step(f"be{l}_{u}"))
                            if l == 2:
                                dve.wait_ge(*V.at(f"be{l}_{u}", i))
                                xt = G.x[:, bass.ds(i * GT + u, 1), :].rearrange("p a d -> p (a d)")
                                dve.scalar_tensor_tensor(xt, zt, 0.0, xt, ALU.max, ALU.add).then_inc(*V.step(f"x{u}"))

            @block.scalar
            def _(act):
                with act.Fori(0, NG) as i:
                    act.wait_ge(*M.ended(i))
                    act.copy(hs[:], h0[:, bass.ds(i * GT, GT), :]).then_inc(*A.step("hs"))
                    for l in range(3):
                        for u in range(GT):
                            for b in range(1 if l == 0 else 2):
                                act.wait_ge(*M.at(f"tr{l}_{u}_{b}", i))
                                if b == 0:
                                    q = l * GT + u - 2
                                    act.wait_ge(*(M.at(f"mm{q // GT}_{q % GT}", i) if q >= 0 else M.ended(i)))
                                m = 2 if l == 0 else 4
                                act.copy(inT[:, (l * GT + u) % 2, 4 * b:4 * b + m, :], tr[b][:, 0:m, :]).then_inc(*A.step(f"T{l}_{u}_{b}"))
                            act.wait_ge(*V.at(f"ep{l}_{u}", i))
                            act.activation(std[:, u:u + 1], var[:, u:u + 1], ACT.Sqrt).then_inc(*A.step(f"sq{l}_{u}"))
                            if l < 2:
                                act.wait_ge(*V.at(f"be{l}_{u}", i))
                                act.activation(z[:, u, :], z[:, u, :], ACT.Relu).then_inc(*A.step(f"relu{l}_{u}"))

            @block.tensor
            def _(pe):
                pe.wait_ge(loaded, 16 * 12)
                with pe.Fori(0, NG) as i:
                    for l in range(3):
                        for u in range(GT):
                            pe.wait_ge(*(A.at("hs", i) if l == 0 else A.at(f"relu{l - 1}_{u}", i)))
                            src = hs if l == 0 else z
                            for b in range(1 if l == 0 else 2):
                                if u:
                                    pe.wait_ge(*A.at(f"T{l}_{u - 1}_{b}", i))
                                elif l:
                                    pe.wait_ge(*A.at(f"T{l - 1}_{GT - 1}_{b if l > 1 else 0}", i))
                                m = 2 if l == 0 else 4
                                for k in range(4 * b, 4 * b + m):
                                    ins = pe.transpose(tr[b][:, k % 4, :], src[:, u, k * P:(k + 1) * P], G.ident[:])
                                ins.then_inc(*M.step(f"tr{l}_{u}_{b}"))
                            pe.wait_ge(*A.at(f"T{l}_{u}_{0 if l == 0 else 1}", i))
                            if l < 2:
                                q = l * GT + u - 2
                                pe.wait_ge(*(V.at(f"b{q // GT}_{q % GT}", i) if q >= 0 else V.ended(i)))
                            else:
                                pe.wait_ge(*(V.at(f"b{l}_{u - 2}", i) if u >= 2 else V.ended(i)))
                            K = 2 if l == 0 else KH
                            w = (w1, w2, w3)[l]
                            s = (l * GT + u) % 2
                            for f in range(2 if l < 2 else 1):
                                c = slice(f * 512, (f + 1) * 512) if l < 2 else slice(0, D)
                                out = (big[u % 2] if l < 2 else small[u % 2])[:, c]
                                for k in range(K):
                                    ins = pe.matmul(out, inT[:, s, k, :], w[:, k, c], start=(k == 0), stop=(k == K - 1))
                            ins.then_inc(*M.step(f"mm{l}_{u}"))


SH, SG = 8, 64
PR = SH // 2
FULL = SH * SG


def slice_logits_weights(nc, G, I, wl, bl):
    with ExitStack() as ctx:
        L = Kit(nc, ctx, "t0")
        wx = L.sb("wx", [P, 2, FULL])
        wxT = L.sb("wxT", [SG, SH, 2, P])
        ws = L.sb("ws", [SG, SG])
        bx = L.sb("bx", [SG, SH])
        bxr = L.sb("bxr", [SG, SH, P])
        bs = L.sb("bs", [P, SG])
        temp = L.sb("temp", [P, SH])
        turn = [L.ps(f"turn{q}", [SG, 2, 2, P]) for q in range(PR)]
        y = [L.ps(f"y{k}", [P, SH, SG]) for k in range(3)]
        loaded, bias_loaded, turned, copied = L.sem("loaded"), L.sem("bias_loaded"), L.sem("turned"), L.sem("copied")
        spread_out, product, chain = L.sem("spread_out"), L.sem("product"), L.sem("chain")
        with nc.Block() as block:
            @block.sync
            def _(sp):
                sp.dma_start(wx[:], I["L3_ffn_W_x"].rearrange("(k p) n -> p k n", p=P)).then_inc(loaded, 16)
                sp.dma_start(ws[:], I["L3_ffn_W_slice"]).then_inc(loaded, 16)
                with nc.allow_non_contiguous_dma(reason="a bias, features to partitions"):
                    sp.dma_start(bx[:], I["L3_ffn_b_x"].rearrange("(h c) -> c h", h=SH)).then_inc(bias_loaded, 16)
                sp.dma_start(bs[:], spread(I["L3_ffn_b_slice"], SG)).then_inc(bias_loaded, 16)
                sp.dma_start(temp[:], spread(I["L3_ffn_temperature"].rearrange("a h b c -> (a h b c)"),
                                             SH)).then_inc(bias_loaded, 16)

            @block.tensor
            def _(pe):
                pe.wait_ge(loaded, 32)
                for h in range(SH):
                    for k in range(2):
                        ins = pe.transpose(turn[h // 2][:, h % 2, k, :], wx[:, k, h * SG:(h + 1) * SG], G.ident[:])
                    if h % 2:
                        ins.then_inc(turned, 1)
                pe.wait_ge(copied, PR)
                for k in range(2):
                    for h in range(SH):
                        ins = pe.matmul(y[k][:, h, :], wxT[:, h, k, :], ws[:], start=True, stop=True)
                    ins.then_inc(product, 1)
                pe.wait_ge(spread_out, 1)
                for h in range(SH):
                    ins = pe.matmul(y[2][:, h, :], bxr[:, h, :], ws[:], start=True, stop=True)
                ins.then_inc(product, 1)

            @block.scalar
            def _(act):
                for q in range(PR):
                    act.wait_ge(turned, q + 1)
                    act.copy(wxT[:, 2 * q:2 * q + 2], turn[q]).then_inc(copied, 1)

            @block.vector
            def _(dve):
                link = chained(dve, chain)
                dve.wait_ge(bias_loaded, 48)
                dve.tensor_copy(bxr[:], bx[:].unsqueeze(2).broadcast_to([SG, SH, P])).then_inc(spread_out, 1)
                link(dve.tensor_scalar(temp[:], temp[:], 0.1, 5.0, ALU.max, ALU.min))
                link(dve.reciprocal(temp[:], temp[:]))
                per = temp[:].unsqueeze(2).broadcast_to([P, SH, SG])
                for k in range(2):
                    dve.wait_ge(product, k + 1)
                    link(dve.tensor_tensor(wl[:, k, :].rearrange("p (h g) -> p h g", h=SH), y[k], per, ALU.mult))
                b = bl[:].rearrange("p (h g) -> p h g", h=SH)
                dve.wait_ge(product, 3)
                link(dve.tensor_tensor(b, y[2], bs[:].unsqueeze(1).broadcast_to([P, SH, SG]), ALU.add))
                link(dve.tensor_tensor(b, b, per, ALU.mult))


def slice_pass(nc, G, I, wl, bl, wT, tok):
    with ExitStack() as ctx:
        L = Kit(nc, ctx, "t1")
        nrm = Norm(L, G)
        wf = L.sb("wf", [P, 2, FULL])
        bf = L.sb("bf", [P, FULL])
        fx = L.sb("fx", [P, GT, PR, P + 1])
        w = L.sb("w", [P, GT, FULL])
        top = L.sb("top", [P, GT, SH])
        sums = L.sb("sums", [P, GT, SH])
        valid = L.sb("valid", [P, NT])
        fxp = L.ps("fxp", [P, PR, P])
        lgp = L.ps("lgp", [P, FULL])
        turn = [L.ps(f"turn{s}", [P, PR, P]) for s in range(2)]
        total = [L.ps(f"total{s}", [P, 2, P + 1]) for s in range(2)]
        loaded, filled = L.sem("loaded"), L.sem("filled")
        us = range(GT)
        M = L.steps("pe_slices", " ".join(f"fx{u} lg{u}" for u in us) + " " + " ".join(f"tr{u}" for u in us) + " sum0 sum1")
        V = L.steps("dve_softmax", " ".join(f"fx{u} lg{u}" for u in us) + " top less sum inv valid w tok0 tok1")
        A = L.steps("act_exp", "exp " + " ".join(f"cp{u}" for u in us))
        with nc.Block() as block:
            @block.sync
            def _(sp):
                L.open(sp)
                sp.dma_start(wf[:], I["L3_ffn_W_fx"].rearrange("(k p) n -> p k n", p=P)).then_inc(loaded, 16)
                sp.dma_start(bf[:], spread(I["L3_ffn_b_fx"], FULL)).then_inc(loaded, 16)

            @block.vector
            def _(dve):
                dve.memset(tok[:], 0.0).then_inc(filled, 1)
                dve.memset(fx[:, :, :, P:P + 1], 1.0).then_inc(filled, 1)
                dve.memset(valid[:, 0:NT - 1], 1.0).then_inc(filled, 1)
                dve.tensor_scalar(valid[:, NT - 1:NT], G.part[:, 0:1], float(N - (NT - 1) * P), None,
                                  ALU.is_lt).then_inc(filled, 1)
                dve.wait_ge(filled, 4)
                dve.wait_ge(loaded, 32)
                with dve.Fori(0, NG) as i:
                    nrm.dve(dve, i)
                    dve.wait_ge(*M.ended(i))
                    for u in us:
                        dve.wait_ge(*M.at(f"fx{u}", i))
                        dve.tensor_tensor(fx[:, u, :, 0:P], fxp, bf[:].rearrange("p (q c) -> p q c", q=PR),
                                          ALU.add).then_inc(*V.step(f"fx{u}"))
                        dve.wait_ge(*M.at(f"lg{u}", i))
                        dve.tensor_tensor(w[:, u, :], lgp, bl[:], ALU.add).then_inc(*V.step(f"lg{u}"))
                    heads = w[:].rearrange("p u (h g) -> p (u h) g", h=SH)

                    def per(a):
                        return a[:].rearrange("p u h -> p (u h)").unsqueeze(2).broadcast_to([P, GT * SH, SG])
                    dve.wait_ge(*V.at(f"lg{GT - 1}", i))
                    dve.tensor_reduce(top[:].rearrange("p u h -> p (u h)"), heads, AX.X, ALU.max).then_inc(*V.step("top"))
                    dve.wait_ge(*V.at("top", i))
                    dve.tensor_tensor(heads, heads, per(top), ALU.subtract).then_inc(*V.step("less"))
                    dve.wait_ge(*A.at("exp", i))
                    dve.tensor_reduce(sums[:].rearrange("p u h -> p (u h)"), heads, AX.X, ALU.add).then_inc(*V.step("sum"))
                    dve.wait_ge(*V.at("sum", i))
                    dve.reciprocal(sums[:], sums[:]).then_inc(*V.step("inv"))
                    dve.wait_ge(*V.at("inv", i))
                    dve.tensor_tensor(sums[:], sums[:], valid[:, bass.ds(i * GT, GT)].unsqueeze(2)
                                      .broadcast_to([P, GT, SH]), ALU.mult).then_inc(*V.step("valid"))
                    dve.wait_ge(*V.at("valid", i))
                    dve.tensor_tensor(heads, heads, per(sums), ALU.mult).then_inc(*V.step("w"))
                    for s in range(2):
                        dve.wait_ge(*M.at(f"sum{s}", i))
                        dve.tensor_tensor(tok[:, 2 * s:2 * s + 2, :], tok[:, 2 * s:2 * s + 2, :], total[s],
                                          ALU.add).then_inc(*V.step(f"tok{s}"))

            @block.scalar
            def _(act):
                act.wait_ge(loaded, 32)
                with act.Fori(0, NG) as i:
                    nrm.act(act, i, M.ended(i))
                    act.wait_ge(*V.at("less", i))
                    act.activation(w[:], w[:], ACT.Exp).then_inc(*A.step("exp"))
                    for u in us:
                        act.wait_ge(*M.at(f"tr{u}", i))
                        act.copy(wT[:, :, bass.ds(i * (GT * P) + u * P, P)], turn[u % 2]).then_inc(*A.step(f"cp{u}"))

            @block.tensor
            def _(pe):
                pe.wait_ge(loaded, 32)
                with pe.Fori(0, NG) as i:
                    nrm.pe(pe, i)
                    for u in us:
                        pe.wait_ge(*nrm.C.at(f"cp{u}", i))
                        xT = nrm.xT[:, :, u * P:(u + 1) * P]
                        pe.wait_ge(*(V.at(f"fx{u - 1}", i) if u else V.ended(i)))
                        for k in range(2):
                            ins = pe.matmul(fxp.rearrange("p q c -> p (q c)"), xT[:, k, :], wf[:, k, :],
                                            start=(k == 0), stop=(k == 1))
                        ins.then_inc(*M.step(f"fx{u}"))
                        if u:
                            pe.wait_ge(*V.at(f"lg{u - 1}", i))
                        for k in range(2):
                            ins = pe.matmul(lgp, xT[:, k, :], wl[:, k, :], start=(k == 0), stop=(k == 1))
                        ins.then_inc(*M.step(f"lg{u}"))
                    pe.wait_ge(*V.at("w", i))
                    for u in us:
                        pe.wait_ge(*(A.at(f"cp{u - 2}", i) if u >= 2 else A.ended(i)))
                        for q in range(PR):
                            ins = pe.transpose(turn[u % 2][:, q, :], w[:, u, q * P:(q + 1) * P], G.ident[:])
                        ins.then_inc(*M.step(f"tr{u}"))
                    for s in range(2):
                        for q in range(2):
                            pair = 2 * s + q
                            for u in us:
                                ins = pe.matmul(total[s][:, q, :], w[:, u, pair * P:(pair + 1) * P],
                                                fx[:, u, pair, :], start=(u == 0), stop=(u == GT - 1))
                        ins.then_inc(*M.step(f"sum{s}"))


def slice_attention(nc, G, I, tok, M4):
    with ExitStack() as ctx:
        L = Kit(nc, ctx, "t2")
        wq = L.sb("wq", [SG, 3, SG])
        wo = L.sb("wo", [P, PR, D])
        inv = L.sb("inv", [P, PR])
        t = L.sb("t", [P, PR, SG])
        tT = L.sb("tT", [SG, PR * P])
        qk = L.sb("qk", [SG, 2, PR * P])
        v = L.sb("v", [P, PR, P])
        a = L.sb("a", [P, PR, SG])
        ab = L.sb("ab", [P, PR, P])
        abT = L.sb("abT", [P, PR, P])
        osT = L.sb("osT", [P, PR, P])
        top = L.sb("top", [P, PR])
        turn = L.ps("turn", [P, PR, P])
        qkp = [L.ps(f"qkp{s}", [SG, PR * P]) for s in range(2)]
        vp = L.ps("vp", [P, PR, SG])
        lg = L.ps("lg", [P, PR, P])
        op = L.ps("op", [P, PR, P])
        mp = [L.ps(f"mp{s}", [P, 2, D]) for s in range(2)]
        loaded, chain, worked, exps = L.sem("loaded"), L.sem("chain"), L.sem("worked"), L.sem("exps")
        done = L.sem("done")
        halves = [(slice(f * SG, (f + 1) * SG), slice(f * SG, (f + 1) * SG)) for f in range(2)]
        with nc.Block() as block:
            @block.sync
            def _(sp):
                for n, name in enumerate(("L3_ffn_W_q", "L3_ffn_W_k", "L3_ffn_W_v")):
                    sp.dma_start(wq[:, n, :], I[name]).then_inc(loaded, 16)
                sp.dma_start(wo[:], I["L3_ffn_W_out"].rearrange("(q p) n -> p q n", p=P)).then_inc(loaded, 16)

            @block.vector
            def _(dve):
                link = chained(dve, chain)
                link(dve.memset(v[:], 0.0))
                link(dve.memset(ab[:], 0.0))
                link(dve.tensor_scalar(inv[:], tok[:, :, P], 1e-5, None, ALU.add))
                link(dve.reciprocal(inv[:], inv[:]))
                for p, c in halves:
                    link(dve.tensor_tensor(t[p], tok[p, :, c], inv[p].unsqueeze(2).broadcast_to([SG, PR, SG]), ALU.mult))
                dve.sem_inc(done, 1)
                dve.wait_ge(worked, 1)
                link(dve.tensor_copy(tT[:], turn[0:SG].rearrange("p q c -> p (q c)")))
                dve.sem_inc(done, 1)
                dve.wait_ge(worked, 2)
                for s in range(2):
                    link(dve.tensor_copy(qk[:, s, :], qkp[s]))
                dve.sem_inc(done, 1)
                for p, c in halves:
                    link(dve.tensor_copy(v[p, :, c], vp[p]))
                dve.wait_ge(worked, 3)
                for p, c in halves:
                    link(dve.tensor_scalar(a[p], lg[p, :, c], SG ** -0.5, None, ALU.mult))
                link(dve.tensor_reduce(top[:], a[:], AX.X, ALU.max))
                link(dve.tensor_tensor(a[:], a[:], top[:].unsqueeze(2).broadcast_to([P, PR, SG]), ALU.subtract))
                dve.sem_inc(done, 1)
                dve.wait_ge(exps, 1)
                link(dve.tensor_reduce(top[:], a[:], AX.X, ALU.add))
                link(dve.reciprocal(top[:], top[:]))
                for p, c in halves:
                    link(dve.tensor_tensor(ab[p, :, c], a[p], top[p].unsqueeze(2).broadcast_to([SG, PR, SG]), ALU.mult))
                dve.sem_inc(done, 1)
                dve.wait_ge(worked, 4)
                link(dve.tensor_copy(abT[:], turn))
                dve.sem_inc(done, 1)
                dve.wait_ge(worked, 5)
                link(dve.tensor_copy(osT[:], op))
                dve.sem_inc(done, 1)
                dve.wait_ge(worked, 6)
                for s in range(2):
                    link(dve.tensor_copy(M4[:, 2 * s:2 * s + 2, :], mp[s]))

            @block.scalar
            def _(act):
                act.wait_ge(done, 4)
                act.activation(a[:], a[:], ACT.Exp).then_inc(exps, 1)

            @block.tensor
            def _(pe):
                def pairs(work):
                    for q in range(PR):
                        ins = work(q, slice(q * P, (q + 1) * P))
                    ins.then_inc(worked, 1)
                pe.wait_ge(loaded, 64)
                pe.wait_ge(done, 1)
                pairs(lambda q, c: pe.transpose(turn[0:SG, q, :], t[:, q, :], G.ident[:]))
                pe.wait_ge(done, 2)
                for s in range(2):
                    pe.matmul(qkp[s], wq[:, s, :], tT[:], start=True, stop=True)
                pairs(lambda q, c: pe.matmul(vp[:, q, :], tT[:, c], wq[:, 2, :], start=True, stop=True))
                pe.wait_ge(done, 3)
                pairs(lambda q, c: pe.matmul(lg[:, q, :], qk[:, 0, c], qk[:, 1, c], start=True, stop=True))
                pe.wait_ge(done, 5)
                pairs(lambda q, c: pe.transpose(turn[:, q, :], ab[:, q, :], G.ident[:]))
                pe.wait_ge(done, 6)
                pairs(lambda q, c: pe.matmul(op[:, q, :], v[:, q, :], abT[:, q, :], start=True, stop=True))
                pe.wait_ge(done, 7)
                pairs(lambda q, c: pe.matmul(mp[q // 2][:, q % 2, :], osT[:, q, :], wo[:, q, :], start=True, stop=True))


def unslice(nc, G, I, wT, M4):
    with ExitStack() as ctx:
        L = Kit(nc, ctx, "t3")
        st = L.sb("st", [P, 2, PR, P])
        bo = L.sb("bo", [P, D])
        y = [L.ps(f"y{s}", [P, D]) for s in range(2)]
        loaded = L.sem("loaded")
        us = range(GT)
        A = L.steps("act_staged", " ".join(f"st{u}" for u in us))
        M = L.steps("pe_out", " ".join(f"mm{u}" for u in us))
        V = L.steps("dve_out", "bias " + " ".join(f"x{u}" for u in us))
        with nc.Block() as block:
            @block.sync
            def _(sp):
                L.open(sp)
                sp.dma_start(bo[:], spread(I["L3_ffn_b_out"], D)).then_inc(loaded, 16)

            @block.scalar
            def _(act):
                with act.Fori(0, NG) as i:
                    for u in us:
                        act.wait_ge(*(M.at(f"mm{u - 2}", i) if u >= 2 else M.ended(i)))
                        act.copy(st[:, u % 2], wT[:, :, bass.ds(i * (GT * P) + u * P, P)]).then_inc(*A.step(f"st{u}"))

            @block.tensor
            def _(pe):
                with pe.Fori(0, NG) as i:
                    for u in us:
                        pe.wait_ge(*A.at(f"st{u}", i))
                        pe.wait_ge(*(V.at(f"x{u - 2}", i) if u >= 2 else V.ended(i)))
                        for q in range(PR):
                            ins = pe.matmul(y[u % 2], st[:, u % 2, q, :], M4[:, q, :], start=(q == 0), stop=(q == PR - 1))
                        ins.then_inc(*M.step(f"mm{u}"))

            @block.vector
            def _(dve):
                dve.wait_ge(loaded, 16)
                with dve.Fori(0, NG) as i:
                    xs = G.x[:, bass.ds(i * GT, GT), :]
                    dve.tensor_tensor(xs, xs, bo[:].unsqueeze(1).broadcast_to([P, GT, D]), ALU.add).then_inc(*V.step("bias"))
                    dve.wait_ge(*V.at("bias", i))
                    for u in us:
                        dve.wait_ge(*M.at(f"mm{u}", i))
                        xt = G.x[:, bass.ds(i * GT + u, 1), :].rearrange("p a d -> p (a d)")
                        dve.tensor_tensor(xt, xt, y[u % 2], ALU.add).then_inc(*V.step(f"x{u}"))


def program(nc, I, out):
    with ExitStack() as ctx:
        K = Kit(nc, ctx, "")
        K.row_sems()
        G = Globals()
        constants(nc, K, G)
        X = Edges(K, "g_", NCH)
        R = Edges(K, "r_", FNC)

        def dram(name, shape):
            return nc.dram_tensor(name, shape, F32, kind="Internal").ap()

        g_first, g_rows = dram("g_first", [P * EJ, REC]), dram("g_rows", [P * NCH, REC])
        r_first, r_rows = dram("r_first", [P * FEJ, 2]), dram("r_rows", [P * FNC, 2])
        with ExitStack() as sctx:
            S = Kit(nc, sctx, "s")
            G.chunk = S.sb("chunk", [P, NCH])
            numbered = S.sem("numbered")
            with nc.Block() as block:
                @block.gpsimd
                def _(pool):
                    pool.iota(G.chunk[:], [[1, NCH]], base=0, channel_multiplier=0,
                              allow_small_or_imprecise_dtypes=True).then_inc(numbered, 1)
            sort_edges(nc, K, G, "sr", FEJ, 2, fill_router(nc, G, I), r_first, r_rows, FNC, (R.tile_of, R.tile))
            sort_edges(nc, K, G, "sg", EJ, REC, fill_graph(nc, G, I), g_first, g_rows, NCH, (X.tile_of, X.tile))
        field = K.sb("field", [P, NCH, 9])
        load_edges(nc, "lr", R, r_rows, 2)
        load_edges(nc, "lg", X, g_rows, REC, field)
        G.x = K.sb("x_sb", [P, NT, D])
        xin = K.sem("xin")
        full = N // P
        with nc.Block() as block:
            @block.vector
            def _(dve):
                dve.memset(G.x[:, full, :], 0.0).then_inc(xin, 1)

            @block.sync
            def _(sp):
                sp.wait_ge(xin, 1)
                sp.dma_start(G.x[:, 0:full, :], I["x"][0:full * P, :].rearrange("(t p) d -> p t d", p=P)).then_inc(xin, 16)
                sp.dma_start(G.x[0:N - full * P, full, :], I["x"][full * P:N, :]).then_inc(xin, 16)
                sp.wait_ge(xin, 33)
        T = Tables(dram)
        for sublayer in SUBLAYERS:
            sublayer(nc, G, I, X, R, field, g_rows, T)
        stored = K.sem("stored")
        with nc.Block() as block:
            @block.sync
            def _(sp):
                sp.dma_start(out[0:full * P, :].rearrange("(t p) d -> p t d", p=P), G.x[:, 0:full, :]).then_inc(stored, 16)
                sp.dma_start(out[full * P:N, :], G.x[0:N - full * P, full, :]).then_inc(stored, 16)
                sp.wait_ge(stored, 32)


class Tables:

    def __init__(self, dram):
        self.rows = dram("rows", [NP, D])
        self.logit = dram("logit", [NP, 8])
        self.router = dram("router", [NP, 20])
        self.counted = dram("counted", [NP, D + 1])


def layer0_gnn(nc, G, I, X, R, field, g_rows, T):
    H = 8
    with ExitStack() as ctx:
        L = Kit(nc, ctx, "l0")
        acc = L.sb("acc", [P, NT, D + H])
        alpha = L.sb("alpha", [P, NCH, H])
        ar = L.sb("ar", [P, NT, H])
        clear(nc, "c0", acc[:])
        gat_nodes(nc, G, I, "a0", I["L0_gnn_W_lin"], I["L0_gnn_W_res"],
                  I["L0_gnn_att_l"].rearrange("a h c -> (a h c)"), I["L0_gnn_att_r"].rearrange("a h c -> (a h c)"),
                  T.rows, T.logit, lambda i: ar[:, bass.ds(i * GT, GT), :])
        attention_pass(nc, G, "b0", X, H, T.logit, H, 0, ar, alpha, weight=field[:, :, R_EW])
        softmax_pass(nc, G, "s0", X, H, alpha[:])
        message_pass(nc, G, "m0", X, H, 32, T.rows, alpha, acc)
        finish_l0_gnn(nc, G, acc)


def layer0_experts(nc, G, I, X, R, field, g_rows, T):
    with ExitStack() as ctx:
        L = Kit(nc, ctx, "l0f")
        gates = L.sb("gates", [P, NT, 4])
        b2 = L.sb("b2", [4, D])
        with ExitStack() as inner:
            L2 = Kit(nc, inner, "l0r")
            acc = L2.sb("acc", [P, NT, 20])
            alpha = L2.sb("alpha", [P, FNC, 4])
            hrow = L2.sb("hrow", [P, FNC, 16])
            ad = L2.sb("ad", [P, NT, 4])
            clear(nc, "c1", acc[:])
            router_nodes(nc, G, I, T.router, ad)
            attention_pass(nc, G, "b1", R, 4, T.router, 20, 16, ad, alpha, keep=hrow)
            softmax_pass(nc, G, "s1", R, 4, alpha[:])
            message_pass(nc, G, "m1", R, 4, 4, None, alpha, acc, rows=hrow)
            router_gates(nc, G, I, acc, gates)
        gelu_experts(nc, G, "e0", I["L0_ffn_W1"], I["L0_ffn_b1"], I["L0_ffn_W2"], gates, 4)
        load(nc, "lb0", b2[:], I["L0_ffn_b2"])
        gate_bias(nc, G, "gb0", gates, 4, b2)


def layer1_gnn(nc, G, I, X, R, field, g_rows, T):
    with ExitStack() as ctx:
        L = Kit(nc, ctx, "l1")
        acc = L.sb("acc", [P, NT, D])
        types, weight = field[:, :, R_TYPE], field[:, :, R_EW1]
        conv_nodes(nc, G, "n1", I["L1_gnn_loop_w1"], I["L1_gnn_b1"], T.rows, acc)
        conv_pass(nc, G, "v1", X, T.rows, types, weight, I["L1_gnn_w1"], acc)
        conv_nodes(nc, G, "n2", I["L1_gnn_loop_w2"], I["L1_gnn_b2"], T.rows, acc, relu_of=acc)
        conv_pass(nc, G, "v2", X, T.rows, types, weight, I["L1_gnn_w2"], acc)
        add_to_x(nc, G, "x1", acc[:])


def layer1_experts(nc, G, I, X, R, field, g_rows, T):
    with ExitStack() as ctx:
        L = Kit(nc, ctx, "l1f")
        gates = L.sb("gates", [P, NT, 8])
        b2 = L.sb("b2", [8, D])
        affine = (I["L1_ffn_gamma"], I["L1_ffn_beta"])
        scores_of(nc, G, "g1", I["L1_ffn_Wr"], 8, I["L1_ffn_br"], gates, affine)
        gelu_experts(nc, G, "e1", I["L1_ffn_W1"], I["L1_ffn_b1"], I["L1_ffn_W2"], gates, 8, affine)
        load(nc, "lb1", b2[:], I["L1_ffn_b2"])
        gate_bias(nc, G, "gb1", gates, 8, b2)


def layer2_gnn(nc, G, I, X, R, field, g_rows, T):
    H = 8
    with ExitStack() as ctx:
        L = Kit(nc, ctx, "l2")
        acc = L.sb("acc", [P, NT, D + H])
        alpha = L.sb("alpha", [P, NCH, H])
        with ExitStack() as inner:
            L2 = Kit(nc, inner, "l2h")
            hh = L2.sb("hh", [P, NT, D + H])
            ew = L2.sb("ew", [4, D])
            clear(nc, "c2", acc[:])
            with nc.allow_non_contiguous_dma(reason="a small weight, transposed"):
                load(nc, "le2", ew[0:3, :], I["L2_gnn_edge_W"].rearrange("n f -> f n"),
                     ew[3:4, :], I["L2_gnn_edge_b"].rearrange("(o n) -> o n", o=1))
            gat_nodes(nc, G, I, "a2", I["L2_gnn_W"], None, I["L2_gnn_a_src"].rearrange("h c -> (h c)"),
                      I["L2_gnn_a_dst"].rearrange("h c -> (h c)"), T.rows, T.logit,
                      lambda i: hh[:, bass.ds(i * GT, GT), D:D + H], keep=hh, transposed=True)
            edge_attention_pass(nc, G, "b2", X, T.logit, hh, field[:, :, R_EA3:R_EA3 + 4], ew, alpha)
        softmax_pass(nc, G, "s2", X, H, alpha[:])
        message_pass(nc, G, "m2", X, H, 32, T.rows, alpha, acc)
        finish_l2_gnn(nc, G, acc, I["L2_gnn_bias"])


def layer2_experts(nc, G, I, X, R, field, g_rows, T):
    with ExitStack() as ctx:
        L = Kit(nc, ctx, "l2f")
        gates = L.sb("gates", [P, NT, 5])
        b3 = L.sb("b3", [5, D])
        clear(nc, "c3", gates[:], 1.0)
        scores_of(nc, G, "g2", I["L2_ffn_gW"], 4, I["L2_ffn_gb"], gates, soft=True)
        relu_experts(nc, G, I, gates)
        load(nc, "lb2", b3[0:4, :], I["L2_ffn_eb3"], b3[4:5, :], I["L2_ffn_sb3"].rearrange("(o n) -> o n", o=1))
        gate_bias(nc, G, "gb2", gates, 5, b3)


def layer3_gnn(nc, G, I, X, R, field, g_rows, T):
    with ExitStack() as ctx:
        L = Kit(nc, ctx, "l3")
        h0 = L.sb("h0", [P, NT, D])
        counted_nodes(nc, G, T.counted)
        with ExitStack() as inner:
            L2 = Kit(nc, inner, "l3a")
            acc = L2.sb("acc", [P, NT, 2, D + 1])
            clear(nc, "c4", acc[:])
            gine_pass(nc, G, I, "v3", X, T.counted, g_rows, acc)
            gine_nodes(nc, G, I, T.counted, acc, h0)
        gine_mlp(nc, G, I, T.counted, h0)


def layer3_ffn(nc, G, I, X, R, field, g_rows, T):
    with ExitStack() as ctx:
        L = Kit(nc, ctx, "l3f")
        wl = L.sb("wl", [P, 2, FULL])
        bl = L.sb("bl", [P, FULL])
        wT = L.sb("wT", [P, PR, NP])
        tok = L.sb("tok", [P, PR, P + 1])
        M4 = L.sb("M4", [P, PR, D])
        slice_logits_weights(nc, G, I, wl, bl)
        slice_pass(nc, G, I, wl, bl, wT, tok)
        slice_attention(nc, G, I, tok, M4)
        unslice(nc, G, I, wT, M4)


SUBLAYERS = [layer0_gnn, layer0_experts, layer1_gnn, layer1_experts, layer2_gnn, layer2_experts, layer3_gnn,
             layer3_ffn]


INPUTS = ("x", "src", "dst", "edge_attr_3", "edge_attr_64", "edge_type_16", "edge_weight", "edge_weight1",
          "L0_gnn_W_lin", "L0_gnn_att_l", "L0_gnn_att_r", "L0_gnn_W_res", "L0_ffn_W_gat", "L0_ffn_att_src",
          "L0_ffn_att_dst", "L0_ffn_b_gat", "L0_ffn_ln_gamma", "L0_ffn_ln_beta", "L0_ffn_W1", "L0_ffn_b1",
          "L0_ffn_W2", "L0_ffn_b2", "L0_ffn_edge_index", "L1_gnn_w1", "L1_gnn_loop_w1", "L1_gnn_b1",
          "L1_gnn_w2", "L1_gnn_loop_w2", "L1_gnn_b2", "L1_ffn_gamma", "L1_ffn_beta", "L1_ffn_Wr", "L1_ffn_br",
          "L1_ffn_W1", "L1_ffn_b1", "L1_ffn_W2", "L1_ffn_b2", "L2_gnn_W", "L2_gnn_a_src", "L2_gnn_a_dst",
          "L2_gnn_edge_W", "L2_gnn_edge_b", "L2_gnn_bias", "L2_ffn_sW1", "L2_ffn_sb1", "L2_ffn_sW2",
          "L2_ffn_sb2", "L2_ffn_sW3", "L2_ffn_sb3", "L2_ffn_eW1", "L2_ffn_eb1", "L2_ffn_eW2", "L2_ffn_eb2",
          "L2_ffn_eW3", "L2_ffn_eb3", "L2_ffn_gW", "L2_ffn_gb", "L3_gnn_eps", "L3_gnn_ee_w1", "L3_gnn_ee_b1",
          "L3_gnn_ee_w2", "L3_gnn_ee_b2", "L3_gnn_w1", "L3_gnn_b1", "L3_gnn_g1", "L3_gnn_be1", "L3_gnn_w2",
          "L3_gnn_b2", "L3_gnn_g2", "L3_gnn_be2", "L3_gnn_w3", "L3_gnn_b3", "L3_gnn_bn_g", "L3_gnn_bn_b",
          "L3_ffn_W_fx", "L3_ffn_b_fx", "L3_ffn_W_x", "L3_ffn_b_x", "L3_ffn_W_slice", "L3_ffn_b_slice",
          "L3_ffn_W_q", "L3_ffn_W_k", "L3_ffn_W_v", "L3_ffn_W_out", "L3_ffn_b_out", "L3_ffn_temperature")


def kernel(**inputs):
    import numpy as np
    import concourse.bacc as bacc
    from concourse.bass_utils import run_bass_kernel_spmd

    nc = bacc.Bacc("TRN2", target_bir_lowering=False, num_devices=1)
    arrays, aps = {}, {}
    for name in INPUTS:
        a = np.ascontiguousarray(inputs[name])
        arrays["in_" + name] = a = a.reshape(a.shape or (1,))
        aps[name] = nc.dram_tensor("in_" + name, a.shape, mybir.dt.from_np(a.dtype), kind="ExternalInput").ap()
    out = nc.dram_tensor("out_x", (N, D), F32, kind="ExternalOutput").ap()
    program(nc, aps, out)
    return run_bass_kernel_spmd(nc, [arrays], core_ids=[0]).results[0]["out_x"]
```

```python
from contextlib import ExitStack

import concourse.bass as bass
from concourse import mybir

ALU = mybir.AluOpType
ACT = mybir.ActivationFunctionType
AX = mybir.AxisListType
F32 = mybir.dt.float32
BF16 = mybir.dt.bfloat16
I32 = mybir.dt.int32

P = 128
N = 3125
NT = (N + P - 1) // P
NP = NT * P
D = 256
PAD = NP - 1
BIG = 1.0e30
EPS = 1.0e-5

E = 50000
EF = 64
EJ = 392
FE = 32768
FEJ = 288
REC = 9 + EF
R_SRC, R_DST, R_TYPE, R_EW, R_EW1, R_EA3, R_ONE, R_EA = 0, 1, 2, 3, 4, 5, 8, 9
NCH = 416
FNC = 320
U = 4
IT = 2 * U


class Steps:

    def __init__(self, sem, names, lead=0):
        self.sem, self.names = sem, names.split()
        self.base = len(self.names) * (2 if lead else 1)
        self.opening = self.base - lead
        self.n = self.opening

    def step(self, name):
        assert self.names[self.n % len(self.names)] == name, (name, self.names[self.n % len(self.names)])
        self.n += 1
        return self.sem, 1

    def skip(self, count):
        self.n += count
        return self.sem, count

    def at(self, name, i=0):
        return self.sem, i * len(self.names) + (self.base + self.names.index(name) + 1)

    def half(self, name, h, i):
        name = name.replace("#", str(h))
        return self.at("next_" + name, i - 1) if "next_" + name in self.names else self.at(name, i)

    def half_step(self, name, h):
        name = name.replace("#", str(h))
        return self.step("next_" + name if "next_" + name in self.names else name)

    def ended(self, i):
        return self.sem, i * len(self.names) + self.base


class Kit:

    free = [None]
    rows = [None, 0]

    def __init__(self, nc, ctx, tag):
        self.nc, self.ctx, self.tag, self.counted = nc, ctx, tag, []
        if not tag:
            Kit.free[0] = min(nc.free_semaphores)
        self.first = Kit.free[0]
        ctx.callback(self.close)

    def close(self):
        if Kit.free[0] > self.first:
            self.nc.all_engine_barrier(sems_to_clear=range(self.first, Kit.free[0]))
        Kit.free[0] = self.first

    def sb(self, name, shape, dt=F32):
        return self.ctx.enter_context(self.nc.sbuf_tensor(self.tag + name, shape, dt))

    def ps(self, name, shape, dt=F32):
        words = 512 if dt == F32 else 1024
        size = 1
        for n in shape[1:]:
            size *= n
        t = self.ctx.enter_context(self.nc.psum_tensor(self.tag + name, [P, -(-size // words) * words], dt))
        a = t[0:shape[0], 0:size]
        if len(shape) == 2:
            return a
        names = "abcd"[:len(shape) - 1]
        return a.rearrange(f"p ({' '.join(names)}) -> p {' '.join(names)}", **dict(zip(names, shape[1:])))

    def sem(self, name):
        Kit.free[0] += 1
        return self.ctx.enter_context(self.nc.semaphore(self.tag + name, num=Kit.free[0] - 1))

    def row_sems(self, rounds=0):
        if not self.tag:
            Kit.rows[:] = [[self.sem(f"rows_moved{u}_") for u in range(8)], 16]
        before = Kit.rows[1]
        Kit.rows[1] += 16 * rounds
        return Kit.rows[0], before

    def steps(self, name, names, lead=0):
        self.counted.append(Steps(self.sem(name), names, lead))
        return self.counted[-1]

    def open(self, eng):
        for steps in self.counted:
            eng.sem_inc(steps.sem, steps.opening)


def constants(nc, K, G, some_row):
    G.iota = K.sb("iota", [P, P])
    G.part = K.sb("part", [P, 1])
    G.ident = K.sb("ident", [P, P])
    G.identb = K.sb("identb", [P, P], BF16)
    G.ones = K.sb("ones", [P, P])
    G.earlier = K.sb("earlier", [P, P])
    first_dma = K.sb("first_dma", [1, 8, 8], I32)
    filled = K.sem("filled")
    made = K.sem("made")
    block = nc.Block()
    with block:
        @block.gpsimd
        def _(pool):
            pool.iota(G.iota[:], [[1, P]], base=0, channel_multiplier=0,
                      allow_small_or_imprecise_dtypes=True).then_inc(filled, 1)
            pool.iota(G.part[:], [[0, 1]], base=0, channel_multiplier=1,
                      allow_small_or_imprecise_dtypes=True).then_inc(filled, 1)
            for u, moved in enumerate(Kit.rows[0]):
                pool.dma_start(first_dma[0:1, u, :], some_row).then_inc(moved, 16)

        @block.vector
        def _(dve):
            dve.memset(G.ones[:], 1.0).then_inc(made, 1)
            dve.wait_ge(filled, 2)
            dve.tensor_scalar(G.ident[:], G.iota[:], G.part[:, 0:1], None, ALU.is_equal).then_inc(made, 1)
            dve.tensor_scalar(G.identb[:], G.iota[:], G.part[:, 0:1], None, ALU.is_equal).then_inc(made, 1)
            dve.tensor_scalar(G.earlier[:], G.iota[:], G.part[:, 0:1], None, ALU.is_gt).then_inc(made, 1)


def chained(eng, sem):
    k = [0]

    def link(ins):
        k[0] += 1
        ins.then_inc(sem, 1)
        eng.wait_ge(sem, k[0])
    return link


def count_edges(nc, G, tag, cols, dst, low, high, start, X):
    ch = X.chunks
    with ExitStack() as ctx:
        L = Kit(nc, ctx, tag)
        key_i = L.sb("key_i", [P, 3, cols], I32)
        chunk = L.sb("chunk", [P, ch])
        after = L.sb("after", [P, ch, NT - 1])
        ohl = L.sb("ohl", [P, 2, U, P], BF16)
        ohh = L.sb("ohh", [P, 2, U, NT], BF16)
        none = L.sb("none", [P, P], BF16)
        count = L.sb("count", [P, NT])
        whole = L.sb("whole", [P, 3, NT])
        whole_i = L.sb("whole_i", [P, NT], I32)
        zero = L.sb("zero", [P, NT])
        counts = L.ps("counts", [P, NT])
        sums = L.ps("sums", [P, 2, NT])
        numbered, counted, summed, chain = L.sem("numbered"), L.sem("counted"), L.sem("summed"), L.sem("chain")
        V = L.steps("dve_onehot", "low0 high0 low1 high1")
        M = L.steps("pe_count", "count0 count1")
        with nc.Block() as block:
            @block.sync
            def _(sp):
                L.open(sp)

            @block.gpsimd
            def _(pool):
                pool.iota(chunk[:], [[1, ch]], base=0, channel_multiplier=0,
                          allow_small_or_imprecise_dtypes=True).then_inc(numbered, 1)

            @block.vector
            def _(dve):
                link = chained(dve, chain)
                link(dve.memset(none[:], 0.0))
                link(dve.memset(zero[:], 0.0))
                link(dve.tensor_copy(key_i[:, 0, :], dst))
                link(dve.tensor_scalar(key_i[:, 1, :], key_i[:, 0, :], P - 1, None, ALU.bitwise_and))
                link(dve.tensor_scalar(key_i[:, 2, :], key_i[:, 0, :], 7, None, ALU.arith_shift_right))
                link(dve.tensor_copy(low[:], key_i[:, 1, :]))
                link(dve.tensor_copy(high[:], key_i[:, 2, :]))
                with dve.Fori(0, cols // IT) as i:
                    for h in range(2):
                        dve.wait_ge(*M.at(f"count{h}", i - 1))
                        c = i * IT + h * U
                        low_one_hots(dve, G, low, ohl[:, h], c).then_inc(*V.step(f"low{h}"))
                        dve.tensor_tensor(ohh[:, h], G.iota[:, 0:NT].unsqueeze(1).broadcast_to([P, U, NT]),
                                          high[:, bass.ds(c, U)].unsqueeze(2).broadcast_to([P, U, NT]),
                                          ALU.is_equal).then_inc(*V.step(f"high{h}"))
                dve.wait_ge(counted, 1)
                link(dve.tensor_copy(count[:], counts))
                dve.sem_inc(counted, 1)
                dve.wait_ge(summed, 1)
                link(dve.tensor_scalar(whole[:, 0, :], sums[:, 1, :], float(P - 1), None, ALU.add))
                link(dve.tensor_copy(whole_i[:], whole[:, 0, :]))
                link(dve.tensor_scalar(whole_i[:], whole_i[:], 7, None, ALU.arith_shift_right))
                link(dve.tensor_copy(whole[:, 0, :], whole_i[:]))
                link(dve.tensor_tensor_scan(whole[:, 1, :], zero[:], whole[:, 0, :], 0.0, ALU.add, ALU.add))
                link(dve.tensor_tensor(whole[:, 2, :], whole[:, 1, :], whole[:, 0, :], ALU.subtract))
                link(dve.scalar_tensor_tensor(start[:], whole[:, 2, :], float(P), sums[:, 0, :], ALU.mult, ALU.add))
                dve.wait_ge(numbered, 1)
                link(dve.tensor_tensor(after[:], chunk[:].unsqueeze(2).broadcast_to([P, ch, NT - 1]),
                                       whole[:, 1, 0:NT - 1].unsqueeze(1).broadcast_to([P, ch, NT - 1]), ALU.is_ge))
                link(dve.tensor_reduce(X.tile_of[:], after[:], AX.X, ALU.add))
                link(dve.tensor_copy(X.tile[:], X.tile_of[:]))

            @block.tensor
            def _(pe):
                pe.wait_ge(chain, 1)
                pe.matmul(counts, none[:], none[:, 0:NT], start=True, stop=False)
                with pe.Fori(0, cols // IT) as i:
                    for h in range(2):
                        pe.wait_ge(*V.at(f"high{h}", i))
                        for u in range(U):
                            ins = pe.matmul(counts, ohl[:, h, u, :], ohh[:, h, u, :], start=False, stop=False)
                        ins.then_inc(*M.step(f"count{h}"))
                pe.matmul(counts, none[:], none[:, 0:NT], start=False, stop=True).then_inc(counted, 1)
                pe.wait_ge(counted, 2)
                pe.matmul(sums[:, 0, :], G.earlier[:], count[:], start=True, stop=True)
                pe.matmul(sums[:, 1, :], G.ones[:], count[:], start=True, stop=True).then_inc(summed, 1)


def low_one_hots(dve, G, low, oh, c):
    return dve.tensor_tensor(oh, G.iota[:].unsqueeze(1).broadcast_to([P, U, P]),
                             low[:, bass.ds(c, U)].unsqueeze(2).broadcast_to([P, U, P]), ALU.is_equal)


def place_edges(nc, G, tag, cols, words, rec, low, high, start, dram, meanwhile=None):
    NH = NT + 1
    with ExitStack() as ctx:
        L = Kit(nc, ctx, tag)
        row = L.sb("row", [P, IT, words])
        to = L.sb("to", [P, 2, U], I32)
        dst = L.sb("dst", [P, 2, U])
        parts = L.sb("parts", [P, 2, 2, U], BF16)
        ident128 = L.sb("ident128", [P, P], BF16)
        ohl = L.sb("ohl", [P, 2, U, P], BF16)
        ohT = L.sb("ohT", [P, 2, U, P])
        ohh = L.sb("ohh", [P, 2, U, NH], BF16)
        same = L.sb("same", [P, 2, U, P], BF16)
        oneb = L.sb("oneb", [P, 1], BF16)
        run = L.sb("run", [P, 2, U, NT])
        part = L.sb("part", [P, 2, U, NH])
        pos = L.sb("pos", [P, 2, U])
        spread_dst = [L.ps(f"spread_dst{h}", [P, U, P]) for h in range(2)]
        turn = [L.ps(f"turn{h}", [P, U, P], BF16) for h in range(2)]
        hist = [L.ps(f"hist{h}", [P, U, NT]) for h in range(2)]
        mine = [L.ps(f"mine{h}", [P, U, NH]) for h in range(2)]
        sent, before = L.row_sems(cols // IT)
        took, ready = L.sem("took"), L.sem("ready")
        V = L.steps("dve_place", "same1 part0 pos0 to0 next_low0 next_high0 run1 "
                    "next_same0 part1 pos1 to1 next_low1 next_high1 next_run0", lead=10)
        A = L.steps("act_staged", "next_dst0 row0 next_T0 next_dst1 row1 next_T1", lead=6)
        M = L.steps("pe_place", "next_spread0 next_tr0 next_hist0 mine1 next_spread1 next_tr1 next_hist1 next_mine0",
                    lead=8)
        n = cols // IT
        with nc.Block() as block:
            @block.sync
            def _(sp):
                L.open(sp)
                if meanwhile:
                    meanwhile(sp, L.sem("other_loads"))

            @block.gpsimd
            def _(pool):
                with pool.Fori(0, n) as i:
                    for h in range(2):
                        pool.wait_ge(*A.at(f"row{h}", i))
                        pool.sem_inc(took, 1)
                        pool.wait_ge(*V.at(f"to{h}", i))
                        pool.sem_inc(took, 1)
                        for u in range(U):
                            pool.indirect_dma_start(
                                out=dram, out_offset=bass.IndirectOffsetOnAxis(ap=to[:, h, u:u + 1], axis=0),
                                in_=row[:, h * U + u, :], in_offset=None).then_inc(sent[h * U + u], 16)
                for u in range(IT):
                    pool.wait_ge(sent[u], 16 * n + before)

            @block.scalar
            def _(act):
                def dst_of(h, i):
                    act.wait_ge(*M.half("spread#", h, i - 1))
                    act.wait_ge(*V.half("same#", h, i - 1))
                    c = bass.ds(i * IT + h * U, U)
                    act.copy(dst[:, h, :], rec[:, c, R_DST])
                    act.copy(parts[:, 0, h, :], low[:, c])
                    act.copy(parts[:, 1, h, :], high[:, c]).then_inc(*A.half_step("dst#", h))

                def turned(h, i):
                    act.wait_ge(*M.half("tr#", h, i))
                    act.wait_ge(*M.half("mine#", h, i - 1))
                    act.copy(ohT[:, h], turn[h]).then_inc(*A.half_step("T#", h))

                def records(h, i):
                    for u in range(U):
                        act.wait_ge(sent[h * U + u], i * 16 + before)
                    act.copy(row[:, h * U:(h + 1) * U, :],
                             rec[:, bass.ds(i * IT + h * U, U), :]).then_inc(*A.step(f"row{h}"))

                for h in range(2):
                    dst_of(h, 0)
                    act.wait_ge(*A.at(f"next_dst{h}", -1))
                    act.sem_inc(*A.skip(1))
                    turned(h, 0)
                with act.Fori(0, n - 1) as i:
                    for h in range(2):
                        dst_of(h, i + 1)
                        records(h, i)
                        turned(h, i + 1)
                for h in range(2):
                    act.wait_ge(*(A.at("row0", n - 1) if h else A.at("next_T1", n - 2)))
                    act.sem_inc(*A.skip(2 if h else 1))
                    records(h, n - 1)

            @block.vector
            def _(dve):
                def one_hots_of(h, i):
                    c = i * IT + h * U
                    dve.wait_ge(*M.half("hist#", h, i - 1))
                    low_one_hots(dve, G, low, ohl[:, h], c).then_inc(*V.step(f"next_low{h}"))
                    dve.wait_ge(*V.half("part#", h, i - 1))
                    dve.tensor_tensor(ohh[:, h, :, 0:NT], G.iota[:, 0:NT].unsqueeze(1).broadcast_to([P, U, NT]),
                                      high[:, bass.ds(c, U)].unsqueeze(2).broadcast_to([P, U, NT]),
                                      ALU.is_equal).then_inc(*V.step(f"next_high{h}"))

                def same_of(h, i):
                    dve.wait_ge(*M.half("spread#", h, i))
                    dve.wait_ge(*M.half("mine#", h, i - 1))
                    for u in range(U):
                        ins = dve.scalar_tensor_tensor(same[:, h, u, :], spread_dst[h][:, u, :], dst[:, h, u:u + 1],
                                                       G.earlier[:], ALU.is_equal, ALU.mult)
                    ins.then_inc(*V.half_step("same#", h))

                def add_runs(h, i):
                    dve.wait_ge(*M.half("hist#", h, i))
                    dve.wait_ge(*M.half("mine#", 1 - h, i if h else i - 1))
                    dve.wait_ge(*V.half("run#", 1 - h, i if h else i - 1))
                    dve.tensor_tensor(run[:, h], hist[h], run[:, 1 - h, U - 1:U, :].broadcast_to([P, U, NT]),
                                      ALU.add).then_inc(*V.half_step("run#", h))

                def positions(h, i):
                    dve.wait_ge(*M.half("mine#", h, i))
                    dve.tensor_tensor(part[:, h], mine[h], ohh[:, h], ALU.mult).then_inc(*V.half_step("part#", h))
                    dve.wait_ge(*V.half("part#", h, i))
                    dve.wait_ge(*V.at(f"to{h}", i - 1))
                    dve.tensor_reduce(pos[:, h], part[:, h], AX.X, ALU.add).then_inc(*V.half_step("pos#", h))

                def targets(h, i):
                    dve.wait_ge(*V.half("pos#", h, i))
                    for u in range(U):
                        dve.wait_ge(sent[h * U + u], i * 16 + before)
                    dve.tensor_copy(to[:, h], pos[:, h]).then_inc(*V.step(f"to{h}"))

                dve.memset(oneb[:], 1.0).then_inc(ready, 1)
                dve.tensor_scalar(ident128[:], G.ident[:], float(P), None, ALU.mult).then_inc(ready, 1)
                dve.memset(ohh[:, :, :, NT:NH], 1.0).then_inc(ready, 1)
                dve.tensor_copy(run[:, 1, U - 1, :], start[:]).then_inc(ready, 1)
                dve.wait_ge(ready, 4)
                def left_out(name, i, count):
                    dve.wait_ge(*V.at(name, i))
                    dve.sem_inc(*V.skip(count))

                one_hots_of(0, 0)
                left_out("next_high0", -1, 1)
                same_of(0, 0)
                left_out("next_same0", -1, 3)
                one_hots_of(1, 0)
                add_runs(0, 0)
                with dve.Fori(0, n - 1) as i:
                    same_of(1, i)
                    positions(0, i)
                    targets(0, i)
                    one_hots_of(0, i + 1)
                    add_runs(1, i)
                    same_of(0, i + 1)
                    positions(1, i)
                    targets(1, i)
                    one_hots_of(1, i + 1)
                    add_runs(0, i + 1)
                same_of(1, n - 1)
                positions(0, n - 1)
                targets(0, n - 1)
                left_out("to0", n - 1, 2)
                add_runs(1, n - 1)
                left_out("run1", n - 1, 1)
                positions(1, n - 1)
                targets(1, n - 1)

            @block.tensor
            def _(pe):
                def spread_and_count(h, i):
                    pe.wait_ge(*A.half("dst#", h, i))
                    pe.wait_ge(*V.half("same#", h, i - 1))
                    for u in range(U):
                        for q, factor in enumerate((G.identb, ident128)):
                            ins = pe.matmul(spread_dst[h][:, u, :], parts[:, q, h, u:u + 1].broadcast_to([P, P]),
                                            factor[:], start=(q == 0), stop=(q == 1))
                    ins.then_inc(*M.half_step("spread#", h))
                    pe.wait_ge(*V.half("low#", h, i))
                    pe.wait_ge(*A.half("T#", h, i - 1))
                    for u in range(U):
                        ins = pe.transpose(turn[h][:, u, :], ohl[:, h, u, :], G.identb[:])
                    ins.then_inc(*M.half_step("tr#", h))
                    pe.wait_ge(*V.half("high#", h, i))
                    pe.wait_ge(*V.half("run#", h, i - 1))
                    for u in range(U):
                        for q in range(u + 1):
                            ins = pe.matmul(hist[h][:, u, :], ohl[:, h, q, :], ohh[:, h, q, 0:NT],
                                            start=(q == 0), stop=(q == u))
                    ins.then_inc(*M.half_step("hist#", h))

                def look_up(h, i):
                    pe.wait_ge(*A.half("T#", h, i))
                    pe.wait_ge(*V.half("part#", h, i - 1))
                    pe.wait_ge(*V.half("same#", h, i))
                    pe.wait_ge(*V.half("run#", h, i))
                    for u in range(U):
                        pe.matmul(mine[h][:, u, 0:NT], ohT[:, h, u, :],
                                  run[:, h, u - 1, :] if u else run[:, 1 - h, U - 1, :], start=True, stop=True)
                        ins = pe.matmul(mine[h][:, u, NT:NH], same[:, h, u, :], oneb[:], start=True, stop=True)
                    ins.then_inc(*M.half_step("mine#", h))

                pe.wait_ge(ready, 4)
                spread_and_count(0, 0)
                pe.wait_ge(*M.at("next_hist0", -1))
                pe.sem_inc(*M.skip(1))
                spread_and_count(1, 0)
                look_up(0, 0)
                with pe.Fori(0, n - 1) as i:
                    spread_and_count(0, i + 1)
                    look_up(1, i)
                    spread_and_count(1, i + 1)
                    look_up(0, i + 1)
                pe.wait_ge(*M.at("next_mine0", n - 2))
                pe.sem_inc(*M.skip(3))
                look_up(1, n - 1)


def sort_edges(nc, G, tag, cols, words, rec, dram, X, meanwhile=None):
    with ExitStack() as ctx:
        L = Kit(nc, ctx, tag)
        low = L.sb("low", [P, cols])
        high = L.sb("high", [P, cols])
        start = L.sb("start", [P, NT])
        count_edges(nc, G, tag + "n", cols, rec[:, :, R_DST], low, high, start, X)
        place_edges(nc, G, tag + "p", cols, words, rec, low, high, start, dram, meanwhile)


def pad_rows(sp, stored, padrow, dram, rows, before=0):
    step = padrow.shape[1] * P
    for r in range(0, rows, step):
        sp.dma_start(dram[r:r + step, :].rearrange("(p c) w -> p c w", p=P), padrow[:]).then_inc(stored, 16)
        before += 16
        sp.wait_ge(stored, before)


class GraphRecords:

    def __init__(self, nc, K, I, dram):
        self.nc, self.I, self.dram = nc, I, dram
        self.rec = K.sb("rec", [P, EJ, REC])
        self.ints = K.sb("ints", [P, 3, EJ], I32)
        self.scal = K.sb("scal", [P, 2, EJ])
        self.attr = K.sb("attr", [P, EJ, 3])
        self.padrow = K.sb("padrow", [P, 32, REC])

    def prepare(self, tag, others):
        tail = EJ - (P * EJ - E)
        with ExitStack() as ctx:
            L = Kit(self.nc, ctx, tag)
            cleared = L.sem("cleared")
            with self.nc.Block() as block:
                @block.vector
                def _(dve):
                    link = chained(dve, cleared)
                    link(dve.memset(self.rec[96:P, tail:, :], 0.0))
                    for a in (self.scal, self.attr):
                        link(dve.memset(a[:], 0.0))
                    link(dve.memset(self.ints[:], 0))
                    link(dve.memset(self.ints[:, 1, :], PAD))
                    link(dve.memset(self.rec[:, :, R_ONE:R_ONE + 1], 1.0))
                    for row in (self.padrow, others):
                        link(dve.memset(row[:], 0.0))
                        link(dve.memset(row[:, :, R_DST:R_DST + 1], float(PAD)))

    def load(self, sp, loaded):
        I, ints, scal = self.I, self.ints, self.scal
        full = E // EJ
        rest = E - full * EJ
        for f, name in ((0, "src"), (1, "dst"), (2, "edge_type_16")):
            a = I[name]
            sp.dma_start(ints[0:full, f, :], a[0:full * EJ].rearrange("(p j) -> p j", j=EJ)).then_inc(loaded, 16)
            sp.dma_start(ints[full:full + 1, f, 0:rest],
                         a[full * EJ:E].rearrange("(p j) -> p j", j=rest)).then_inc(loaded, 16)
        for f, a in ((0, I["edge_weight"]), (1, I["edge_weight1"].rearrange("e w -> (e w)"))):
            sp.dma_start(scal[0:full, f, :], a[0:full * EJ].rearrange("(p j) -> p j", j=EJ)).then_inc(loaded, 16)
            sp.dma_start(scal[full:full + 1, f, 0:rest],
                         a[full * EJ:E].rearrange("(p j) -> p j", j=rest)).then_inc(loaded, 16)
        for a, to in ((I["edge_attr_3"], self.attr[:]), (I["edge_attr_64"], self.rec[:, :, R_EA:REC])):
            sp.dma_start(to[full:full + 1, 0:rest],
                         a[full * EJ:E, :].rearrange("(p j) w -> p j w", j=rest)).then_inc(loaded, 16)
        sp.dma_start(self.attr[0:full],
                     I["edge_attr_3"][0:full * EJ, :].rearrange("(p j) w -> p j w", j=EJ)).then_inc(loaded, 16)
        count = 16 * 13
        long = I["edge_attr_64"][0:full * EJ, :].rearrange("(p j) w -> p j w", j=EJ)
        for j in range(0, EJ, EJ // 8):
            sp.dma_start(self.rec[0:full, j:j + EJ // 8, R_EA:REC], long[:, j:j + EJ // 8, :]).then_inc(loaded, 16)
            count += 16
            sp.wait_ge(loaded, count)
        pad_rows(sp, loaded, self.padrow, self.dram, self.dram.shape[0], count)

    def convert(self, tag):
        rec = self.rec
        with ExitStack() as ctx:
            L = Kit(self.nc, ctx, tag)
            ready = L.sem("ready")
            with self.nc.Block() as block:
                @block.vector
                def _(dve):
                    for f, row in ((0, R_SRC), (1, R_DST), (2, R_TYPE)):
                        dve.tensor_copy(rec[:, :, row], self.ints[:, f, :]).then_inc(ready, 1)
                    dve.tensor_copy(rec[:, :, R_EW], self.scal[:, 0, :]).then_inc(ready, 1)
                    dve.tensor_copy(rec[:, :, R_EW1], self.scal[:, 1, :]).then_inc(ready, 1)
                    dve.tensor_copy(rec[:, :, R_EA3:R_EA3 + 3], self.attr[:]).then_inc(ready, 1)


def fill_router(nc, G, I, rec, padrow, dram):
    cols = FE // P
    with ExitStack() as ctx:
        L = Kit(nc, ctx, "fr")
        ints = L.sb("ints", [P, 2, cols], I32)
        loaded = L.sem("loaded")
        stored = L.sem("stored")
        ready = L.sem("ready")
        with nc.Block() as block:
            @block.vector
            def _(dve):
                dve.memset(rec[:, cols + NT:, :], float(PAD)).then_inc(ready, 1)
                for f in range(2):
                    for t in range(NT):
                        dve.tensor_scalar(rec[:, cols + t, f:f + 1], G.part[:, 0:1], float(t * P), None,
                                          ALU.add).then_inc(ready, 1)
                dve.wait_ge(loaded, 32)
                for f in range(2):
                    dve.tensor_copy(rec[:, 0:cols, f], ints[:, f, :]).then_inc(ready, 1)

            @block.sync
            def _(sp):
                for f in range(2):
                    sp.dma_start(ints[:, f, :], I["L0_ffn_edge_index"][f, :].rearrange(
                        "(p j) -> p j", j=cols)).then_inc(loaded, 16)
                pad_rows(sp, stored, padrow, dram, P * FNC)


class Globals:
    pass


class Edges:

    def __init__(self, K, tag, chunks):
        self.chunks = chunks
        self.tile_of = K.sb(tag + "tile_of", [P, chunks])
        self.tile = K.sb(tag + "tile", [P, chunks], I32)
        self.src = K.sb(tag + "src", [P, chunks], I32)
        self.dst = K.sb(tag + "dst", [P, chunks])
        self.local = K.sb(tag + "local", [P, chunks])


def load_edges(nc, tag, X, rows, words, small=None):
    with ExitStack() as ctx:
        L = Kit(nc, ctx, tag)
        ch = X.chunks
        w = 8 if small is not None else words
        part = L.sb("part", [P, ch, w]) if small is None else small
        loaded = L.sem("loaded")
        chain = L.sem("chain")
        with nc.Block() as block:
            @block.sync
            def _(sp):
                with nc.allow_non_contiguous_dma(reason="fields of records"):
                    sp.dma_start(part[:, :, 0:w] if small is None else part[:],
                                 rows.rearrange("(c p) w -> p c w", p=P)[:, :, 0:(w if small is None else 9)]
                                 ).then_inc(loaded, 16)

            @block.vector
            def _(dve):
                dve.wait_ge(loaded, 16)
                dve.tensor_copy(X.src[:], part[:, :, R_SRC]).then_inc(chain, 1)
                dve.tensor_copy(X.dst[:], part[:, :, R_DST]).then_inc(chain, 1)
                dve.wait_ge(chain, 2)
                dve.scalar_tensor_tensor(X.local[:], X.tile_of[:], -float(P), X.dst[:], ALU.mult,
                                         ALU.add).then_inc(chain, 1)


GT = 5
NG = NT // GT


class Norm:

    def __init__(self, L, G, affine=None, relu_of=None):
        self.G, self.affine, self.relu_of = G, affine, relu_of
        self.stats = L.sb("n_stats", [P, GT, 6])
        self.mv = L.sb("n_mv", [P, GT, 2])
        self.rstd = L.sb("n_rstd", [P, GT])
        self.std = L.sb("n_std", [P, GT])
        self.xn = L.sb("n_xn", [P, GT, D])
        self.raw = L.sb("n_raw", [P, GT, D]) if affine else None
        self.xT = L.sb("n_xT", [P, 2, GT * P])
        self.tr = [L.ps(f"n_tr{s}", [P, 2, P]) for s in range(2)]
        self.took = L.sem("n_took")
        self.V = L.steps("dve_norm", "norm" if relu_of is not None else "stats aggr eps rstd norm" + (" stats2 aggr2 eps2 rstd2 norm2 gamma beta" if affine else ""))
        self.Q = L.steps("act_std", "std" + (" std2" if affine else ""))
        self.T = L.steps("pe_turned", "tr0 tr1 tr2 tr3 tr4")
        self.C = L.steps("act_turned", "cp0 cp1 cp2 cp3 cp4")
        self.last = "beta" if affine else "norm"

    def dve(self, dve, i, xn_free=()):
        V, Q, G = self.V, self.Q, self.G
        dve.wait_ge(*V.ended(i))
        if self.relu_of is not None:
            dve.wait_ge(*self.T.ended(i))
            for w in xn_free:
                dve.wait_ge(*w)
            dve.tensor_scalar(self.xn[:], self.relu_of[:, bass.ds(i * GT, GT), :], 0.0, None,
                              ALU.max).then_inc(*V.step("norm"))
            return
        for u in range(GT):
            ins = dve.bn_stats(self.stats[:, u, :], G.x[:, bass.ds(i * GT + u, 1), :].rearrange("p a d -> p (a d)"))
        ins.then_inc(*V.step("stats"))
        dve.wait_ge(*V.at("stats", i))
        dve.sem_inc(self.took, 1)
        for u in range(GT):
            ins = dve.bn_aggr(self.mv[:, u, :], self.stats[:, u, :])
        ins.then_inc(*V.step("aggr"))
        dve.wait_ge(*V.at("aggr", i))
        dve.tensor_scalar(self.rstd[:], self.mv[:, :, 1], EPS, None, ALU.add).then_inc(*V.step("eps"))
        dve.wait_ge(*Q.at("std", i))
        dve.reciprocal(self.rstd[:], self.std[:]).then_inc(*V.step("rstd"))
        dve.wait_ge(*V.at("rstd", i))
        dve.wait_ge(*self.T.ended(i))
        for w in xn_free:
            dve.wait_ge(*w)
        to = self.raw if self.affine else self.xn
        for u in range(GT):
            ins = dve.tensor_scalar(to[:, u, :], G.x[:, bass.ds(i * GT + u, 1), :].rearrange("p a d -> p (a d)"),
                                    self.mv[:, u, 0:1], self.rstd[:, u:u + 1], ALU.subtract, ALU.mult)
        ins.then_inc(*V.step("norm"))
        if self.affine:
            gamma, beta = self.affine
            dve.wait_ge(*V.at("norm", i))
            for u in range(GT):
                ins = dve.bn_stats(self.stats[:, u, :], self.raw[:, u, :])
            ins.then_inc(*V.step("stats2"))
            dve.wait_ge(*V.at("stats2", i))
            dve.sem_inc(self.took, 1)
            for u in range(GT):
                ins = dve.bn_aggr(self.mv[:, u, :], self.stats[:, u, :])
            ins.then_inc(*V.step("aggr2"))
            dve.wait_ge(*V.at("aggr2", i))
            dve.tensor_scalar(self.rstd[:], self.mv[:, :, 1], EPS, None, ALU.add).then_inc(*V.step("eps2"))
            dve.wait_ge(*Q.at("std2", i))
            dve.reciprocal(self.rstd[:], self.std[:]).then_inc(*V.step("rstd2"))
            dve.wait_ge(*V.at("rstd2", i))
            for u in range(GT):
                ins = dve.tensor_scalar(self.raw[:, u, :], self.raw[:, u, :], self.mv[:, u, 0:1],
                                        self.rstd[:, u:u + 1], ALU.subtract, ALU.mult)
            ins.then_inc(*V.step("norm2"))
            dve.wait_ge(*V.at("norm2", i))
            dve.tensor_tensor(self.raw[:], self.raw[:], gamma[:].unsqueeze(1).broadcast_to([P, GT, D]),
                              ALU.mult).then_inc(*V.step("gamma"))
            dve.wait_ge(*V.at("gamma", i))
            dve.tensor_tensor(self.xn[:], self.raw[:], beta[:].unsqueeze(1).broadcast_to([P, GT, D]),
                              ALU.add).then_inc(*V.step("beta"))

    def pe(self, pe, i):
        pe.wait_ge(*self.V.at(self.last, i))
        pe.wait_ge(*self.C.ended(i))
        for u in range(GT):
            if u >= 2:
                pe.wait_ge(*self.C.at(f"cp{u - 2}", i))
            for k in range(2):
                ins = pe.transpose(self.tr[u % 2][:, k, :], self.xn[:, u, k * P:(k + 1) * P], self.G.ident[:])
            ins.then_inc(*self.T.step(f"tr{u}"))

    def act(self, act, i, xT_free):
        for n in () if self.relu_of is not None else ("", "2") if self.affine else ("",):
            act.wait_ge(*self.V.at("eps" + n, i))
            act.activation(self.std[:], self.rstd[:], ACT.Sqrt).then_inc(*self.Q.step("std" + n))
        act.wait_ge(*xT_free)
        for u in range(GT):
            act.wait_ge(*self.T.at(f"tr{u}", i))
            act.copy(self.xT[:, :, u * P:(u + 1) * P], self.tr[u % 2]).then_inc(*self.C.step(f"cp{u}"))


def rows_of(dram, i):
    return dram.rearrange("(t p) w -> p t w", p=P)[:, bass.ds(i * GT, GT), :]


def spread(a, n):
    return a.rearrange("(o n) -> o n", o=1).broadcast_to([P, n])


def gat_nodes(nc, G, I, tag, W, Wres, att_l, att_r, table, al_dram, ar, keep=None, transposed=False):
    H, C = 8, 32
    with ExitStack() as ctx:
        L = Kit(nc, ctx, tag)
        nrm = Norm(L, G)
        wide = 2 * D if Wres is not None else D
        w = L.sb("w", [P, 2, wide])
        wn = L.sb("wn", [P, 2, D]) if transposed else None
        att = L.sb("att", [P, 2, D])
        tab = L.sb("tab", [P, GT, D])
        prod = L.sb("prod", [P, GT, D])
        al = L.sb("al", [P, GT, H])
        y = [L.ps(f"y{s}", [P, 512]) for s in range(2)]
        loaded = L.sem("loaded")
        turned = L.sem("turned")
        wready = L.sem("wready")
        stored = L.sem("stored")
        M = L.steps("pe_h", "mm0 mm1 mm2 mm3 mm4")
        A = L.steps("act_h", "tab0 tab1 tab2 tab3 tab4")
        V = L.steps("dve_h", ("res0 res1 res2 res3 res4 " if Wres is not None else "") + "pl al pr ar")

        def rows(i):
            return keep[:, bass.ds(i * GT, GT), 0:D] if keep is not None else tab[:]

        with nc.Block() as block:
            @block.sync
            def _(sp):
                L.open(sp)
                sp.sem_inc(turned, 1)
                sp.dma_start((wn if transposed else w)[:, :, 0:D], W.rearrange("(k p) n -> p k n", p=P)).then_inc(loaded, 16)
                if Wres is not None:
                    sp.dma_start(w[:, :, D:2 * D], Wres.rearrange("(k p) n -> p k n", p=P)).then_inc(loaded, 16)
                sp.dma_start(att[:, 0, :], spread(att_l, D)).then_inc(loaded, 16)
                sp.dma_start(att[:, 1, :], spread(att_r, D)).then_inc(loaded, 16)
                with sp.Fori(0, NG) as i:
                    sp.wait_ge(*V.at("al", i))
                    sp.dma_start(rows_of(table, i), rows(i)).then_inc(stored, 16)
                    sp.dma_start(rows_of(al_dram, i), al[:]).then_inc(stored, 16)
                    sp.wait_ge(stored, i * 32 + 32)
                    sp.sem_inc(turned, 1)

            @block.vector
            def _(dve):
                if transposed:
                    dve.wait_ge(wready, 2)
                    for k in range(2):
                        for n in range(2):
                            ins = dve.tensor_copy(w[:, k, n * P:(n + 1) * P], y[k][:, n * P:(n + 1) * P])
                    ins.then_inc(wready, 1)
                dve.wait_ge(loaded, 64 if Wres is not None else 48)
                with dve.Fori(0, NG) as i:
                    nrm.dve(dve, i)
                    if Wres is not None:
                        for u in range(GT):
                            dve.wait_ge(*M.at(f"mm{u}", i))
                            xt = G.x[:, bass.ds(i * GT + u, 1), :].rearrange("p a d -> p (a d)")
                            dve.tensor_tensor(xt, xt, y[u % 2][:, D:2 * D], ALU.add).then_inc(*V.step(f"res{u}"))
                    dve.wait_ge(*V.ended(i))
                    dve.wait_ge(*A.at("tab4", i))
                    dve.wait_ge(turned, i + 1)
                    dve.tensor_tensor(prod[:], rows(i), att[:, 0, :].unsqueeze(1).broadcast_to([P, GT, D]),
                                      ALU.mult).then_inc(*V.step("pl"))
                    dve.wait_ge(*V.at("pl", i))
                    dve.tensor_reduce(al[:], prod[:].rearrange("p t (h c) -> p t h c", h=H), AX.X,
                                      ALU.add).then_inc(*V.step("al"))
                    dve.wait_ge(*V.at("al", i))
                    dve.tensor_tensor(prod[:], rows(i), att[:, 1, :].unsqueeze(1).broadcast_to([P, GT, D]),
                                      ALU.mult).then_inc(*V.step("pr"))
                    dve.wait_ge(*V.at("pr", i))
                    dve.tensor_reduce(ar(i), prod[:].rearrange("p t (h c) -> p t h c", h=H), AX.X,
                                      ALU.add).then_inc(*V.step("ar"))

            @block.scalar
            def _(act):
                with act.Fori(0, NG) as i:
                    nrm.act(act, i, M.ended(i))
                    if keep is None:
                        act.wait_ge(turned, i + 1)
                        act.wait_ge(*V.ended(i))
                    for u in range(GT):
                        act.wait_ge(*(M.at(f"mm{u}", i) if Wres is None else V.at(f"res{u}", i)))
                        to = tab[:, u, :] if keep is None else keep[:, bass.ds(i * GT + u, 1), 0:D].rearrange("p a d -> p (a d)")
                        act.copy(to, y[u % 2][:, 0:D]).then_inc(*A.step(f"tab{u}"))

            @block.tensor
            def _(pe):
                pe.wait_ge(loaded, 64 if Wres is not None else 48)
                if transposed:
                    for k in range(2):
                        for n in range(2):
                            ins = pe.transpose(y[k][:, n * P:(n + 1) * P], wn[:, n, k * P:(k + 1) * P], G.ident[:])
                        ins.then_inc(wready, 1)
                    pe.wait_ge(wready, 3)
                with pe.Fori(0, NG) as i:
                    nrm.pe(pe, i)
                    pe.wait_ge(*A.ended(i))
                    for u in range(GT):
                        pe.wait_ge(*nrm.C.at(f"cp{u}", i))
                        if u >= 2:
                            pe.wait_ge(*A.at(f"tab{u - 2}", i))
                        for k in range(2):
                            ins = pe.matmul(y[u % 2][:, 0:wide], nrm.xT[:, k, u * P:(u + 1) * P], w[:, k, :],
                                            start=(k == 0), stop=(k == 1))
                        ins.then_inc(*M.step(f"mm{u}"))


def tiles_of(nc, eng, X, c, count=IT):
    return nc.values_load_multi_w_load_instructions(
        X.tile[0:1, bass.ds(c, count)], engines=[eng.engine], min_val=0, max_val=NT - 1,
        skip_runtime_bounds_check_because="a chunk's tile counts how many of NT - 1 compares hold")[1]


def one_hots(dve, G, X, oh, c, chunks=U, scale=None):
    return dve.tensor_tensor(oh, G.iota[:].unsqueeze(1).broadcast_to([P, chunks, P]),
                             X.local[:, bass.ds(c, chunks)].unsqueeze(2).broadcast_to([P, chunks, P]), ALU.is_equal)


def attention_pass(nc, G, tag, X, H, al_dram, width, al_at, ar, alpha, weight=None, keep=None):
    with ExitStack() as ctx:
        L = Kit(nc, ctx, tag)
        row = L.sb("row", [P, IT, width])
        at = L.sb("at", [P, 2, U], I32)
        oh = L.sb("oh", [P, 2, U, P])
        ohT = L.sb("ohT", [P, 2, U * P])
        s = L.sb("s", [P, 2, U, H])
        turn = [L.ps(f"turn{h}", [P, U, P]) for h in range(2)]
        atdst = [L.ps(f"atdst{h}", [P, U, H]) for h in range(2)]
        got, before = L.row_sems(X.chunks // IT)
        took = L.sem("took")
        own = " ".join(f"sum{h} " + (f"w{h} " if weight is not None else "") + f"alpha{h}" for h in range(2))
        V = L.steps("dve_alpha", "next_oh0 next_oh1 " + own, lead=2 + len(own.split()))
        A = L.steps("act_turned", "keep0 next_at0 keep1 next_at1 next_T0 next_T1" if keep is not None else
                    "next_at0 next_at1 next_T0 next_T1", lead=5 if keep is not None else 4)
        M = L.steps("pe_dst", "dst0 dst1 next_tr0 next_tr1", lead=2)
        n = X.chunks // IT
        with nc.Block() as block:
            @block.sync
            def _(sp):
                L.open(sp)

            @block.gpsimd
            def _(pool):
                with pool.Fori(0, n) as i:
                    for h in range(2):
                        pool.wait_ge(*A.at(f"next_at{h}", i - 1))
                        pool.sem_inc(took, 1)
                        for u in range(U):
                            pool.indirect_dma_start(
                                out=row[:, h * U + u, :], out_offset=None, in_=al_dram,
                                in_offset=bass.IndirectOffsetOnAxis(ap=at[:, h, u:u + 1], axis=0)
                            ).then_inc(got[h * U + u], 16)

            @block.scalar
            def _(act):
                def indices(h, i):
                    act.wait_ge(*V.at(f"sum{h}", i - 1))
                    if keep is not None:
                        act.wait_ge(*A.at(f"keep{h}", i - 1))
                    act.copy(at[:, h, :], X.src[:, bass.ds(i * IT + h * U, U)]).then_inc(*A.step(f"next_at{h}"))

                def turned(i):
                    for h in range(2):
                        act.wait_ge(*M.at(f"next_tr{h}", i - 1))
                        act.wait_ge(*M.at(f"dst{h}", i - 1))
                        act.copy(ohT[:, h, :], turn[h][:].rearrange("p u e -> p (u e)")).then_inc(*A.step(f"next_T{h}"))

                def kept(h, i):
                    for u in range(U):
                        act.wait_ge(got[h * U + u], i * 16 + (16 + before))
                    act.copy(keep[:, bass.ds(i * IT + h * U, U), :],
                             row[:, h * U:(h + 1) * U, 0:al_at]).then_inc(*A.step(f"keep{h}"))

                indices(0, 0)
                if keep is not None:
                    act.wait_ge(*A.at("next_at0", -1))
                    act.sem_inc(*A.skip(1))
                indices(1, 0)
                turned(0)
                with act.Fori(0, n - 1) as i:
                    for h in range(2):
                        if keep is not None:
                            kept(h, i)
                        indices(h, i + 1)
                    turned(i + 1)
                if keep is not None:
                    kept(0, n - 1)
                    act.wait_ge(*A.at("keep0", n - 1))
                    act.sem_inc(*A.skip(1))
                    kept(1, n - 1)

            @block.vector
            def _(dve):
                def next_one_hots(i):
                    for h in range(2):
                        dve.wait_ge(*M.at(f"next_tr{h}", i - 2))
                        one_hots(dve, G, X, oh[:, h], i * IT + h * U).then_inc(*V.step(f"next_oh{h}"))

                def halves(i):
                    for h in range(2):
                        c = i * IT + h * U
                        for u in range(U):
                            dve.wait_ge(got[h * U + u], i * 16 + (16 + before))
                        dve.wait_ge(*M.at(f"dst{h}", i))
                        dve.wait_ge(*V.at(f"alpha{h}", i - 1))
                        dve.tensor_tensor(s[:, h], row[:, h * U:(h + 1) * U, al_at:al_at + H], atdst[h][:],
                                          ALU.add).then_inc(*V.step(f"sum{h}"))
                        if weight is not None:
                            dve.wait_ge(*V.at(f"sum{h}", i))
                            dve.tensor_tensor(s[:, h], s[:, h],
                                              weight[:, bass.ds(c, U)].unsqueeze(2).broadcast_to([P, U, H]),
                                              ALU.mult).then_inc(*V.step(f"w{h}"))
                        dve.wait_ge(*V.at(f"w{h}" if weight is not None else f"sum{h}", i))
                        flat = s[:, h].rearrange("p u h -> p (u h)")
                        dve.scalar_tensor_tensor(alpha[:, bass.ds(c, U), :].rearrange("p u h -> p (u h)"), flat, 0.2,
                                                 flat, ALU.mult, ALU.max).then_inc(*V.step(f"alpha{h}"))

                next_one_hots(0)
                dve.wait_ge(*V.at("next_oh1", -1))
                dve.sem_inc(*V.skip(len(own.split())))
                with dve.Fori(0, n - 1) as i:
                    next_one_hots(i + 1)
                    halves(i)
                dve.wait_ge(*V.at("alpha1", n - 2))
                dve.sem_inc(*V.skip(2))
                halves(n - 1)

            @block.tensor
            def _(pe):
                def turn_over(i):
                    for h in range(2):
                        pe.wait_ge(*V.at(f"next_oh{h}", i - 1))
                        pe.wait_ge(*A.at(f"next_T{h}", i - 2))
                        for u in range(U):
                            ins = pe.transpose(turn[h][:, u, :], oh[:, h, u, :], G.ident[:])
                        ins.then_inc(*M.step(f"next_tr{h}"))

                def to_edges(i):
                    for h in range(2):
                        pe.wait_ge(*A.at(f"next_T{h}", i - 1))
                        pe.wait_ge(*V.at(f"sum{h}", i - 1))
                        tiles = tiles_of(nc, pe, X, i * IT + h * U, U)
                        for u in range(U):
                            ins = pe.matmul(atdst[h][:, u, :], ohT[:, h, u * P:(u + 1) * P],
                                            ar[:, bass.ds(tiles[u], 1), :].rearrange("p a h -> p (a h)"),
                                            start=True, stop=True)
                        ins.then_inc(*M.step(f"dst{h}"))

                turn_over(0)
                with pe.Fori(0, n - 1) as i:
                    to_edges(i)
                    turn_over(i + 1)
                to_edges(n - 1)


def softmax_pass(nc, G, tag, X, H, alpha):
    S = P // H
    g = X.chunks // S
    W = g * P
    with ExitStack() as ctx:
        L = Kit(nc, ctx, tag)
        dst8 = L.sb("dst8", [P, X.chunks, H])
        slot = L.sb("slot", [P, 2, 2, P])
        aT = L.sb("aT", [P, W])
        dT = L.sb("dT", [P, W])
        cut = L.sb("cut", [P, W + 1])
        top = L.sb("top", [P, W])
        ends = L.sb("ends", [P, 4])
        rhs = L.sb("rhs", [P, 4, S])
        vk = L.sb("vk", [P, 4, S])
        hit = L.sb("hit", [P, 2, 2 * S])
        both = L.sb("both", [P, 2])
        key_i = L.sb("key_i", [P, 3, P], I32)
        keyf = L.sb("keyf", [P, 3, P])
        same = L.sb("same", [P, P])
        seg = L.sb("seg", [P, S])
        turn = [L.ps(f"turn{s}", [P, 2, P]) for s in range(2)]
        pj = L.ps("pj", [P, 4, S])
        bits = {8: 3, 4: 2}[H]
        chain = L.sem("chain")
        expd = L.sem("expd")
        joined = L.sem("joined")
        ready2 = L.sem("pool_out")
        M = L.steps("pe_in", "in0 in1")
        A = L.steps("act_in", "sa0 sd0 sa1 sd1")
        V = L.steps("dve_in", "a0 d0 a1 d1")
        M2 = L.steps("pe_out", "out0 out1")
        A2 = L.steps("act_out", "out0 out1")
        aview = alpha.rearrange("p (s g) h -> p g s h", g=g)
        dview = dst8[:].rearrange("p (s g) h -> p g s h", g=g)
        with nc.Block() as block:
            @block.sync
            def _(sp):
                L.open(sp)

            @block.vector
            def _(dve):
                k = [0]

                def link(ins):
                    k[0] += 1
                    ins.then_inc(chain, 1)
                    dve.wait_ge(chain, k[0])

                link(dve.tensor_copy(dst8[:], X.dst[:].unsqueeze(2).broadcast_to([P, X.chunks, H])))
                link(dve.tensor_copy(key_i[:, 0, :], G.iota[:]))
                link(dve.tensor_copy(key_i[:, 1, :], G.part[:, 0:1].broadcast_to([P, P])))
                link(dve.tensor_scalar(key_i[:, 2, :], key_i[:, 1, :], bits, None, ALU.arith_shift_right))
                link(dve.tensor_scalar(key_i[:, 0:2, :], key_i[:, 0:2, :], H - 1, None, ALU.bitwise_and))
                link(dve.tensor_copy(keyf[:], key_i[:]))
                link(dve.tensor_tensor(same[:], keyf[:, 0, :], keyf[:, 1, :], ALU.is_equal))
                link(dve.tensor_tensor(seg[:], G.iota[:, 0:S], keyf[:, 2, 0:S], ALU.is_equal))
                with dve.Fori(0, g // 2) as i:
                    for s in range(2):
                        dve.wait_ge(*M.at(f"in{s}", i))
                        dve.tensor_copy(aT[:, bass.ds((i * 2 + s) * P, P)], turn[s][:, 0, :]).then_inc(*V.step(f"a{s}"))
                        dve.tensor_copy(dT[:, bass.ds((i * 2 + s) * P, P)], turn[s][:, 1, :]).then_inc(*V.step(f"d{s}"))
                dve.wait_ge(*V.ended(g // 2))
                link(dve.memset(cut[:], 0.0))
                link(dve.tensor_tensor(cut[:, 1:W], dT[:, 1:W], dT[:, 0:W - 1], ALU.not_equal))
                link(dve.tensor_scalar(cut[:, 1:W], cut[:, 1:W], -BIG, None, ALU.mult))
                link(dve.tensor_tensor_scan(top[:], cut[:, 0:W], aT[:], -BIG, ALU.add, ALU.max))
                link(dve.tensor_tensor_scan(top[:, ::-1], cut[:, W:0:-1], top[:, ::-1], -BIG, ALU.add, ALU.max))
                link(dve.tensor_copy(ends[:, 0:1], top[:, 0:1]))
                link(dve.tensor_copy(ends[:, 1:2], top[:, W - 1:W]))
                link(dve.tensor_copy(ends[:, 2:3], dT[:, 0:1]))
                link(dve.tensor_copy(ends[:, 3:4], dT[:, W - 1:W]))
                for q in range(4):
                    link(dve.tensor_scalar(rhs[:, q, :], seg[:], ends[:, q:q + 1], None, ALU.mult))
                dve.wait_ge(joined, 1)
                link(dve.tensor_copy(vk[:], pj[:]))
                val = vk[:, 0:2, :].rearrange("p a s -> p (a s)")
                key = vk[:, 2:4, :].rearrange("p a s -> p (a s)")
                for q in range(2):
                    link(dve.tensor_scalar(hit[:, q, :], key, ends[:, 2 + q:3 + q], -BIG, ALU.not_equal, ALU.mult))
                    link(dve.tensor_tensor(hit[:, q, :], hit[:, q, :], val, ALU.add))
                    link(dve.tensor_reduce(both[:, q:q + 1], hit[:, q, :], AX.X, ALU.max))
                for q in range(2):
                    link(dve.tensor_scalar(cut[:, 0:W], dT[:], ends[:, 2 + q:3 + q], -BIG, ALU.not_equal, ALU.mult))
                    link(dve.scalar_tensor_tensor(top[:], cut[:, 0:W], both[:, q:q + 1], top[:], ALU.add, ALU.max))
                link(dve.tensor_tensor(aT[:], aT[:], top[:], ALU.subtract))
                dve.sem_inc(joined, 1)

            @block.scalar
            def _(act):
                act.wait_ge(chain, 1)
                with act.Fori(0, g // 2) as i:
                    for s in range(2):
                        act.wait_ge(*M.ended(i))
                        v = slot[:, s, 0, :].rearrange("p (s h) -> p s h", h=H)
                        w = slot[:, s, 1, :].rearrange("p (s h) -> p s h", h=H)
                        act.copy(v, aview[:, bass.ds(i * 2 + s, 1)].rearrange("p a s h -> p (a s) h")).then_inc(*A.step(f"sa{s}"))
                        act.copy(w, dview[:, bass.ds(i * 2 + s, 1)].rearrange("p a s h -> p (a s) h")).then_inc(*A.step(f"sd{s}"))
                act.wait_ge(joined, 2)
                act.activation(top[:], aT[:], ACT.Exp).then_inc(expd, 1)
                act.wait_ge(expd, 1)
                with act.Fori(0, g // 2) as i:
                    for s in range(2):
                        act.wait_ge(*M2.at(f"out{s}", i))
                        act.copy(aview[:, bass.ds(i * 2 + s, 1)].rearrange("p a s h -> p (a s) h"),
                                 turn[s][:, 0, :].rearrange("p (s h) -> p s h", h=H)).then_inc(*A2.step(f"out{s}"))

            @block.tensor
            def _(pe):
                with pe.Fori(0, g // 2) as i:
                    for s in range(2):
                        pe.wait_ge(*A.at(f"sd{s}", i))
                        pe.wait_ge(*V.ended(i))
                        pe.transpose(turn[s][:, 0, :], slot[:, s, 0, :], G.ident[:])
                        pe.transpose(turn[s][:, 1, :], slot[:, s, 1, :], G.ident[:]).then_inc(*M.step(f"in{s}"))
                pe.wait_ge(chain, 21)
                pe.matmul(pj[:], same[:], rhs[:], start=True, stop=True).then_inc(joined, 1)
                pe.wait_ge(expd, 2)
                with pe.Fori(0, g // 2) as i:
                    for s in range(2):
                        pe.wait_ge(ready2, i * 2 + s + 1)
                        pe.wait_ge(*A2.ended(i))
                        pe.transpose(turn[s][:, 0, :], slot[:, s, 0, :], G.ident[:]).then_inc(*M2.step(f"out{s}"))

            @block.gpsimd
            def _(pool):
                pool.wait_ge(expd, 1)
                pool.sem_inc(expd, 1)
                with pool.Fori(0, g // 2) as i:
                    for s in range(2):
                        pool.wait_ge(*M2.ended(i))
                        pool.sem_inc(joined, 1)
                        pool.tensor_copy(slot[:, s, 0, :], top[:, bass.ds((i * 2 + s) * P, P)]).then_inc(ready2, 1)


def message_pass(nc, G, tag, X, H, C, table, ex, acc, rows=None):
    W = H * C
    AW = W + H
    with ExitStack() as ctx:
        L = Kit(nc, ctx, tag)
        row = L.sb("row", [P, IT, W]) if rows is None else None
        at = L.sb("at", [P, 2, U], I32)
        oh = L.sb("oh", [P, 2, U, P])
        msg = L.sb("msg", [P, 2, U, AW])
        banks = [[L.ps(f"sum{h}_{u}", [P, 512]) for u in range(U)] for h in range(2)]
        got, before = L.row_sems(X.chunks // IT if rows is None else 0)
        took = L.sem("took")
        V = L.steps("dve_msg", "msg0 late4 late5 late6 late7 oh1 ex1 msg1 acc0 acc1 acc2 acc3 next_oh next_ex", lead=2)
        A = L.steps("act_at", "at0 at1")
        M = L.steps("pe_sum", " ".join(f"sum{u}" for u in range(IT)))
        n = X.chunks // IT
        with nc.Block() as block:
            @block.sync
            def _(sp):
                L.open(sp)

            if rows is None:
                @block.gpsimd
                def _(pool):
                    with pool.Fori(0, n) as i:
                        for h in range(2):
                            pool.wait_ge(*A.at(f"at{h}", i))
                            pool.sem_inc(took, 1)
                            for u in range(U):
                                pool.indirect_dma_start(
                                    out=row[:, h * U + u, :], out_offset=None, in_=table,
                                    in_offset=bass.IndirectOffsetOnAxis(ap=at[:, h, u:u + 1], axis=0)
                                ).then_inc(got[h * U + u], 16)

                @block.scalar
                def _(act):
                    with act.Fori(0, n) as i:
                        for h in range(2):
                            act.wait_ge(*V.at(f"msg{h}", i - 1))
                            act.copy(at[:, h, :], X.src[:, bass.ds(i * IT + h * U, U)]).then_inc(*A.step(f"at{h}"))

            @block.vector
            def _(dve):
                def one_hots_of(h, i):
                    c = i * IT + h * U
                    dve.wait_ge(*M.at(f"sum{h * U + U - 1}", i - 1))
                    one_hots(dve, G, X, oh[:, h], c).then_inc(*V.step("oh1" if h else "next_oh"))
                    dve.tensor_copy(msg[:, h, :, W:AW], ex[:, bass.ds(c, U), :]).then_inc(*V.step("ex1" if h else "next_ex"))

                def messages(h, i):
                    c = i * IT + h * U
                    if rows is None:
                        for u in range(U):
                            dve.wait_ge(got[h * U + u], i * 16 + (16 + before))
                        r = row[:, h * U:(h + 1) * U, :]
                    else:
                        r = rows[:, bass.ds(c, U), :]
                    dve.tensor_tensor(msg[:, h, :, 0:W].rearrange("p u (h c) -> p u h c", h=H),
                                      r.rearrange("p u (h c) -> p u h c", h=H),
                                      ex[:, bass.ds(c, U), :].unsqueeze(3).broadcast_to([P, U, H, C]),
                                      ALU.mult).then_inc(*V.step(f"msg{h}"))

                def add_sum(u, tile, summed, before):
                    a = acc[:, bass.ds(tile, 1), :].rearrange("p a w -> p (a w)")
                    dve.wait_ge(*summed)
                    dve.wait_ge(*before)
                    return dve.tensor_tensor(a, a, banks[u // U][u % U][:, 0:AW], ALU.add)

                def halves(i, first=False, last=False):
                    messages(0, i)
                    tiles = tiles_of(nc, dve, X, 0 if first else i * IT - U, U if first else IT)
                    if first:
                        dve.wait_ge(*V.at("msg0", i))
                        dve.sem_inc(*V.skip(U))
                    else:
                        for u in range(U, IT):
                            add_sum(u, tiles[u - U], M.at(f"sum{u}", i - 1),
                                    V.at(f"late{u - 1}", i) if u > U else V.at(f"acc{U - 1}", i - 1)
                                    ).then_inc(*V.step(f"late{u}"))
                    one_hots_of(1, i)
                    messages(1, i)
                    for u in range(U):
                        add_sum(u, tiles[u if first else u + U], M.at(f"sum{u}", i),
                                V.at(f"acc{u - 1}" if u else f"late{IT - 1}", i)).then_inc(*V.step(f"acc{u}"))
                    if not last:
                        one_hots_of(0, i + 1)

                one_hots_of(0, 0)
                halves(0, first=True)
                with dve.Fori(1, n - 1) as i:
                    halves(i)
                halves(n - 1, last=True)
                dve.wait_ge(*V.at(f"acc{U - 1}", n - 1))
                dve.sem_inc(*V.skip(2))
                tiles = tiles_of(nc, dve, X, n * IT - U, U)
                for u in range(U, IT):
                    add_sum(u, tiles[u - U], M.at(f"sum{u}", n - 1), (V.sem, V.at("msg0", n)[1] - 1 + u - U)
                            ).then_inc(V.sem, 1)

            @block.tensor
            def _(pe):
                with pe.Fori(0, n) as i:
                    for h in range(2):
                        pe.wait_ge(*V.at(f"msg{h}", i))
                        for u in range(U):
                            pe.wait_ge(*(V.at(f"late{h * U + u}", i) if h else V.at(f"acc{u}", i - 1)))
                            pe.matmul(banks[h][u][:, 0:AW], oh[:, h, u, :], msg[:, h, u, :],
                                      start=True, stop=True).then_inc(*M.step(f"sum{h * U + u}"))


def clear(nc, tag, t, value=0.0):
    with ExitStack() as ctx:
        L = Kit(nc, ctx, tag)
        done = L.sem("done")
        with nc.Block() as block:
            @block.vector
            def _(dve):
                dve.memset(t, value).then_inc(done, 1)


def finish_l0_gnn(nc, G, acc):
    H, C = 8, 32
    with ExitStack() as ctx:
        L = Kit(nc, ctx, "f0")
        den = L.sb("den", [P, NT, H])
        z = L.sb("z", [P, GT, D])
        low = L.sb("low", [P, GT, D])
        ready = L.sem("ready")
        V = L.steps("dve_elu", "z low x1 x2")
        A = L.steps("act_elu", "exp")
        with nc.Block() as block:
            @block.sync
            def _(sp):
                L.open(sp)

            @block.vector
            def _(dve):
                dve.tensor_scalar(den[:], acc[:, :, D:D + H], 1e-16, None, ALU.add).then_inc(ready, 1)
                dve.wait_ge(ready, 1)
                dve.reciprocal(den[:], den[:]).then_inc(ready, 1)
                dve.wait_ge(ready, 2)
                with dve.Fori(0, NG) as i:
                    dve.wait_ge(*V.ended(i))
                    dve.tensor_tensor(z[:].rearrange("p t (h c) -> p t h c", h=H),
                                      acc[:, bass.ds(i * GT, GT), 0:D].rearrange("p t (h c) -> p t h c", h=H),
                                      den[:, bass.ds(i * GT, GT), :].unsqueeze(3).broadcast_to([P, GT, H, C]),
                                      ALU.mult).then_inc(*V.step("z"))
                    dve.wait_ge(*V.at("z", i))
                    dve.tensor_scalar(low[:], z[:], 0.0, None, ALU.min).then_inc(*V.step("low"))
                    xg = G.x[:, bass.ds(i * GT, GT), :].rearrange("p t d -> p (t d)")
                    dve.scalar_tensor_tensor(xg, z[:].rearrange("p t d -> p (t d)"), 0.0, xg, ALU.max,
                                             ALU.add).then_inc(*V.step("x1"))
                    dve.wait_ge(*V.at("x1", i))
                    dve.wait_ge(*A.at("exp", i))
                    dve.scalar_tensor_tensor(xg, low[:].rearrange("p t d -> p (t d)"), -1.0, xg, ALU.add,
                                             ALU.add).then_inc(*V.step("x2"))

            @block.scalar
            def _(act):
                with act.Fori(0, NG) as i:
                    act.wait_ge(*V.at("low", i))
                    act.activation(low[:], low[:], ACT.Exp).then_inc(*A.step("exp"))


def router_nodes(nc, G, I, table, ad):
    HE = 16
    with ExitStack() as ctx:
        L = Kit(nc, ctx, "rn")
        nrm = Norm(L, G)
        w = L.sb("w", [P, 2, HE])
        att = L.sb("att", [P, 2, HE])
        rows = L.sb("rows", [P, GT, HE + 4])
        prod = L.sb("prod", [P, GT, HE])
        y = [L.ps(f"y{s}", [P, HE]) for s in range(2)]
        loaded = L.sem("loaded")
        stored = L.sem("stored")
        M = L.steps("pe_h", "mm0 mm1 mm2 mm3 mm4")
        V = L.steps("dve_h", "h0 h1 h2 h3 h4 ps as pd ad")
        with nc.Block() as block:
            @block.sync
            def _(sp):
                L.open(sp)
                with nc.allow_non_contiguous_dma(reason="a small weight"):
                    sp.dma_start(w[:], I["L0_ffn_W_gat"].rearrange("(k p) n -> p k n", p=P)).then_inc(loaded, 16)
                sp.dma_start(att[:, 0, :], spread(I["L0_ffn_att_src"].rearrange("h e -> (h e)"), HE)).then_inc(loaded, 16)
                sp.dma_start(att[:, 1, :], spread(I["L0_ffn_att_dst"].rearrange("h e -> (h e)"), HE)).then_inc(loaded, 16)
                sp.sem_inc(stored, 16)
                with sp.Fori(0, NG) as i:
                    sp.wait_ge(*V.at("as", i))
                    sp.dma_start(rows_of(table, i), rows[:]).then_inc(stored, 16)
                sp.wait_ge(stored, 16 * NG + 16)

            @block.vector
            def _(dve):
                dve.wait_ge(loaded, 48)
                with dve.Fori(0, NG) as i:
                    nrm.dve(dve, i)
                    dve.wait_ge(stored, i * 16 + 16)
                    for u in range(GT):
                        dve.wait_ge(*M.at(f"mm{u}", i))
                        dve.tensor_copy(rows[:, u, 0:HE], y[u % 2]).then_inc(*V.step(f"h{u}"))
                    dve.wait_ge(*V.at("h4", i))
                    for q, (p, a) in enumerate((("ps", "as"), ("pd", "ad"))):
                        if q:
                            dve.wait_ge(*V.at("as", i))
                        dve.tensor_tensor(prod[:], rows[:, :, 0:HE],
                                          att[:, q, :].unsqueeze(1).broadcast_to([P, GT, HE]), ALU.mult).then_inc(*V.step(p))
                        dve.wait_ge(*V.at(p, i))
                        to = rows[:, :, HE:HE + 4] if q == 0 else ad[:, bass.ds(i * GT, GT), :]
                        dve.tensor_reduce(to, prod[:].rearrange("p t (h e) -> p t h e", h=4), AX.X,
                                          ALU.add).then_inc(*V.step(a))

            @block.scalar
            def _(act):
                with act.Fori(0, NG) as i:
                    nrm.act(act, i, M.ended(i))

            @block.tensor
            def _(pe):
                pe.wait_ge(loaded, 48)
                with pe.Fori(0, NG) as i:
                    nrm.pe(pe, i)
                    for u in range(GT):
                        pe.wait_ge(*nrm.C.at(f"cp{u}", i))
                        pe.wait_ge(*(V.at(f"h{u - 2}", i) if u >= 2 else V.ended(i)))
                        for k in range(2):
                            ins = pe.matmul(y[u % 2], nrm.xT[:, k, u * P:(u + 1) * P], w[:, k, :],
                                            start=(k == 0), stop=(k == 1))
                        ins.then_inc(*M.step(f"mm{u}"))


def top2(L, G, dve, link, score, gates, n):
    rank = L.sb("t_rank", [P, NT, n])
    pair = L.sb("t_pair", [P, NT, n, n])
    tie = L.sb("t_tie", [P, NT, n, n])
    first = L.sb("t_first", [P, n, n])
    big = L.sb("t_big", [P, 4, NT])
    one = L.sb("t_one", [P, 2, NT, n])
    pick = L.sb("t_pick", [P, NT, n])
    other = score.unsqueeze(2).broadcast_to([P, NT, n, n])
    own = score.unsqueeze(3).broadcast_to([P, NT, n, n])
    for e in range(n):
        link(dve.tensor_scalar(first[:, e, :], G.iota[:, 0:n], float(e), None, ALU.is_lt))
    link(dve.tensor_tensor(tie[:], other, own, ALU.is_equal))
    for t in range(NT):
        link(dve.tensor_tensor(tie[:, t], tie[:, t], first[:], ALU.mult))
    link(dve.tensor_tensor(pair[:], other, own, ALU.is_gt))
    link(dve.tensor_tensor(pair[:], pair[:], tie[:], ALU.add))
    link(dve.tensor_reduce(rank[:], pair[:], AX.X, ALU.add))
    for r in range(2):
        link(dve.tensor_scalar(one[:, r], rank[:], float(r), None, ALU.is_equal))
        link(dve.tensor_tensor(pick[:], one[:, r], score, ALU.mult))
        link(dve.tensor_reduce(big[:, r, :], pick[:], AX.X, ALU.add))
    link(dve.tensor_tensor(big[:, 2, :], big[:, 1, :], big[:, 0, :], ALU.subtract))

    def after_exp():
        link(dve.tensor_scalar(big[:, 3, :], big[:, 2, :], 1.0, None, ALU.add))
        link(dve.reciprocal(big[:, 3, :], big[:, 3, :]))
        link(dve.tensor_tensor(big[:, 2, :], big[:, 2, :], big[:, 3, :], ALU.mult))
        link(dve.tensor_tensor(one[:, 0], one[:, 0], big[:, 3, :].unsqueeze(2).broadcast_to([P, NT, n]), ALU.mult))
        link(dve.tensor_tensor(one[:, 1], one[:, 1], big[:, 2, :].unsqueeze(2).broadcast_to([P, NT, n]), ALU.mult))
        link(dve.tensor_tensor(gates, one[:, 0], one[:, 1], ALU.add))
    return big[:, 2, :], after_exp


def router_gates(nc, G, I, acc, gates):
    HE = 16
    with ExitStack() as ctx:
        L = Kit(nc, ctx, "rg")
        par = L.sb("par", [P, 3, HE])
        z = L.sb("z", [P, NT, HE])
        sq = L.sb("sq", [P, NT, HE])
        den = L.sb("den", [P, NT, 4])
        mean = L.sb("mean", [P, NT])
        var = L.sb("var", [P, NT])
        score = L.sb("score", [P, NT, 4])
        loaded, chain, ask, done = L.sem("loaded"), L.sem("chain"), L.sem("ask"), L.sem("done")
        second = {}
        with nc.Block() as block:
            @block.sync
            def _(sp):
                for q, name in enumerate(("L0_ffn_b_gat", "L0_ffn_ln_gamma", "L0_ffn_ln_beta")):
                    sp.dma_start(par[:, q, :], spread(I[name], HE)).then_inc(loaded, 16)

            @block.vector
            def _(dve):
                link = chained(dve, chain)

                def row(q):
                    return par[:, q, :].unsqueeze(1).broadcast_to([P, NT, HE])

                def per_token(a):
                    return a.unsqueeze(2).broadcast_to([P, NT, HE])

                link(dve.tensor_scalar(den[:], acc[:, :, HE:HE + 4], 1e-16, None, ALU.add))
                link(dve.reciprocal(den[:], den[:]))
                link(dve.tensor_tensor(z[:].rearrange("p t (h e) -> p t h e", h=4),
                                       acc[:, :, 0:HE].rearrange("p t (h e) -> p t h e", h=4),
                                       den[:].unsqueeze(3).broadcast_to([P, NT, 4, 4]), ALU.mult))
                dve.wait_ge(loaded, 48)
                link(dve.tensor_tensor(z[:], z[:], row(0), ALU.add))
                link(dve.tensor_reduce(mean[:], z[:], AX.X, ALU.add))
                link(dve.tensor_scalar(mean[:], mean[:], 1.0 / HE, None, ALU.mult))
                link(dve.tensor_tensor(z[:], z[:], per_token(mean[:]), ALU.subtract))
                link(dve.tensor_tensor(sq[:], z[:], z[:], ALU.mult))
                link(dve.tensor_reduce(var[:], sq[:], AX.X, ALU.add))
                link(dve.tensor_scalar(var[:], var[:], 1.0 / HE, EPS, ALU.mult, ALU.add))
                dve.sem_inc(ask, 1)
                dve.wait_ge(done, 1)
                link(dve.reciprocal(var[:], mean[:]))
                link(dve.tensor_tensor(z[:], z[:], per_token(var[:]), ALU.mult))
                link(dve.tensor_tensor(z[:], z[:], row(1), ALU.mult))
                link(dve.tensor_tensor(z[:], z[:], row(2), ALU.add))
                link(dve.tensor_reduce(score[:], z[:].rearrange("p t (h e) -> p t e h", h=4), AX.X, ALU.add))
                link(dve.tensor_scalar(score[:], score[:], 0.25, None, ALU.mult))
                second["ap"], after = top2(L, G, dve, link, score[:], gates[:], 4)
                dve.sem_inc(ask, 1)
                dve.wait_ge(done, 2)
                after()

            @block.scalar
            def _(act):
                act.wait_ge(ask, 1)
                act.activation(mean[:], var[:], ACT.Sqrt).then_inc(done, 1)
                act.wait_ge(ask, 2)
                act.activation(second["ap"], second["ap"], ACT.Exp).then_inc(done, 1)


def gate_bias(nc, G, tag, gates, n, bias):
    with ExitStack() as ctx:
        L = Kit(nc, ctx, tag)
        gs = L.sb("gs", [P, GT, n])
        gT = L.sb("gT", [n, GT, P])
        tr = [L.ps(f"tr{s}", [n, P]) for s in range(2)]
        y = [L.ps(f"y{s}", [P, D]) for s in range(2)]
        M = L.steps("pe_bias", "tr0 tr1 tr2 tr3 tr4 mm0 mm1 mm2 mm3 mm4")
        A = L.steps("act_bias", "gs cp0 cp1 cp2 cp3 cp4")
        V = L.steps("dve_bias", "x0 x1 x2 x3 x4")
        with nc.Block() as block:
            @block.sync
            def _(sp):
                L.open(sp)

            @block.scalar
            def _(act):
                with act.Fori(0, NG) as i:
                    act.wait_ge(*M.ended(i))
                    act.copy(gs[:], gates[:, bass.ds(i * GT, GT), :]).then_inc(*A.step("gs"))
                    for u in range(GT):
                        act.wait_ge(*M.at(f"tr{u}", i))
                        act.copy(gT[:, u, :], tr[u % 2]).then_inc(*A.step(f"cp{u}"))

            @block.tensor
            def _(pe):
                with pe.Fori(0, NG) as i:
                    pe.wait_ge(*A.at("gs", i))
                    for u in range(GT):
                        if u >= 2:
                            pe.wait_ge(*A.at(f"cp{u - 2}", i))
                        pe.transpose(tr[u % 2], gs[:, u, :], G.ident[:]).then_inc(*M.step(f"tr{u}"))
                    for u in range(GT):
                        pe.wait_ge(*A.at(f"cp{u}", i))
                        pe.wait_ge(*(V.at(f"x{u - 2}", i) if u >= 2 else V.ended(i)))
                        pe.matmul(y[u % 2], gT[:, u, :], bias[:], start=True, stop=True).then_inc(*M.step(f"mm{u}"))

            @block.vector
            def _(dve):
                with dve.Fori(0, NG) as i:
                    for u in range(GT):
                        dve.wait_ge(*M.at(f"mm{u}", i))
                        xt = G.x[:, bass.ds(i * GT + u, 1), :].rearrange("p a d -> p (a d)")
                        dve.tensor_tensor(xt, xt, y[u % 2], ALU.add).then_inc(*V.step(f"x{u}"))


def gelu_experts(nc, G, tag, W1, b1, W2, gates, n, affine_of=None):
    F = 512
    HC = F // P
    HALF = GT * P // 2
    with ExitStack() as ctx:
        L = Kit(nc, ctx, tag)
        affine = (L.sb("gamma", [P, D]), L.sb("beta", [P, D])) if affine_of else None
        nrm = Norm(L, G, affine)
        w1 = L.sb("w1", [P, n, 2, F])
        w2 = L.sb("w2", [P, n, HC, D])
        b1T = L.sb("b1T", [P, n, HC])
        hT = L.sb("hT", [P, 2, HC, GT * P])
        hp = [[L.ps(f"hp{s}{f}", [P, HALF]) for f in range(2)] for s in range(2)]
        y = [L.ps(f"y{s}", [P, D]) for s in range(2)]
        loaded = L.sem("loaded")
        names = ""
        for e in range(n + 1):
            if e < n:
                names += " ".join(f"h{e}_{c}" for c in range(HC)) + " "
            if e:
                names += " ".join(f"y{e - 1}_{u}" for u in range(GT)) + " "
        M = L.steps("pe_ffn", names)
        A = L.steps("act_gelu", " ".join(f"g{e}_{c}" for e in range(n) for c in range(HC)))
        V = L.steps("dve_gated", " ".join(f"x{e}_{u}" for e in range(n) for u in range(GT)))
        loads = 16 * (3 + (2 if affine_of else 0))
        with nc.Block() as block:
            @block.sync
            def _(sp):
                L.open(sp)
                if affine_of:
                    sp.dma_start(affine[0][:], spread(affine_of[0], D)).then_inc(loaded, 16)
                    sp.dma_start(affine[1][:], spread(affine_of[1], D)).then_inc(loaded, 16)
                with nc.allow_non_contiguous_dma(reason="biases, hidden units to partitions"):
                    sp.dma_start(b1T[:], b1.rearrange("e (c p) -> p e c", p=P)).then_inc(loaded, 16)
                sp.dma_start(w1[:], W1.rearrange("e (k p) f -> p e k f", p=P)).then_inc(loaded, 16)
                sp.dma_start(w2[:], W2.rearrange("e (c p) d -> p e c d", p=P)).then_inc(loaded, 16)

            @block.vector
            def _(dve):
                dve.wait_ge(loaded, loads)
                with dve.Fori(0, NG) as i:
                    nrm.dve(dve, i)
                    for e in range(n):
                        for u in range(GT):
                            dve.wait_ge(*M.at(f"y{e}_{u}", i))
                            if e:
                                dve.wait_ge(*V.at(f"x{e - 1}_{u}", i))
                            xt = G.x[:, bass.ds(i * GT + u, 1), :].rearrange("p a d -> p (a d)")
                            dve.scalar_tensor_tensor(
                                xt, y[u % 2], gates[:, bass.ds(i * GT + u, 1), e:e + 1].rearrange("p a e -> p (a e)"),
                                xt, ALU.mult, ALU.add).then_inc(*V.step(f"x{e}_{u}"))

            @block.scalar
            def _(act):
                act.wait_ge(loaded, loads)
                with act.Fori(0, NG) as i:
                    nrm.act(act, i, M.ended(i))
                    for e in range(n):
                        for c in range(HC):
                            if c == 0:
                                act.wait_ge(*(M.at(f"y{e - 2}_{GT - 1}", i) if e >= 2 else M.ended(i)))
                            act.wait_ge(*M.at(f"h{e}_{c}", i))
                            for f in range(2):
                                ins = act.activation(hT[:, e % 2, c, f * HALF:(f + 1) * HALF],
                                                     hp[c % 2][f], ACT.Gelu, bias=b1T[:, e, c:c + 1])
                            ins.then_inc(*A.step(f"g{e}_{c}"))

            @block.tensor
            def _(pe):
                pe.wait_ge(loaded, loads)
                with pe.Fori(0, NG) as i:
                    nrm.pe(pe, i)
                    pe.wait_ge(*nrm.C.at(f"cp{GT - 1}", i))
                    for e in range(n + 1):
                        if e < n:
                            for c in range(HC):
                                q = e * HC + c - 2
                                pe.wait_ge(*(A.at(f"g{q // HC}_{q % HC}", i) if q >= 0 else A.ended(i)))
                                for f in range(2):
                                    for k in range(2):
                                        ins = pe.matmul(hp[c % 2][f], w1[:, e, k, c * P:(c + 1) * P],
                                                        nrm.xT[:, k, f * HALF:(f + 1) * HALF],
                                                        start=(k == 0), stop=(k == 1))
                                ins.then_inc(*M.step(f"h{e}_{c}"))
                        if e:
                            pe.wait_ge(*A.at(f"g{e - 1}_{HC - 1}", i))
                            for u in range(GT):
                                q = (e - 1) * GT + u
                                if u >= 2:
                                    pe.wait_ge(*V.at(f"x{e - 1}_{u - 2}", i))
                                else:
                                    pe.wait_ge(*(V.at(f"x{e - 2}_{GT - 1}", i) if e >= 2 else V.ended(i)))
                                for c in range(HC):
                                    ins = pe.matmul(y[u % 2], hT[:, (e - 1) % 2, c, u * P:(u + 1) * P],
                                                    w2[:, e - 1, c, :], start=(c == 0), stop=(c == HC - 1))
                                ins.then_inc(*M.step(f"y{e - 1}_{u}"))


def load(nc, tag, *pairs):
    with ExitStack() as ctx:
        L = Kit(nc, ctx, tag)
        loaded = L.sem("loaded")
        with nc.Block() as block:
            @block.sync
            def _(sp):
                for to, a in zip(pairs[::2], pairs[1::2]):
                    sp.dma_start(to, a).then_inc(loaded, 16)
                sp.wait_ge(loaded, 16 * (len(pairs) // 2))


def conv_nodes(nc, G, tag, W, bias, table, acc, relu_of=None):
    with ExitStack() as ctx:
        L = Kit(nc, ctx, tag)
        nrm = Norm(L, G, relu_of=relu_of)
        w = L.sb("w", [P, 2, D])
        b = L.sb("b", [P, D])
        y = [L.ps(f"y{s}", [P, D]) for s in range(2)]
        loaded = L.sem("loaded")
        stored = L.sem("stored")
        M = L.steps("pe_loop", "mm0 mm1 mm2 mm3 mm4")
        V = L.steps("dve_loop", "b0 b1 b2 b3 b4")
        with nc.Block() as block:
            @block.sync
            def _(sp):
                L.open(sp)
                sp.dma_start(w[:], W.rearrange("(k p) n -> p k n", p=P)).then_inc(loaded, 16)
                sp.dma_start(b[:], spread(bias, D)).then_inc(loaded, 16)
                with sp.Fori(0, NG) as i:
                    sp.wait_ge(*nrm.V.at(nrm.last, i))
                    sp.dma_start(rows_of(table, i), nrm.xn[:]).then_inc(stored, 16)
                sp.wait_ge(stored, 16 * NG)

            @block.vector
            def _(dve):
                dve.wait_ge(loaded, 32)
                with dve.Fori(0, NG) as i:
                    nrm.dve(dve, i, [(stored, i * 16)])
                    for u in range(GT):
                        dve.wait_ge(*M.at(f"mm{u}", i))
                        dve.tensor_tensor(acc[:, bass.ds(i * GT + u, 1), :].rearrange("p a d -> p (a d)"), y[u % 2],
                                          b[:], ALU.add).then_inc(*V.step(f"b{u}"))

            @block.scalar
            def _(act):
                with act.Fori(0, NG) as i:
                    nrm.act(act, i, M.ended(i))

            @block.tensor
            def _(pe):
                pe.wait_ge(loaded, 32)
                with pe.Fori(0, NG) as i:
                    nrm.pe(pe, i)
                    for u in range(GT):
                        pe.wait_ge(*nrm.C.at(f"cp{u}", i))
                        pe.wait_ge(*(V.at(f"b{u - 2}", i) if u >= 2 else V.ended(i)))
                        for k in range(2):
                            ins = pe.matmul(y[u % 2], nrm.xT[:, k, u * P:(u + 1) * P], w[:, k, :],
                                            start=(k == 0), stop=(k == 1))
                        ins.then_inc(*M.step(f"mm{u}"))


def three_parts(dve, link, whole, rest, parts):
    link(dve.tensor_copy(parts[:], whole[:]))
    link(dve.tensor_tensor(rest[:], whole[:], parts[:], ALU.subtract))
    link(dve.tensor_copy(parts[32:64, :], rest[32:64, :]))
    link(dve.tensor_copy(parts[64:96, :], rest[64:96, :]))
    link(dve.tensor_tensor(rest[64:96, :], rest[64:96, :], parts[64:96, :], ALU.subtract))
    link(dve.tensor_copy(parts[64:96, :], rest[64:96, :]))


def conv_pass(nc, G, tag, X, table, types, weight, W, acc):
    R, B2 = 16, 512
    KP = 96
    with ExitStack() as ctx:
        L = Kit(nc, ctx, tag)
        wf = L.sb("wf", [KP, B2])
        rest = L.sb("rest", [KP, B2])
        parts = L.sb("parts", [KP, B2], BF16)
        kind = L.sb("kind", [P, KP])
        kind_i = L.sb("kind_i", [P, KP], I32)
        row = L.sb("row", [P, IT, D])
        at = L.sb("at", [P, 2, U], I32)
        oh = L.sb("oh", [P, 2, U, P])
        et = L.sb("et", [P, 2, U, KP], BF16)
        etT = L.sb("etT", [KP, 2, U * P], BF16)
        prod = L.sb("prod", [P, 2, U, B2])
        turn = [L.ps(f"turn{h}", [KP, U, P], BF16) for h in range(2)]
        wide = [L.ps(f"wide{u}", [P, B2]) for u in range(2)]
        sums = [L.ps(f"sums{u}", [P, D]) for u in range(U)]
        got, before = L.row_sems(X.chunks // IT)
        took, loaded, chain = L.sem("took"), L.sem("loaded"), L.sem("chain")
        V = L.steps("dve_conv", "prod0 late6 prod1 late7 oh1 et1 prod2 acc0 prod3 acc1 prod4 acc2 prod5 acc3 "
                    "next_oh next_et prod6 acc4 prod7 acc5", lead=6)
        A = L.steps("act_conv", "at1 row0 row1 row2 row3 T1 row4 next_at row5 row6 row7 next_T", lead=5)
        M = L.steps("pe_conv", "w2 sum0 w3 sum1 tr1 w4 sum2 w5 sum3 w6 sum4 w7 sum5 next_tr next_w0 sum6 next_w1 sum7",
                    lead=5)
        n = X.chunks // IT
        with nc.Block() as block:
            @block.sync
            def _(sp):
                L.open(sp)
                sp.wait_ge(chain, 2)
                for q in range(3):
                    sp.dma_start(wf[32 * q:32 * q + R, :], W.rearrange("r b i o -> r (b i o)")).then_inc(loaded, 16)

            @block.gpsimd
            def _(pool):
                with pool.Fori(0, n) as i:
                    for h in range(2):
                        pool.wait_ge(*(A.at("at1", i) if h else A.at("next_at", i - 1)))
                        pool.sem_inc(took, 1)
                        for u in range(U):
                            pool.indirect_dma_start(
                                out=row[:, h * U + u, :], out_offset=None, in_=table,
                                in_offset=bass.IndirectOffsetOnAxis(ap=at[:, h, u:u + 1], axis=0)
                            ).then_inc(got[h * U + u], 16)

            @block.scalar
            def _(act):
                def indices(h, i):
                    act.wait_ge(*V.at(f"prod{h * U + U - 1}", i - 1))
                    act.copy(at[:, h, :], X.src[:, bass.ds(i * IT + h * U, U)]).then_inc(
                        *A.step("at1" if h else "next_at"))

                def turned(h, i):
                    act.wait_ge(*(M.at("tr1", i) if h else M.at("next_tr", i - 1)))
                    act.wait_ge(*M.at("w7" if h else "w3", i - 1))
                    act.copy(etT[:, h, :], turn[h].rearrange("p u e -> p (u e)")).then_inc(
                        *A.step("T1" if h else "next_T"))

                def weigh(u, i):
                    act.wait_ge(got[u], i * 16 + (16 + before))
                    act.activation(row[:, u, :], row[:, u, :], ACT.Copy,
                                   scale=weight[:, bass.ds(i * IT + u, 1)]).then_inc(*A.step(f"row{u}"))

                def chunks(i, last=False):
                    indices(1, i)
                    for u in range(U):
                        weigh(u, i)
                    turned(1, i)
                    weigh(U, i)
                    if last:
                        act.wait_ge(*A.at(f"row{U}", i))
                        act.sem_inc(*A.skip(1))
                    else:
                        indices(0, i + 1)
                    for u in range(U + 1, IT):
                        weigh(u, i)
                    if not last:
                        turned(0, i + 1)

                indices(0, 0)
                act.wait_ge(*A.at("next_at", -1))
                act.sem_inc(*A.skip(3))
                turned(0, 0)
                with act.Fori(0, n - 1) as i:
                    chunks(i)
                chunks(n - 1, last=True)

            @block.vector
            def _(dve):
                link = chained(dve, chain)
                link(dve.memset(wf[:], 0.0))
                link(dve.memset(parts[:], 0.0))
                link(dve.tensor_copy(kind_i[:], G.iota[:, 0:KP]))
                link(dve.tensor_scalar(kind_i[:], kind_i[:], 31, None, ALU.bitwise_and))
                link(dve.tensor_copy(kind[:], kind_i[:]))
                dve.wait_ge(loaded, 48)
                three_parts(dve, link, wf, rest, parts)

                def one_hots_of(h, i):
                    c = i * IT + h * U
                    dve.wait_ge(*M.at(f"sum{h * U + U - 1}", i - 1))
                    one_hots(dve, G, X, oh[:, h], c).then_inc(*V.step("oh1" if h else "next_oh"))
                    dve.tensor_tensor(et[:, h], kind[:].unsqueeze(1).broadcast_to([P, U, KP]),
                                      types[:, bass.ds(c, U)].unsqueeze(2).broadcast_to([P, U, KP]),
                                      ALU.is_equal).then_inc(*V.step("et1" if h else "next_et"))

                def add_sum(u, tile, i, before):
                    a = acc[:, bass.ds(tile, 1), :].rearrange("p a w -> p (a w)")
                    dve.wait_ge(*M.at(f"sum{u}", i - 1 if u >= IT - 2 else i))
                    dve.wait_ge(*V.at(before, i - 1 if u == IT - 2 else i))
                    dve.tensor_tensor(a, a, sums[u % U], ALU.add).then_inc(
                        *V.step(f"late{u}" if u >= IT - 2 else f"acc{u}"))

                def chunks(i, first=False, last=False):
                    tiles = tiles_of(nc, dve, X, 0 if first else i * IT - 2)
                    for u in range(IT):
                        dve.wait_ge(*A.at(f"row{u}", i))
                        dve.wait_ge(*(M.at(f"w{u}", i) if u >= 2 else M.at(f"next_w{u}", i - 1)))
                        dve.wait_ge(*M.at(f"sum{u}", i - 1))
                        dve.tensor_tensor(prod[:, u // U, u % U, :].rearrange("p (c o) -> p c o", o=2),
                                          wide[u % 2].rearrange("p (c o) -> p c o", o=2),
                                          row[:, u, :].unsqueeze(2).broadcast_to([P, D, 2]), ALU.mult
                                          ).then_inc(*V.step(f"prod{u}"))
                        if first and u < 2:
                            dve.wait_ge(*V.at(f"prod{u}", i))
                            dve.sem_inc(*V.skip(1))
                        elif u < 2:
                            add_sum(IT - 2 + u, tiles[u], i, f"late{IT - 2}" if u else f"acc{IT - 3}")
                        else:
                            add_sum(u - 2, tiles[u - 2 if first else u], i, f"acc{u - 3}" if u > 2 else f"late{IT - 1}")
                        if u == 1:
                            one_hots_of(1, i)
                        if u == 5 and last:
                            dve.wait_ge(*V.at("acc3", i))
                            dve.sem_inc(*V.skip(2))
                        elif u == 5:
                            one_hots_of(0, i + 1)

                one_hots_of(0, 0)
                dve.wait_ge(*V.at("next_et", -1))
                dve.sem_inc(*V.skip(4))
                chunks(0, first=True)
                with dve.Fori(1, n - 1) as i:
                    chunks(i)
                chunks(n - 1, last=True)
                tiles = tiles_of(nc, dve, X, n * IT - 2, 2)
                for u in range(2):
                    a = acc[:, bass.ds(tiles[u], 1), :].rearrange("p a w -> p (a w)")
                    dve.wait_ge(*M.at(f"sum{IT - 2 + u}", n - 1))
                    dve.wait_ge(*(V.at("prod0", n) if u else V.at("acc5", n - 1)))
                    dve.tensor_tensor(a, a, sums[(IT - 2 + u) % U], ALU.add).then_inc(V.sem, 1)

            @block.tensor
            def _(pe):
                pe.wait_ge(chain, 11)

                def turn_types(h, i):
                    pe.wait_ge(*(V.at("et1", i) if h else V.at("next_et", i - 1)))
                    pe.wait_ge(*(A.at("T1", i - 1) if h else A.at("next_T", i - 2)))
                    for u in range(U):
                        ins = pe.transpose(turn[h][:, u, :], et[:, h, u, :], G.identb[:])
                    ins.then_inc(*M.step("tr1" if h else "next_tr"))

                def blocks_of(u, i):
                    h = u // U
                    pe.wait_ge(*(A.at("T1", i) if h else A.at("next_T", i - 1)))
                    pe.wait_ge(*(V.at(f"prod{u - 2}", i) if u >= 2 else V.at(f"prod{IT - 2 + u}", i - 1)))
                    pe.matmul(wide[u % 2], etT[:, h, u % U * P:(u % U + 1) * P], parts[:], start=True,
                              stop=True).then_inc(*M.step(f"w{u}" if u >= 2 else f"next_w{u}"))

                def chunks(i, last=False):
                    for u in range(IT):
                        if u + 2 < IT:
                            blocks_of(u + 2, i)
                        elif last:
                            pe.wait_ge(*M.at(f"sum{u - 1}", i))
                            pe.sem_inc(*M.skip(2 if u + 2 == IT else 1))
                        else:
                            if u + 2 == IT:
                                turn_types(0, i + 1)
                            blocks_of(u + 2 - IT, i + 1)
                        pe.wait_ge(*V.at(f"prod{u}", i))
                        pe.wait_ge(*(V.at(f"acc{u - U}", i) if u >= U else V.at(f"acc{u + U}", i - 1) if u < 2 else
                                     V.at(f"late{u + U}", i)))
                        p4 = prod[:, u // U, u % U, :].rearrange("p (b i o) -> p i b o", i=2, o=2)
                        for q in range(2):
                            ins = pe.matmul(sums[u % U].rearrange("p (b o) -> p b o", o=2),
                                            oh[:, u // U, u % U, :], p4[:, q], start=(q == 0), stop=(q == 1))
                        ins.then_inc(*M.step(f"sum{u}"))
                        if u == 1:
                            turn_types(1, i)

                turn_types(0, 0)
                for u in range(2):
                    blocks_of(u, 0)
                    pe.wait_ge(*M.at(f"next_w{u}", -1))
                    pe.sem_inc(*M.skip(1))
                with pe.Fori(0, n - 1) as i:
                    chunks(i)
                chunks(n - 1, last=True)


def scores_of(nc, G, tag, W, n, bias, gates, affine_of=None, soft=False):
    with ExitStack() as ctx:
        L = Kit(nc, ctx, tag)
        score = L.sb("score", [P, NT, n])
        with ExitStack() as inner:
            L1 = Kit(nc, inner, tag + "n")
            affine = (L1.sb("gamma", [P, D]), L1.sb("beta", [P, D])) if affine_of else None
            nrm = Norm(L1, G, affine)
            w = L1.sb("w", [P, 2, n])
            b = L1.sb("b", [P, n])
            y = [L1.ps(f"y{s}", [P, n]) for s in range(2)]
            loaded = L1.sem("loaded")
            M = L1.steps("pe_score", "mm0 mm1 mm2 mm3 mm4")
            V = L1.steps("dve_score", "b0 b1 b2 b3 b4")
            loads = 16 * (4 if affine_of else 2)
            with nc.Block() as block:
                @block.sync
                def _(sp):
                    L1.open(sp)
                    with nc.allow_non_contiguous_dma(reason="a small weight"):
                        sp.dma_start(w[:], W.rearrange("(k p) n -> p k n", p=P)).then_inc(loaded, 16)
                    sp.dma_start(b[:], spread(bias, n)).then_inc(loaded, 16)
                    if affine_of:
                        sp.dma_start(affine[0][:], spread(affine_of[0], D)).then_inc(loaded, 16)
                        sp.dma_start(affine[1][:], spread(affine_of[1], D)).then_inc(loaded, 16)

                @block.vector
                def _(dve):
                    dve.wait_ge(loaded, loads)
                    with dve.Fori(0, NG) as i:
                        nrm.dve(dve, i)
                        for u in range(GT):
                            dve.wait_ge(*M.at(f"mm{u}", i))
                            dve.tensor_tensor(score[:, bass.ds(i * GT + u, 1), :].rearrange("p a d -> p (a d)"),
                                              y[u % 2], b[:], ALU.add).then_inc(*V.step(f"b{u}"))

                @block.scalar
                def _(act):
                    with act.Fori(0, NG) as i:
                        nrm.act(act, i, M.ended(i))

                @block.tensor
                def _(pe):
                    pe.wait_ge(loaded, loads)
                    with pe.Fori(0, NG) as i:
                        nrm.pe(pe, i)
                        for u in range(GT):
                            pe.wait_ge(*nrm.C.at(f"cp{u}", i))
                            pe.wait_ge(*(V.at(f"b{u - 2}", i) if u >= 2 else V.ended(i)))
                            for k in range(2):
                                ins = pe.matmul(y[u % 2], nrm.xT[:, k, u * P:(u + 1) * P], w[:, k, :],
                                                start=(k == 0), stop=(k == 1))
                            ins.then_inc(*M.step(f"mm{u}"))
        top = L.sb("top", [P, NT])
        chain, ask, done = L.sem("chain"), L.sem("ask"), L.sem("done")
        second = {}
        with nc.Block() as block:
            @block.vector
            def _(dve):
                link = chained(dve, chain)
                if soft:
                    link(dve.tensor_reduce(top[:], score[:], AX.X, ALU.max))
                    link(dve.tensor_tensor(score[:], score[:], top[:].unsqueeze(2).broadcast_to([P, NT, n]),
                                           ALU.subtract))
                    dve.sem_inc(ask, 1)
                    dve.wait_ge(done, 1)
                    link(dve.tensor_reduce(top[:], score[:], AX.X, ALU.add))
                    link(dve.reciprocal(top[:], top[:]))
                    link(dve.tensor_tensor(score[:], score[:], top[:].unsqueeze(2).broadcast_to([P, NT, n]), ALU.mult))
                second["ap"], after = top2(L, G, dve, link, score[:], gates[:, :, 0:n], n)
                dve.sem_inc(ask, 1)
                dve.wait_ge(done, 2 if soft else 1)
                after()

            @block.scalar
            def _(act):
                if soft:
                    act.wait_ge(ask, 1)
                    act.activation(score[:], score[:], ACT.Exp).then_inc(done, 1)
                act.wait_ge(ask, 2 if soft else 1)
                act.activation(second["ap"], second["ap"], ACT.Exp).then_inc(done, 1)


def add_to_x(nc, G, tag, t):
    with ExitStack() as ctx:
        L = Kit(nc, ctx, tag)
        done = L.sem("done")
        with nc.Block() as block:
            @block.vector
            def _(dve):
                dve.tensor_tensor(G.x[:], G.x[:], t, ALU.add).then_inc(done, 1)


def edge_attention_pass(nc, G, tag, X, al_dram, hparts, edges, weight_rows, alpha):
    H, EP, KP = 8, 12, 96
    with ExitStack() as ctx:
        L = Kit(nc, ctx, tag)
        row = L.sb("row", [P, IT, H])
        at = L.sb("at", [P, 2, U], I32)
        oh = L.sb("oh", [P, 2, U, P], BF16)
        ohT = L.sb("ohT", [P, 2, U * P], BF16)
        eparts = L.sb("eparts", [P, X.chunks, EP], BF16)
        erest = L.sb("erest", [P, X.chunks, 4])
        wf = L.sb("wf", [KP, D])
        rest = L.sb("rest", [KP, D])
        parts = L.sb("parts", [KP, D], BF16)
        ea = L.sb("ea", [P, 2, U, KP], BF16)
        eaT = L.sb("eaT", [KP, 2, U * P], BF16)
        enc = L.sb("enc", [P, 2, U, D])
        prod = L.sb("prod", [P, U, D])
        s = L.sb("s", [P, U, H])
        dot = L.sb("dot", [P, U, H])
        turn = L.ps("turn", [P, 2, U, P], BF16)
        encp = [L.ps(f"encp{q}", [P, 2, D]) for q in range(2)]
        hdst = [L.ps(f"hdst{h}", [P, U, D]) for h in range(2)]
        addst = L.ps("addst", [P, U, 3, H])
        got, before = L.row_sems(X.chunks // IT)
        took, loaded, chain, split = L.sem("took"), L.sem("loaded"), L.sem("chain"), L.sem("split")
        V = L.steps("dve_alpha", " ".join(f"next_oh{h} prod{h} ad{h} sum{h} dot{h} add{h} alpha{h}" for h in range(2)),
                    lead=14)
        A = L.steps("act_alpha", "next_ea0 T1 ET1 next_ea1 r1_0 r1_1 next_at0 next_T0 next_ET0 next_r0_0 next_r0_1 next_at1",
                    lead=12)
        M = L.steps("pe_alpha", "tr1 te1 h0 ad0 enc1_0 enc1_1 next_tr0 next_te0 h1 ad1 next_enc0_0 next_enc0_1", lead=6)
        n = X.chunks // IT

        with nc.Block() as block:
            @block.sync
            def _(sp):
                L.open(sp)
                sp.wait_ge(chain, 2)
                with nc.allow_non_contiguous_dma(reason="a small weight, transposed"):
                    for r in range(9):
                        p = r // 3 * 32 + r % 3 * 4
                        sp.dma_start(wf[p:p + 3, :], weight_rows[0]).then_inc(loaded, 16)
                        sp.dma_start(wf[p + 3:p + 4, :], weight_rows[1]).then_inc(loaded, 16)

            @block.gpsimd
            def _(pool):
                with pool.Fori(0, n) as i:
                    for h in range(2):
                        pool.wait_ge(*A.half("at#", h, i))
                        pool.sem_inc(took, 1)
                        for u in range(U):
                            pool.indirect_dma_start(
                                out=row[:, h * U + u, :], out_offset=None, in_=al_dram,
                                in_offset=bass.IndirectOffsetOnAxis(ap=at[:, h, u:u + 1], axis=0)
                            ).then_inc(got[h * U + u], 16)

            @block.scalar
            def _(act):
                def indices(h, i):
                    act.wait_ge(*V.at(f"sum{h}", i - 1))
                    act.copy(at[:, h, :], X.src[:, bass.ds(i * IT + h * U, U)]).then_inc(*A.half_step("at#", h))

                def staged(h, i):
                    act.wait_ge(*M.half("te#", h, i - 1))
                    act.copy(ea[:, h].rearrange("p u (w k) -> p u w k", w=3)[:, :, :, 0:EP],
                             eparts[:, bass.ds(i * IT + h * U, U), :].unsqueeze(2).broadcast_to([P, U, 3, EP])
                             ).then_inc(*A.half_step("ea#", h))

                def turned(h, i):
                    act.wait_ge(*M.half("te#", h, i))
                    act.wait_ge(*M.at(f"ad{h}", i - 1))
                    act.copy(ohT[:, h, :], turn[:, 0].rearrange("p u e -> p (u e)")).then_inc(*A.half_step("T#", h))
                    act.wait_ge(*M.half("enc#_1", h, i - 1))
                    act.copy(eaT[:, h, :], turn[0:KP, 1].rearrange("p u e -> p (u e)")).then_inc(*A.half_step("ET#", h))

                def encoded(h, i):
                    for q in range(2):
                        act.wait_ge(*M.half(f"enc#_{q}", h, i))
                        act.wait_ge(*V.at(f"prod{h}", i - 1))
                        act.activation(enc[:, h, 2 * q:2 * q + 2, :], encp[q], ACT.Relu).then_inc(*A.half_step(f"r#_{q}", h))

                act.wait_ge(split, 1)
                staged(0, 0)
                act.wait_ge(*A.at("next_ea0", -1))
                act.sem_inc(*A.skip(2))
                staged(1, 0)
                act.wait_ge(*A.at("next_ea1", -1))
                act.sem_inc(*A.skip(2))
                indices(0, 0)
                turned(0, 0)
                encoded(0, 0)
                indices(1, 0)
                with act.Fori(0, n - 1) as i:
                    staged(0, i + 1)
                    turned(1, i)
                    staged(1, i + 1)
                    encoded(1, i)
                    indices(0, i + 1)
                    turned(0, i + 1)
                    encoded(0, i + 1)
                    indices(1, i + 1)
                act.wait_ge(*A.at("next_at1", n - 2))
                act.sem_inc(*A.skip(1))
                turned(1, n - 1)
                act.wait_ge(*A.at("ET1", n - 1))
                act.sem_inc(*A.skip(1))
                encoded(1, n - 1)

            @block.vector
            def _(dve):
                link = chained(dve, chain)
                link(dve.memset(wf[:], 0.0))
                link(dve.memset(ea[:], 0.0))
                dve.wait_ge(loaded, 16 * 18)
                three_parts(dve, link, wf, rest, parts)
                for e in range(3):
                    left = edges if e == 0 else erest[:]
                    link(dve.tensor_copy(eparts[:, :, 4 * e:4 * e + 4], left))
                    if e < 2:
                        link(dve.tensor_tensor(erest[:], left, eparts[:, :, 4 * e:4 * e + 4], ALU.subtract))
                dve.sem_inc(split, 1)

                def next_one_hots(h, i):
                    dve.wait_ge(*M.half("tr#", h, i - 1))
                    one_hots(dve, G, X, oh[:, h], i * IT + h * U).then_inc(*V.step(f"next_oh{h}"))

                def chunks(i, more):
                    for h in range(2):
                        c = i * IT + h * U
                        if more:
                            next_one_hots(h, i + 1)
                        else:
                            dve.wait_ge(*(V.at("alpha0", i) if h else V.at("alpha1", i - 1)))
                            dve.sem_inc(*V.skip(1))
                        dve.wait_ge(*A.half("r#_1", h, i))
                        dve.wait_ge(*M.at(f"h{h}", i))
                        dve.wait_ge(*(V.at("dot0", i) if h else V.at("dot1", i - 1)))
                        dve.tensor_tensor(prod[:], enc[:, h], hdst[h], ALU.mult).then_inc(*V.step(f"prod{h}"))
                        dve.wait_ge(*M.at(f"ad{h}", i))
                        dve.wait_ge(*(V.at("alpha0", i) if h else V.at("alpha1", i - 1)))
                        dve.tensor_reduce(s[:], addst.rearrange("p u q h -> p u h q"), AX.X,
                                          ALU.add).then_inc(*V.step(f"ad{h}"))
                        dve.wait_ge(*V.at(f"ad{h}", i))
                        for u in range(U):
                            dve.wait_ge(got[h * U + u], i * 16 + (16 + before))
                        dve.tensor_tensor(s[:], s[:], row[:, h * U:(h + 1) * U, :], ALU.add).then_inc(*V.step(f"sum{h}"))
                        dve.wait_ge(*V.at(f"prod{h}", i))
                        dve.tensor_reduce(dot[:], prod[:].rearrange("p u (h c) -> p u h c", h=H), AX.X,
                                          ALU.add).then_inc(*V.step(f"dot{h}"))
                        dve.wait_ge(*V.at(f"dot{h}", i))
                        dve.tensor_tensor(s[:], s[:], dot[:], ALU.add).then_inc(*V.step(f"add{h}"))
                        dve.wait_ge(*V.at(f"add{h}", i))
                        flat = s[:].rearrange("p u h -> p (u h)")
                        dve.scalar_tensor_tensor(alpha[:, bass.ds(c, U), :].rearrange("p u h -> p (u h)"), flat, 0.2,
                                                 flat, ALU.mult, ALU.max).then_inc(*V.step(f"alpha{h}"))

                for h in range(2):
                    next_one_hots(h, 0)
                    dve.wait_ge(*V.at(f"next_oh{h}", -1))
                    dve.sem_inc(*V.skip(6))
                with dve.Fori(0, n - 1) as i:
                    chunks(i, True)
                chunks(n - 1, False)

            @block.tensor
            def _(pe):
                def turn_over(h, i):
                    pe.wait_ge(*V.at(f"next_oh{h}", i - 1))
                    pe.wait_ge(*(A.half("ET#", 0, i) if h else A.half("ET#", 1, i - 1)))
                    for u in range(U):
                        ins = pe.transpose(turn[:, 0, u, :], oh[:, h, u, :], G.identb[:])
                    ins.then_inc(*M.half_step("tr#", h))
                    pe.wait_ge(*A.half("ea#", h, i))
                    for u in range(U):
                        ins = pe.transpose(turn[0:KP, 1, u, :], ea[:, h, u, :], G.identb[:])
                    ins.then_inc(*M.half_step("te#", h))

                def encode(h, i):
                    pe.wait_ge(*A.half("ET#", h, i))
                    for q in range(2):
                        pe.wait_ge(*(A.half(f"r#_{q}", 0, i) if h else A.half(f"r#_{q}", 1, i - 1)))
                        for u in range(2 * q, 2 * q + 2):
                            ins = pe.matmul(encp[q][:, u % 2, :], eaT[:, h, u * P:(u + 1) * P], parts[:],
                                            start=True, stop=True)
                        ins.then_inc(*M.half_step(f"enc#_{q}", h))

                def to_edges(h, i):
                    pe.wait_ge(*A.half("T#", h, i))
                    pe.wait_ge(*V.at(f"prod{h}", i - 1))
                    tiles = tiles_of(nc, pe, X, i * IT + h * U, U)
                    for u in range(U):
                        for q in range(3):
                            ins = pe.matmul(hdst[h][:, u, :], ohT[:, h, u * P:(u + 1) * P],
                                            hparts[:, bass.ds(tiles[u], 1), q, 0:D].rearrange("p a w -> p (a w)"),
                                            start=(q == 0), stop=(q == 2))
                    ins.then_inc(*M.step(f"h{h}"))
                    pe.wait_ge(*(V.at("ad0", i) if h else V.at("ad1", i - 1)))
                    for u in range(U):
                        ins = pe.matmul(addst[:, u], ohT[:, h, u * P:(u + 1) * P],
                                        hparts[:, bass.ds(tiles[u], 1), :, D:D + H].rearrange("p a q w -> p (a q) w"),
                                        start=True, stop=True)
                    ins.then_inc(*M.step(f"ad{h}"))

                pe.wait_ge(split, 1)
                turn_over(0, 0)
                pe.wait_ge(*M.at("next_te0", -1))
                pe.sem_inc(*M.skip(2))
                encode(0, 0)
                with pe.Fori(0, n - 1) as i:
                    turn_over(1, i)
                    to_edges(0, i)
                    encode(1, i)
                    turn_over(0, i + 1)
                    to_edges(1, i)
                    encode(0, i + 1)
                turn_over(1, n - 1)
                to_edges(0, n - 1)
                encode(1, n - 1)
                pe.wait_ge(*M.at("enc1_1", n - 1))
                pe.sem_inc(*M.skip(2))
                to_edges(1, n - 1)


def split_rows(nc, tag, rows, parts, rest):
    with ExitStack() as ctx:
        L = Kit(nc, ctx, tag)
        chain = L.sem("chain")
        with nc.Block() as block:
            @block.vector
            def _(dve):
                link = chained(dve, chain)
                left = rows
                for q in range(3):
                    link(dve.tensor_copy(parts[:, :, q, :], left))
                    if q < 2:
                        link(dve.tensor_tensor(rest, left, parts[:, :, q, :], ALU.subtract))
                        left = rest


def finish_l2_gnn(nc, G, acc, bias):
    H, C = 8, 32
    with ExitStack() as ctx:
        L = Kit(nc, ctx, "f2")
        den = L.sb("den", [P, NT, H])
        b = L.sb("b", [P, D])
        loaded, ready = L.sem("loaded"), L.sem("ready")
        V = L.steps("dve_out", "z x1 x2")
        with nc.Block() as block:
            @block.sync
            def _(sp):
                L.open(sp)
                sp.dma_start(b[:], spread(bias, D)).then_inc(loaded, 16)

            @block.vector
            def _(dve):
                link = chained(dve, ready)
                link(dve.tensor_scalar(den[:], acc[:, :, D:D + H], 1e-10, None, ALU.max))
                link(dve.reciprocal(den[:], den[:]))
                dve.wait_ge(loaded, 16)
                with dve.Fori(0, NG) as i:
                    z = acc[:, bass.ds(i * GT, GT), 0:D]
                    zh = z.rearrange("p t (h c) -> p t h c", h=H)
                    xg = G.x[:, bass.ds(i * GT, GT), :]
                    dve.tensor_tensor(zh, zh, den[:, bass.ds(i * GT, GT), :].unsqueeze(3).broadcast_to([P, GT, H, C]),
                                      ALU.mult).then_inc(*V.step("z"))
                    dve.tensor_tensor(xg, xg, b[:].unsqueeze(1).broadcast_to([P, GT, D]), ALU.add).then_inc(*V.step("x1"))
                    dve.wait_ge(*V.at("x1", i))
                    dve.tensor_tensor(xg, xg, z, ALU.add).then_inc(*V.step("x2"))


def relu_experts(nc, G, I, gates):
    n, HALF = 4, GT * P // 2
    S1, S2, E1, E2 = 256, 128, 128, 64
    C1 = S1 // P + n
    with ExitStack() as ctx:
        L = Kit(nc, ctx, "x2")
        nrm = Norm(L, G)
        w1 = L.sb("w1", [P, 2, C1 * P])
        b1 = L.sb("b1", [P, C1])
        w2s = L.sb("w2s", [P, 2, S2])
        w2e = L.sb("w2e", [P, n, E2])
        b2s = L.sb("b2s", [P, 1])
        b2e = L.sb("b2e", [E2, n])
        w3s = L.sb("w3s", [P, D])
        w3e = L.sb("w3e", [E2, n, D])
        h1 = L.sb("h1", [P, C1, GT * P])
        h2s = L.sb("h2s", [P, GT * P])
        h2e = L.sb("h2e", [E2, n, GT * P])
        hp = [[L.ps(f"hp{s}{f}", [P, HALF]) for f in range(2)] for s in range(2)]
        y = [L.ps(f"y{s}", [P, D]) for s in range(2)]
        loaded = L.sem("loaded")
        JOBS = C1 + 1 + n
        M = L.steps("pe_mlp", " ".join(f"j{j}" for j in range(JOBS)) + " " +
                    " ".join(f"y{e}_{u}" for e in range(n + 1) for u in range(GT)))
        A = L.steps("act_relu", " ".join(f"j{j}" for j in range(JOBS)))
        V = L.steps("dve_sum", " ".join(f"x{e}_{u}" for e in range(n + 1) for u in range(GT)))
        with nc.Block() as block:
            @block.sync
            def _(sp):
                L.open(sp)
                with nc.allow_non_contiguous_dma(reason="biases, hidden units to partitions"):
                    for to, a in (
                            (w1[:, :, 0:S1], I["L2_ffn_sW1"].rearrange("(k p) n -> p k n", p=P)),
                            (b1[:, 0:2], I["L2_ffn_sb1"].rearrange("(c p) -> p c", p=P)),
                            (b1[:, 2:C1], I["L2_ffn_eb1"].rearrange("e p -> p e")),
                            (w2s[:], I["L2_ffn_sW2"].rearrange("(k p) n -> p k n", p=P)),
                            (w2e[:], I["L2_ffn_eW2"].rearrange("e p n -> p e n")),
                            (b2s[:], I["L2_ffn_sb2"].rearrange("(p o) -> p o", o=1)),
                            (b2e[:], I["L2_ffn_eb2"].rearrange("e p -> p e")),
                            (w3s[:], I["L2_ffn_sW3"]),
                            (w3e[:], I["L2_ffn_eW3"].rearrange("e p n -> p e n"))):
                        sp.dma_start(to, a).then_inc(loaded, 16)
                    for e in range(n):
                        sp.dma_start(w1[:, :, S1 + e * E1:S1 + (e + 1) * E1],
                                     I["L2_ffn_eW1"][e].rearrange("(k p) n -> p k n", p=P)).then_inc(loaded, 16)

            @block.vector
            def _(dve):
                dve.wait_ge(loaded, 16 * 13)
                with dve.Fori(0, NG) as i:
                    nrm.dve(dve, i)
                    for e in range(n + 1):
                        for u in range(GT):
                            dve.wait_ge(*M.at(f"y{e}_{u}", i))
                            if e:
                                dve.wait_ge(*V.at(f"x{e - 1}_{u}", i))
                            xt = G.x[:, bass.ds(i * GT + u, 1), :].rearrange("p a d -> p (a d)")
                            q = (e * GT + u) % 2
                            if e == 0:
                                dve.tensor_tensor(xt, xt, y[q], ALU.add).then_inc(*V.step(f"x{e}_{u}"))
                            else:
                                g = gates[:, bass.ds(i * GT + u, 1), e - 1:e].rearrange("p a e -> p (a e)")
                                dve.scalar_tensor_tensor(xt, y[q], g, xt, ALU.mult, ALU.add).then_inc(*V.step(f"x{e}_{u}"))

            @block.scalar
            def _(act):
                act.wait_ge(loaded, 16 * 13)
                with act.Fori(0, NG) as i:
                    nrm.act(act, i, M.ended(i))
                    for j in range(JOBS):
                        act.wait_ge(*M.at(f"j{j}", i))
                        for f in range(2):
                            c = slice(f * HALF, (f + 1) * HALF)
                            if j < C1:
                                to, b, rows = h1[:, j, c], b1[:, j:j + 1], P
                            elif j == C1:
                                to, b, rows = h2s[:, c], b2s[:, 0:1], P
                            else:
                                e = j - C1 - 1
                                to, b, rows = h2e[:, e, c], b2e[:, e:e + 1], E2
                            ins = act.activation(to, hp[j % 2][f][0:rows, :], ACT.Relu, bias=b)
                        ins.then_inc(*A.step(f"j{j}"))

            @block.tensor
            def _(pe):
                pe.wait_ge(loaded, 16 * 13)
                with pe.Fori(0, NG) as i:
                    nrm.pe(pe, i)
                    pe.wait_ge(*nrm.C.at(f"cp{GT - 1}", i))
                    for j in range(JOBS):
                        pe.wait_ge(*(A.at(f"j{j - 2}", i) if j >= 2 else A.ended(i)))
                        e = j - C1 - 1
                        if j == C1:
                            pe.wait_ge(*A.at("j1", i))
                        elif j > C1:
                            pe.wait_ge(*A.at(f"j{2 + e}", i))
                        for f in range(2):
                            c = slice(f * HALF, (f + 1) * HALF)
                            if j < C1:
                                for k in range(2):
                                    ins = pe.matmul(hp[j % 2][f], w1[:, k, j * P:(j + 1) * P], nrm.xT[:, k, c],
                                                    start=(k == 0), stop=(k == 1))
                            elif j == C1:
                                for k in range(2):
                                    ins = pe.matmul(hp[j % 2][f], w2s[:, k, :], h1[:, k, c],
                                                    start=(k == 0), stop=(k == 1))
                            else:
                                ins = pe.matmul(hp[j % 2][f][0:E2, :], w2e[:, e, :], h1[:, 2 + e, c],
                                                start=True, stop=True)
                        ins.then_inc(*M.step(f"j{j}"))
                    for e in range(n + 1):
                        pe.wait_ge(*A.at(f"j{C1 + e}", i))
                        for u in range(GT):
                            q = e * GT + u
                            pe.wait_ge(*(V.at(f"x{(q - 2) // GT}_{(q - 2) % GT}", i) if q >= 2 else V.ended(i)))
                            c = slice(u * P, (u + 1) * P)
                            if e == 0:
                                ins = pe.matmul(y[q % 2], h2s[:, c], w3s[:], start=True, stop=True)
                            else:
                                ins = pe.matmul(y[q % 2], h2e[:, e - 1, c], w3e[:, e - 1, :], start=True, stop=True)
                            ins.then_inc(*M.step(f"y{e}_{u}"))


HID = 1024


def counted_nodes(nc, G, table):
    with ExitStack() as ctx:
        L = Kit(nc, ctx, "cn")
        nrm = Norm(L, G)
        rows = L.sb("rows", [P, GT, D + 1])
        ones_set, stored = L.sem("ones_set"), L.sem("stored")
        V = L.steps("dve_rows", "rows")
        with nc.Block() as block:
            @block.sync
            def _(sp):
                L.open(sp)
                sp.sem_inc(stored, 16)
                with sp.Fori(0, NG) as i:
                    sp.wait_ge(*V.at("rows", i))
                    sp.dma_start(rows_of(table, i), rows[:]).then_inc(stored, 16)
                sp.wait_ge(stored, 16 * NG + 16)

            @block.vector
            def _(dve):
                dve.memset(rows[:], 1.0).then_inc(ones_set, 1)
                dve.wait_ge(ones_set, 1)
                with dve.Fori(0, NG) as i:
                    nrm.dve(dve, i)
                    dve.wait_ge(*nrm.V.at("norm", i))
                    dve.wait_ge(stored, i * 16 + 16)
                    dve.tensor_copy(rows[:, :, 0:D], nrm.xn[:]).then_inc(*V.step("rows"))

            @block.scalar
            def _(act):
                with act.Fori(0, NG) as i:
                    nrm.act(act, i, nrm.C.ended(i))

            @block.tensor
            def _(pe):
                with pe.Fori(0, NG) as i:
                    nrm.pe(pe, i)


def gine_pass(nc, G, I, tag, X, table, g_rows, acc):
    K1, W = EF + 1, D + 1
    with ExitStack() as ctx:
        L = Kit(nc, ctx, tag)
        w1 = L.sb("w1", [K1, D])
        row = L.sb("row", [P, IT, W])
        at = L.sb("at", [P, 2, U], I32)
        ea = L.sb("ea", [P, 2, U, K1])
        eaT = L.sb("eaT", [K1, 2, U * P])
        enc = L.sb("enc", [P, 2, U, W])
        oh = L.sb("oh", [P, 2, U, P])
        eturn = L.ps("eturn", [K1, U, P])
        encp = [L.ps(f"encp{q}", [P, 2, D]) for q in range(2)]
        sums = [L.ps(f"sums{q}", [P, 2, 512]) for q in range(2)]
        got, before = L.row_sems(X.chunks // IT)
        took, loaded, ones_set = L.sem("took"), L.sem("loaded"), L.sem("ones_set")
        attrs = [L.sem(f"attrs{h}_") for h in range(2)]
        V = L.steps("dve_gine", "oh1 acc0 acc1 acc2 acc3 acc4 next_oh acc5 acc6 acc7", lead=4)
        A = L.steps("act_gine", "at1 ET1 r1_0 r1_1 next_at next_ET next_r_0 next_r_1", lead=4)
        M = L.steps("pe_gine", "te1 sum0 sum1 enc1_0 sum2 enc1_1 sum3 next_te sum4 sum5 next_enc_0 sum6 next_enc_1 sum7",
                    lead=7)
        n = X.chunks // IT
        attr_rows = g_rows.rearrange("(c p) w -> p c w", p=P)
        with nc.Block() as block:
            @block.sync
            def _(sp):
                L.open(sp)
                sp.dma_start(w1[0:1, :], I["L3_gnn_ee_b1"].rearrange("(o n) -> o n", o=1)).then_inc(loaded, 16)
                sp.dma_start(w1[1:K1, :], I["L3_gnn_ee_w1"]).then_inc(loaded, 16)
                with sp.Fori(0, n) as i:
                    for h in range(2):
                        sp.wait_ge(*(M.at("te1", i - 1) if h else M.at("next_te", i - 2)))
                        sp.dma_start(ea[:, h], attr_rows[:, bass.ds(i * IT + h * U, U), R_ONE:REC]).then_inc(attrs[h], 16)

            @block.gpsimd
            def _(pool):
                with pool.Fori(0, n) as i:
                    for h in range(2):
                        pool.wait_ge(*(A.at("at1", i) if h else A.at("next_at", i - 1)))
                        pool.sem_inc(took, 1)
                        for u in range(U):
                            pool.indirect_dma_start(
                                out=row[:, h * U + u, :], out_offset=None, in_=table,
                                in_offset=bass.IndirectOffsetOnAxis(ap=at[:, h, u:u + 1], axis=0)
                            ).then_inc(got[h * U + u], 16)

            @block.scalar
            def _(act):
                act.wait_ge(ones_set, 1)

                def indices(h, i):
                    act.wait_ge(*M.at(f"sum{h * U + U - 1}", i - 1))
                    act.copy(at[:, h, :], X.src[:, bass.ds(i * IT + h * U, U)]).then_inc(
                        *A.step("at1" if h else "next_at"))

                def encoded(h, i):
                    act.wait_ge(*(M.at("te1", i) if h else M.at("next_te", i - 1)))
                    act.wait_ge(*(M.at("enc1_1", i - 1) if h else M.at("next_enc_1", i - 2)))
                    act.copy(eaT[:, h, :], eturn.rearrange("p u e -> p (u e)")).then_inc(*A.step("ET1" if h else "next_ET"))
                    for q in range(2):
                        act.wait_ge(*(M.at(f"enc1_{q}", i) if h else M.at(f"next_enc_{q}", i - 1)))
                        act.wait_ge(*M.at(f"sum{h * U + 2 * q + 1}", i - 1))
                        act.activation(enc[:, h, 2 * q:2 * q + 2, 0:D], encp[q], ACT.Relu).then_inc(
                            *A.step(f"r1_{q}" if h else f"next_r_{q}"))

                indices(0, 0)
                encoded(0, 0)
                with act.Fori(0, n - 1) as i:
                    indices(1, i)
                    encoded(1, i)
                    indices(0, i + 1)
                    encoded(0, i + 1)
                indices(1, n - 1)
                encoded(1, n - 1)

            @block.vector
            def _(dve):
                dve.memset(enc[:], 1.0).then_inc(ones_set, 1)

                def ones_of(h, i):
                    dve.wait_ge(*M.at(f"sum{h * U + U - 1}", i - 1))
                    one_hots(dve, G, X, oh[:, h], i * IT + h * U).then_inc(*V.step("oh1" if h else "next_oh"))

                def chunks(i, last=False):
                    tiles = tiles_of(nc, dve, X, i * IT)
                    ones_of(1, i)
                    for u in range(IT):
                        a = acc[:, bass.ds(tiles[u], 1), :, :].rearrange("p a q w -> p (a q) w")
                        dve.wait_ge(*M.at(f"sum{u}", i))
                        dve.wait_ge(*(V.at(f"acc{u - 1}", i) if u else V.at(f"acc{IT - 1}", i - 1)))
                        dve.tensor_tensor(a, a, sums[u % 2][:, :, 0:W], ALU.add).then_inc(*V.step(f"acc{u}"))
                        if u == U and last:
                            dve.wait_ge(*V.at(f"acc{U}", i))
                            dve.sem_inc(*V.skip(1))
                        elif u == U:
                            ones_of(0, i + 1)

                ones_of(0, 0)
                dve.wait_ge(*V.at("next_oh", -1))
                dve.sem_inc(*V.skip(3))
                with dve.Fori(0, n - 1) as i:
                    chunks(i)
                chunks(n - 1, last=True)

            @block.tensor
            def _(pe):
                def turn(h, i):
                    pe.wait_ge(attrs[h], i * 16 + 16)
                    pe.wait_ge(*(A.at("next_ET", i - 1) if h else A.at("ET1", i - 1)))
                    for u in range(U):
                        ins = pe.transpose(eturn[:, u, :], ea[:, h, u, :], G.ident[:])
                    ins.then_inc(*M.step("te1" if h else "next_te"))

                def encode(h, i, q):
                    pe.wait_ge(*(A.at("ET1", i) if h else A.at("next_ET", i - 1)))
                    pe.wait_ge(*(A.at(f"next_r_{q}", i - 1) if h else A.at(f"r1_{q}", i - 1)))
                    for u in range(2 * q, 2 * q + 2):
                        ins = pe.matmul(encp[q][:, u % 2, :], eaT[:, h, u * P:(u + 1) * P], w1[:],
                                        start=True, stop=True)
                    ins.then_inc(*M.step(f"enc1_{q}" if h else f"next_enc_{q}"))

                def add(u, i):
                    h = u // U
                    pe.wait_ge(*(V.at("oh1", i) if h else V.at("next_oh", i - 1)))
                    pe.wait_ge(got[u], i * 16 + (16 + before))
                    q = u % U // 2
                    pe.wait_ge(*(A.at(f"r1_{q}", i) if h else A.at(f"next_r_{q}", i - 1)))
                    pe.wait_ge(*(V.at(f"acc{u - 2}", i) if u >= 2 else V.at(f"acc{IT - 2 + u}", i - 1)))
                    pe.matmul(sums[u % 2][:, 0, 0:W], oh[:, h, u % U, :], row[:, u, :], start=True, stop=True)
                    pe.matmul(sums[u % 2][:, 1, 0:W], oh[:, h, u % U, :], enc[:, h, u % U, :], start=True,
                              stop=True).then_inc(*M.step(f"sum{u}"))

                def chunks(i, last=False):
                    turn(1, i)
                    for u in range(IT):
                        if u == U and not last:
                            turn(0, i + 1)
                        if u % U >= 2 and (u < U or not last):
                            encode(1 if u < U else 0, i if u < U else i + 1, u % U - 2)
                        if last and u in (U, U + 2, U + 3):
                            pe.wait_ge(*M.at(f"sum{u - 1}", i))
                            pe.sem_inc(*M.skip(1))
                        add(u, i)

                pe.wait_ge(loaded, 32)
                pe.wait_ge(ones_set, 1)
                turn(0, 0)
                for q in range(2):
                    pe.wait_ge(*(M.at("next_enc_0", -1) if q else M.at("next_te", -1)))
                    pe.sem_inc(*M.skip(1 if q else 2))
                    encode(0, 0, q)
                pe.wait_ge(*M.at("next_enc_1", -1))
                pe.sem_inc(*M.skip(1))
                with pe.Fori(0, n - 1) as i:
                    chunks(i)
                chunks(n - 1, last=True)


def gine_nodes(nc, G, I, table, acc, h0):
    with ExitStack() as ctx:
        L = Kit(nc, ctx, "gn")
        w2 = L.sb("w2", [P, 2, D])
        self1 = L.sb("self1", [P, D])
        b2 = L.sb("b2", [P, D])
        eps2 = L.sb("eps2", [P, 1])
        cnt = L.sb("cnt", [P, NT])
        xn = L.sb("xn", [P, GT, D])
        e = L.sb("e", [P, GT, D])
        eT = L.sb("eT", [P, GT, 2, P])
        h = L.sb("h", [P, GT, D])
        tr = [L.ps(f"tr{s}", [P, 2, P]) for s in range(2)]
        y = [L.ps(f"y{s}", [P, D]) for s in range(2)]
        loaded, ready, rows_in = L.sem("loaded"), L.sem("ready"), L.sem("rows_in")
        V = L.steps("dve_h", "e h " + " ".join(f"c{u} x{u}" for u in range(GT)))
        A = L.steps("act_h", " ".join(f"cp{u}" for u in range(GT)))
        M = L.steps("pe_h", " ".join(f"tr{u}" for u in range(GT)) + " " + " ".join(f"mm{u}" for u in range(GT)))
        with nc.Block() as block:
            @block.sync
            def _(sp):
                L.open(sp)
                sp.dma_start(w2[:], I["L3_gnn_ee_w2"].rearrange("(k p) n -> p k n", p=P)).then_inc(loaded, 16)
                sp.dma_start(self1[:], spread(I["L3_gnn_ee_b1"], D)).then_inc(loaded, 16)
                sp.dma_start(b2[:], spread(I["L3_gnn_ee_b2"], D)).then_inc(loaded, 16)
                sp.dma_start(eps2[:], spread(I["L3_gnn_eps"], 1)).then_inc(loaded, 16)
                with sp.Fori(0, NG) as i:
                    sp.wait_ge(*V.ended(i))
                    sp.dma_start(xn[:], rows_of(table, i)[:, :, 0:D]).then_inc(rows_in, 16)

            @block.vector
            def _(dve):
                link = chained(dve, ready)
                dve.wait_ge(loaded, 64)
                link(dve.tensor_scalar(self1[:], self1[:], 0.0, None, ALU.max))
                link(dve.tensor_scalar(eps2[:], eps2[:], 1.0, 1.0, ALU.add, ALU.add))
                link(dve.tensor_scalar(cnt[:], acc[:, :, 0, D], 1.0, None, ALU.add))
                with dve.Fori(0, NG) as i:
                    g = bass.ds(i * GT, GT)
                    dve.wait_ge(*M.ended(i))
                    dve.tensor_tensor(e[:], acc[:, g, 1, 0:D], self1[:].unsqueeze(1).broadcast_to([P, GT, D]),
                                      ALU.add).then_inc(*V.step("e"))
                    dve.wait_ge(rows_in, i * 16 + 16)
                    dve.wait_ge(*V.ended(i))
                    dve.scalar_tensor_tensor(h[:], xn[:], eps2[:, 0:1], acc[:, g, 0, 0:D], ALU.mult,
                                             ALU.add).then_inc(*V.step("h"))
                    dve.wait_ge(*V.at("h", i))
                    for u in range(GT):
                        dve.scalar_tensor_tensor(h[:, u, :], b2[:], cnt[:, bass.ds(i * GT + u, 1)], h[:, u, :],
                                                 ALU.mult, ALU.add).then_inc(*V.step(f"c{u}"))
                        dve.wait_ge(*V.at(f"c{u}", i))
                        dve.wait_ge(*M.at(f"mm{u}", i))
                        dve.tensor_tensor(h0[:, bass.ds(i * GT + u, 1), :].rearrange("p a d -> p (a d)"), h[:, u, :],
                                          y[u % 2], ALU.add).then_inc(*V.step(f"x{u}"))

            @block.scalar
            def _(act):
                with act.Fori(0, NG) as i:
                    act.wait_ge(*M.ended(i))
                    for u in range(GT):
                        act.wait_ge(*M.at(f"tr{u}", i))
                        act.copy(eT[:, u], tr[u % 2]).then_inc(*A.step(f"cp{u}"))

            @block.tensor
            def _(pe):
                pe.wait_ge(loaded, 64)
                with pe.Fori(0, NG) as i:
                    pe.wait_ge(*V.at("e", i))
                    pe.wait_ge(*A.ended(i))
                    for u in range(GT):
                        if u >= 2:
                            pe.wait_ge(*A.at(f"cp{u - 2}", i))
                        for k in range(2):
                            ins = pe.transpose(tr[u % 2][:, k, :], e[:, u, k * P:(k + 1) * P], G.ident[:])
                        ins.then_inc(*M.step(f"tr{u}"))
                    for u in range(GT):
                        pe.wait_ge(*A.at(f"cp{u}", i))
                        pe.wait_ge(*(V.at(f"x{u - 2}", i) if u >= 2 else V.ended(i)))
                        for k in range(2):
                            ins = pe.matmul(y[u % 2], eT[:, u, k, :], w2[:, k, :], start=(k == 0), stop=(k == 1))
                        ins.then_inc(*M.step(f"mm{u}"))


def gine_mlp(nc, G, I, table, h0):
    KH = HID // P
    with ExitStack() as ctx:
        L = Kit(nc, ctx, "gm")
        w1 = L.sb("w1", [P, 2, HID])
        w2 = L.sb("w2", [P, KH, HID])
        w3 = L.sb("w3", [P, KH, D])
        par = L.sb("par", [P, 6, HID])
        last = L.sb("last", [P, 3, D])
        xn = L.sb("xn", [P, GT, D])
        hs = L.sb("hs", [P, GT, D])
        inT = L.sb("inT", [P, 2, KH, P])
        z = L.sb("z", [P, GT, HID])
        stats = L.sb("stats", [P, GT, 2, 6])
        mv = L.sb("mv", [P, GT, 2])
        var = L.sb("var", [P, GT])
        std = L.sb("std", [P, GT])
        rstd = L.sb("rstd", [P, GT])
        tr = [L.ps(f"tr{s}", [P, 4, P]) for s in range(2)]
        big = [L.ps(f"big{s}", [P, HID]) for s in range(2)]
        small = [L.ps(f"small{s}", [P, D]) for s in range(2)]
        loaded, rows_in, took = L.sem("loaded"), L.sem("rows_in"), L.sem("took")
        jobs = [(l, u) for l in range(3) for u in range(GT)]

        def turns(l):
            return range(1 if l == 0 else 2)

        PEN = "tr0_0_0 "
        ACN = "hs T0_0_0 "
        DVN = ""
        for (l, u), after in zip(jobs, jobs[1:] + [None]):
            if after:
                for b in turns(after[0]):
                    PEN += f"tr{after[0]}_{after[1]}_{b} "
                    ACN += f"T{after[0]}_{after[1]}_{b} "
            PEN += f"mm{l}_{u} "
            DVN += f"b{l}_{u} " + ("xn%d " % u if l == 2 else "") + f"st{l}_{u} ag{l}_{u} ep{l}_{u} rs{l}_{u} g{l}_{u} be{l}_{u} "
            if l < 2:
                ACN += f"sq{l}_{u} relu{l}_{u} "
            else:
                ACN += f"sq{l}_{u} "
                DVN += f"x{u} "
        M = L.steps("pe_mlp", PEN)
        A = L.steps("act_mlp", ACN)
        V = L.steps("dve_mlp", DVN)
        with nc.Block() as block:
            @block.sync
            def _(sp):
                L.open(sp)
                sp.dma_start(w1[:], I["L3_gnn_w1"].rearrange("(k p) n -> p k n", p=P)).then_inc(loaded, 16)
                sp.dma_start(w2[:], I["L3_gnn_w2"].rearrange("(k p) n -> p k n", p=P)).then_inc(loaded, 16)
                sp.dma_start(w3[:], I["L3_gnn_w3"].rearrange("(k p) n -> p k n", p=P)).then_inc(loaded, 16)
                for q, name in enumerate(("b1", "g1", "be1", "b2", "g2", "be2")):
                    sp.dma_start(par[:, q, :], spread(I["L3_gnn_" + name], HID)).then_inc(loaded, 16)
                for q, name in enumerate(("b3", "bn_g", "bn_b")):
                    sp.dma_start(last[:, q, :], spread(I["L3_gnn_" + name], D)).then_inc(loaded, 16)
                with sp.Fori(0, NG) as i:
                    sp.wait_ge(*V.ended(i))
                    sp.dma_start(xn[:], rows_of(table, i)[:, :, 0:D]).then_inc(rows_in, 16)

            @block.vector
            def _(dve):
                dve.wait_ge(loaded, 16 * 12)
                with dve.Fori(0, NG) as i:
                    for l in range(3):
                        for u in range(GT):
                            zt = z[:, u, 0:HID if l < 2 else D]
                            b, g, be = ((par[:, 3 * l + q, :] for q in range(3)) if l < 2 else
                                        (last[:, q, :] for q in range(3)))
                            src = big[(l * GT + u) % 2] if l < 2 else small[u % 2]
                            dve.wait_ge(*M.at(f"mm{l}_{u}", i))
                            if l == 0:
                                dve.wait_ge(*V.ended(i))
                            dve.tensor_tensor(zt, src, b, ALU.add).then_inc(*V.step(f"b{l}_{u}"))
                            dve.wait_ge(*V.at(f"b{l}_{u}", i))
                            if l == 2:
                                dve.wait_ge(rows_in, i * 16 + 16)
                                dve.tensor_tensor(zt, zt, xn[:, u, :], ALU.add).then_inc(*V.step(f"xn{u}"))
                                dve.wait_ge(*V.at(f"xn{u}", i))
                                ins = dve.bn_stats(stats[:, u, 0, :], zt)
                            else:
                                for f in range(2):
                                    ins = dve.bn_stats(stats[:, u, f, :], z[:, u, f * 512:(f + 1) * 512])
                            ins.then_inc(*V.step(f"st{l}_{u}"))
                            dve.wait_ge(*V.at(f"st{l}_{u}", i))
                            dve.sem_inc(took, 1)
                            if l < 2:
                                ins = dve.bn_aggr(mv[:, u, :], stats[:, u].rearrange("p f s -> p (f s)"))
                            else:
                                ins = dve.bn_aggr(mv[:, u, :], stats[:, u, 0, :])
                            ins.then_inc(*V.step(f"ag{l}_{u}"))
                            dve.wait_ge(*V.at(f"ag{l}_{u}", i))
                            dve.tensor_scalar(var[:, u:u + 1], mv[:, u, 1:2], EPS, None, ALU.add).then_inc(*V.step(f"ep{l}_{u}"))
                            dve.wait_ge(*A.at(f"sq{l}_{u}", i))
                            dve.reciprocal(rstd[:, u:u + 1], std[:, u:u + 1]).then_inc(*V.step(f"rs{l}_{u}"))
                            dve.wait_ge(*V.at(f"rs{l}_{u}", i))
                            dve.scalar_tensor_tensor(zt, zt, mv[:, u, 0:1], g, ALU.subtract, ALU.mult).then_inc(*V.step(f"g{l}_{u}"))
                            dve.wait_ge(*V.at(f"g{l}_{u}", i))
                            dve.scalar_tensor_tensor(zt, zt, rstd[:, u:u + 1], be, ALU.mult, ALU.add).then_inc(*V.step(f"be{l}_{u}"))
                            if l == 2:
                                dve.wait_ge(*V.at(f"be{l}_{u}", i))
                                xt = G.x[:, bass.ds(i * GT + u, 1), :].rearrange("p a d -> p (a d)")
                                dve.scalar_tensor_tensor(xt, zt, 0.0, xt, ALU.max, ALU.add).then_inc(*V.step(f"x{u}"))

            @block.scalar
            def _(act):
                def turned(i, l, u):
                    for b in turns(l):
                        act.wait_ge(*M.at(f"tr{l}_{u}_{b}", i))
                        if b == 0:
                            q = l * GT + u - 2
                            act.wait_ge(*(M.at(f"mm{q // GT}_{q % GT}", i) if q >= 0 else M.ended(i)))
                        m = 2 if l == 0 else 4
                        act.copy(inT[:, (l * GT + u) % 2, 4 * b:4 * b + m, :], tr[b][:, 0:m, :]).then_inc(*A.step(f"T{l}_{u}_{b}"))

                with act.Fori(0, NG) as i:
                    act.wait_ge(*M.ended(i))
                    act.copy(hs[:], h0[:, bass.ds(i * GT, GT), :]).then_inc(*A.step("hs"))
                    turned(i, 0, 0)
                    for (l, u), after in zip(jobs, jobs[1:] + [None]):
                        if after:
                            turned(i, *after)
                        act.wait_ge(*V.at(f"ep{l}_{u}", i))
                        act.activation(std[:, u:u + 1], var[:, u:u + 1], ACT.Sqrt).then_inc(*A.step(f"sq{l}_{u}"))
                        if l < 2:
                            act.wait_ge(*V.at(f"be{l}_{u}", i))
                            act.activation(z[:, u, :], z[:, u, :], ACT.Relu).then_inc(*A.step(f"relu{l}_{u}"))

            @block.tensor
            def _(pe):
                def turn(i, l, u):
                    pe.wait_ge(*(A.at("hs", i) if l == 0 else A.at(f"relu{l - 1}_{u}", i)))
                    src = hs if l == 0 else z
                    for b in turns(l):
                        if u:
                            pe.wait_ge(*A.at(f"T{l}_{u - 1}_{b}", i))
                        elif l:
                            pe.wait_ge(*A.at(f"T{l - 1}_{GT - 1}_{b if l > 1 else 0}", i))
                        m = 2 if l == 0 else 4
                        for k in range(4 * b, 4 * b + m):
                            ins = pe.transpose(tr[b][:, k % 4, :], src[:, u, k * P:(k + 1) * P], G.ident[:])
                        ins.then_inc(*M.step(f"tr{l}_{u}_{b}"))

                pe.wait_ge(loaded, 16 * 12)
                with pe.Fori(0, NG) as i:
                    turn(i, 0, 0)
                    for (l, u), after in zip(jobs, jobs[1:] + [None]):
                        if after:
                            turn(i, *after)
                        pe.wait_ge(*A.at(f"T{l}_{u}_{0 if l == 0 else 1}", i))
                        if l < 2:
                            q = l * GT + u - 2
                            pe.wait_ge(*(V.at(f"b{q // GT}_{q % GT}", i) if q >= 0 else V.ended(i)))
                        else:
                            pe.wait_ge(*(V.at(f"b{l}_{u - 2}", i) if u >= 2 else V.ended(i)))
                        K = 2 if l == 0 else KH
                        w = (w1, w2, w3)[l]
                        s = (l * GT + u) % 2
                        for f in range(2 if l < 2 else 1):
                            c = slice(f * 512, (f + 1) * 512) if l < 2 else slice(0, D)
                            out = (big[s] if l < 2 else small[u % 2])[:, c]
                            for k in range(K):
                                ins = pe.matmul(out, inT[:, s, k, :], w[:, k, c], start=(k == 0), stop=(k == K - 1))
                        ins.then_inc(*M.step(f"mm{l}_{u}"))


SH, SG = 8, 64
PR = SH // 2
FULL = SH * SG


def slice_logits_weights(nc, G, I, wl, bl):
    with ExitStack() as ctx:
        L = Kit(nc, ctx, "t0")
        wx = L.sb("wx", [P, 2, FULL])
        wxT = L.sb("wxT", [SG, SH, 2, P])
        ws = L.sb("ws", [SG, SG])
        bx = L.sb("bx", [SG, SH])
        bxr = L.sb("bxr", [SG, SH, P])
        bs = L.sb("bs", [P, SG])
        temp = L.sb("temp", [P, SH])
        turn = [L.ps(f"turn{q}", [SG, 2, 2, P]) for q in range(PR)]
        y = [L.ps(f"y{k}", [P, SH, SG]) for k in range(3)]
        loaded, bias_loaded, turned, copied = L.sem("loaded"), L.sem("bias_loaded"), L.sem("turned"), L.sem("copied")
        spread_out, product, chain = L.sem("spread_out"), L.sem("product"), L.sem("chain")
        with nc.Block() as block:
            @block.sync
            def _(sp):
                sp.dma_start(wx[:], I["L3_ffn_W_x"].rearrange("(k p) n -> p k n", p=P)).then_inc(loaded, 16)
                sp.dma_start(ws[:], I["L3_ffn_W_slice"]).then_inc(loaded, 16)
                with nc.allow_non_contiguous_dma(reason="a bias, features to partitions"):
                    sp.dma_start(bx[:], I["L3_ffn_b_x"].rearrange("(h c) -> c h", h=SH)).then_inc(bias_loaded, 16)
                sp.dma_start(bs[:], spread(I["L3_ffn_b_slice"], SG)).then_inc(bias_loaded, 16)
                sp.dma_start(temp[:], spread(I["L3_ffn_temperature"].rearrange("a h b c -> (a h b c)"),
                                             SH)).then_inc(bias_loaded, 16)

            @block.tensor
            def _(pe):
                pe.wait_ge(loaded, 32)
                for h in range(SH):
                    for k in range(2):
                        ins = pe.transpose(turn[h // 2][:, h % 2, k, :], wx[:, k, h * SG:(h + 1) * SG], G.ident[:])
                    if h % 2:
                        ins.then_inc(turned, 1)
                pe.wait_ge(copied, PR)
                for k in range(2):
                    for h in range(SH):
                        ins = pe.matmul(y[k][:, h, :], wxT[:, h, k, :], ws[:], start=True, stop=True)
                    ins.then_inc(product, 1)
                pe.wait_ge(spread_out, 1)
                for h in range(SH):
                    ins = pe.matmul(y[2][:, h, :], bxr[:, h, :], ws[:], start=True, stop=True)
                ins.then_inc(product, 1)

            @block.scalar
            def _(act):
                for q in range(PR):
                    act.wait_ge(turned, q + 1)
                    act.copy(wxT[:, 2 * q:2 * q + 2], turn[q]).then_inc(copied, 1)

            @block.vector
            def _(dve):
                link = chained(dve, chain)
                dve.wait_ge(bias_loaded, 48)
                dve.tensor_copy(bxr[:], bx[:].unsqueeze(2).broadcast_to([SG, SH, P])).then_inc(spread_out, 1)
                link(dve.tensor_scalar(temp[:], temp[:], 0.1, 5.0, ALU.max, ALU.min))
                link(dve.reciprocal(temp[:], temp[:]))
                per = temp[:].unsqueeze(2).broadcast_to([P, SH, SG])
                for k in range(2):
                    dve.wait_ge(product, k + 1)
                    link(dve.tensor_tensor(wl[:, k, :].rearrange("p (h g) -> p h g", h=SH), y[k], per, ALU.mult))
                b = bl[:].rearrange("p (h g) -> p h g", h=SH)
                dve.wait_ge(product, 3)
                link(dve.tensor_tensor(b, y[2], bs[:].unsqueeze(1).broadcast_to([P, SH, SG]), ALU.add))
                link(dve.tensor_tensor(b, b, per, ALU.mult))


def slice_pass(nc, G, I, wl, bl, wT, tok):
    with ExitStack() as ctx:
        L = Kit(nc, ctx, "t1")
        nrm = Norm(L, G)
        wf = L.sb("wf", [P, 2, FULL])
        bf = L.sb("bf", [P, FULL])
        fx = L.sb("fx", [P, GT, PR, P + 1])
        w = L.sb("w", [P, GT, FULL])
        top = L.sb("top", [P, GT, SH])
        sums = L.sb("sums", [P, GT, SH])
        valid = L.sb("valid", [P, NT])
        fxp = L.ps("fxp", [P, PR, P])
        lgp = L.ps("lgp", [P, FULL])
        turn = [L.ps(f"turn{s}", [P, PR, P]) for s in range(2)]
        total = [L.ps(f"total{s}", [P, 2, P + 1]) for s in range(2)]
        loaded, filled = L.sem("loaded"), L.sem("filled")
        us = range(GT)
        M = L.steps("pe_slices", " ".join(f"fx{u} lg{u}" for u in us) + " " + " ".join(f"tr{u}" for u in us) + " sum0 sum1")
        V = L.steps("dve_softmax", " ".join(f"fx{u} lg{u}" for u in us) + " top less sum inv valid w tok0 tok1")
        A = L.steps("act_exp", "exp " + " ".join(f"cp{u}" for u in us))
        with nc.Block() as block:
            @block.sync
            def _(sp):
                L.open(sp)
                sp.dma_start(wf[:], I["L3_ffn_W_fx"].rearrange("(k p) n -> p k n", p=P)).then_inc(loaded, 16)
                sp.dma_start(bf[:], spread(I["L3_ffn_b_fx"], FULL)).then_inc(loaded, 16)

            @block.vector
            def _(dve):
                dve.memset(tok[:], 0.0).then_inc(filled, 1)
                dve.memset(fx[:, :, :, P:P + 1], 1.0).then_inc(filled, 1)
                dve.memset(valid[:, 0:NT - 1], 1.0).then_inc(filled, 1)
                dve.tensor_scalar(valid[:, NT - 1:NT], G.part[:, 0:1], float(N - (NT - 1) * P), None,
                                  ALU.is_lt).then_inc(filled, 1)
                dve.wait_ge(filled, 4)
                dve.wait_ge(loaded, 32)
                with dve.Fori(0, NG) as i:
                    nrm.dve(dve, i)
                    dve.wait_ge(*M.ended(i))
                    for u in us:
                        dve.wait_ge(*M.at(f"fx{u}", i))
                        dve.tensor_tensor(fx[:, u, :, 0:P], fxp, bf[:].rearrange("p (q c) -> p q c", q=PR),
                                          ALU.add).then_inc(*V.step(f"fx{u}"))
                        dve.wait_ge(*M.at(f"lg{u}", i))
                        dve.tensor_tensor(w[:, u, :], lgp, bl[:], ALU.add).then_inc(*V.step(f"lg{u}"))
                    heads = w[:].rearrange("p u (h g) -> p (u h) g", h=SH)

                    def per(a):
                        return a[:].rearrange("p u h -> p (u h)").unsqueeze(2).broadcast_to([P, GT * SH, SG])
                    dve.wait_ge(*V.at(f"lg{GT - 1}", i))
                    dve.tensor_reduce(top[:].rearrange("p u h -> p (u h)"), heads, AX.X, ALU.max).then_inc(*V.step("top"))
                    dve.wait_ge(*V.at("top", i))
                    dve.tensor_tensor(heads, heads, per(top), ALU.subtract).then_inc(*V.step("less"))
                    dve.wait_ge(*A.at("exp", i))
                    dve.tensor_reduce(sums[:].rearrange("p u h -> p (u h)"), heads, AX.X, ALU.add).then_inc(*V.step("sum"))
                    dve.wait_ge(*V.at("sum", i))
                    dve.reciprocal(sums[:], sums[:]).then_inc(*V.step("inv"))
                    dve.wait_ge(*V.at("inv", i))
                    dve.tensor_tensor(sums[:], sums[:], valid[:, bass.ds(i * GT, GT)].unsqueeze(2)
                                      .broadcast_to([P, GT, SH]), ALU.mult).then_inc(*V.step("valid"))
                    dve.wait_ge(*V.at("valid", i))
                    dve.tensor_tensor(heads, heads, per(sums), ALU.mult).then_inc(*V.step("w"))
                    for s in range(2):
                        dve.wait_ge(*M.at(f"sum{s}", i))
                        dve.tensor_tensor(tok[:, 2 * s:2 * s + 2, :], tok[:, 2 * s:2 * s + 2, :], total[s],
                                          ALU.add).then_inc(*V.step(f"tok{s}"))

            @block.scalar
            def _(act):
                act.wait_ge(loaded, 32)
                with act.Fori(0, NG) as i:
                    nrm.act(act, i, M.ended(i))
                    act.wait_ge(*V.at("less", i))
                    act.activation(w[:], w[:], ACT.Exp).then_inc(*A.step("exp"))
                    for u in us:
                        act.wait_ge(*M.at(f"tr{u}", i))
                        act.copy(wT[:, :, bass.ds(i * (GT * P) + u * P, P)], turn[u % 2]).then_inc(*A.step(f"cp{u}"))

            @block.tensor
            def _(pe):
                pe.wait_ge(loaded, 32)
                with pe.Fori(0, NG) as i:
                    nrm.pe(pe, i)
                    for u in us:
                        pe.wait_ge(*nrm.C.at(f"cp{u}", i))
                        xT = nrm.xT[:, :, u * P:(u + 1) * P]
                        pe.wait_ge(*(V.at(f"fx{u - 1}", i) if u else V.ended(i)))
                        for k in range(2):
                            ins = pe.matmul(fxp.rearrange("p q c -> p (q c)"), xT[:, k, :], wf[:, k, :],
                                            start=(k == 0), stop=(k == 1))
                        ins.then_inc(*M.step(f"fx{u}"))
                        if u:
                            pe.wait_ge(*V.at(f"lg{u - 1}", i))
                        for k in range(2):
                            ins = pe.matmul(lgp, xT[:, k, :], wl[:, k, :], start=(k == 0), stop=(k == 1))
                        ins.then_inc(*M.step(f"lg{u}"))
                    pe.wait_ge(*V.at("w", i))
                    for u in us:
                        pe.wait_ge(*(A.at(f"cp{u - 2}", i) if u >= 2 else A.ended(i)))
                        for q in range(PR):
                            ins = pe.transpose(turn[u % 2][:, q, :], w[:, u, q * P:(q + 1) * P], G.ident[:])
                        ins.then_inc(*M.step(f"tr{u}"))
                    for s in range(2):
                        for q in range(2):
                            pair = 2 * s + q
                            for u in us:
                                ins = pe.matmul(total[s][:, q, :], w[:, u, pair * P:(pair + 1) * P],
                                                fx[:, u, pair, :], start=(u == 0), stop=(u == GT - 1))
                        ins.then_inc(*M.step(f"sum{s}"))


def slice_attention(nc, G, I, tok, M4):
    with ExitStack() as ctx:
        L = Kit(nc, ctx, "t2")
        wq = L.sb("wq", [SG, 3, SG])
        wo = L.sb("wo", [P, PR, D])
        inv = L.sb("inv", [P, PR])
        t = L.sb("t", [P, PR, SG])
        tT = L.sb("tT", [SG, PR * P])
        qk = L.sb("qk", [SG, 2, PR * P])
        v = L.sb("v", [P, PR, P])
        a = L.sb("a", [P, PR, SG])
        ab = L.sb("ab", [P, PR, P])
        abT = L.sb("abT", [P, PR, P])
        osT = L.sb("osT", [P, PR, P])
        top = L.sb("top", [P, PR])
        turn = L.ps("turn", [P, PR, P])
        qkp = [L.ps(f"qkp{s}", [SG, PR * P]) for s in range(2)]
        vp = L.ps("vp", [P, PR, SG])
        lg = L.ps("lg", [P, PR, P])
        op = L.ps("op", [P, PR, P])
        mp = [L.ps(f"mp{s}", [P, 2, D]) for s in range(2)]
        loaded, chain, worked, exps = L.sem("loaded"), L.sem("chain"), L.sem("worked"), L.sem("exps")
        done = L.sem("done")
        halves = [(slice(f * SG, (f + 1) * SG), slice(f * SG, (f + 1) * SG)) for f in range(2)]
        with nc.Block() as block:
            @block.sync
            def _(sp):
                for n, name in enumerate(("L3_ffn_W_q", "L3_ffn_W_k", "L3_ffn_W_v")):
                    sp.dma_start(wq[:, n, :], I[name]).then_inc(loaded, 16)
                sp.dma_start(wo[:], I["L3_ffn_W_out"].rearrange("(q p) n -> p q n", p=P)).then_inc(loaded, 16)

            @block.vector
            def _(dve):
                link = chained(dve, chain)
                link(dve.memset(v[:], 0.0))
                link(dve.memset(ab[:], 0.0))
                link(dve.tensor_scalar(inv[:], tok[:, :, P], 1e-5, None, ALU.add))
                link(dve.reciprocal(inv[:], inv[:]))
                for p, c in halves:
                    link(dve.tensor_tensor(t[p], tok[p, :, c], inv[p].unsqueeze(2).broadcast_to([SG, PR, SG]), ALU.mult))
                dve.sem_inc(done, 1)
                dve.wait_ge(worked, 1)
                link(dve.tensor_copy(tT[:], turn[0:SG].rearrange("p q c -> p (q c)")))
                dve.sem_inc(done, 1)
                dve.wait_ge(worked, 2)
                for s in range(2):
                    link(dve.tensor_copy(qk[:, s, :], qkp[s]))
                dve.sem_inc(done, 1)
                for p, c in halves:
                    link(dve.tensor_copy(v[p, :, c], vp[p]))
                dve.wait_ge(worked, 3)
                for p, c in halves:
                    link(dve.tensor_scalar(a[p], lg[p, :, c], SG ** -0.5, None, ALU.mult))
                link(dve.tensor_reduce(top[:], a[:], AX.X, ALU.max))
                link(dve.tensor_tensor(a[:], a[:], top[:].unsqueeze(2).broadcast_to([P, PR, SG]), ALU.subtract))
                dve.sem_inc(done, 1)
                dve.wait_ge(exps, 1)
                link(dve.tensor_reduce(top[:], a[:], AX.X, ALU.add))
                link(dve.reciprocal(top[:], top[:]))
                for p, c in halves:
                    link(dve.tensor_tensor(ab[p, :, c], a[p], top[p].unsqueeze(2).broadcast_to([SG, PR, SG]), ALU.mult))
                dve.sem_inc(done, 1)
                dve.wait_ge(worked, 4)
                link(dve.tensor_copy(abT[:], turn))
                dve.sem_inc(done, 1)
                dve.wait_ge(worked, 5)
                link(dve.tensor_copy(osT[:], op))
                dve.sem_inc(done, 1)
                dve.wait_ge(worked, 6)
                for s in range(2):
                    link(dve.tensor_copy(M4[:, 2 * s:2 * s + 2, :], mp[s]))

            @block.scalar
            def _(act):
                act.wait_ge(done, 4)
                act.activation(a[:], a[:], ACT.Exp).then_inc(exps, 1)

            @block.tensor
            def _(pe):
                def pairs(work):
                    for q in range(PR):
                        ins = work(q, slice(q * P, (q + 1) * P))
                    ins.then_inc(worked, 1)
                pe.wait_ge(loaded, 64)
                pe.wait_ge(done, 1)
                pairs(lambda q, c: pe.transpose(turn[0:SG, q, :], t[:, q, :], G.ident[:]))
                pe.wait_ge(done, 2)
                for s in range(2):
                    pe.matmul(qkp[s], wq[:, s, :], tT[:], start=True, stop=True)
                pairs(lambda q, c: pe.matmul(vp[:, q, :], tT[:, c], wq[:, 2, :], start=True, stop=True))
                pe.wait_ge(done, 3)
                pairs(lambda q, c: pe.matmul(lg[:, q, :], qk[:, 0, c], qk[:, 1, c], start=True, stop=True))
                pe.wait_ge(done, 5)
                pairs(lambda q, c: pe.transpose(turn[:, q, :], ab[:, q, :], G.ident[:]))
                pe.wait_ge(done, 6)
                pairs(lambda q, c: pe.matmul(op[:, q, :], v[:, q, :], abT[:, q, :], start=True, stop=True))
                pe.wait_ge(done, 7)
                pairs(lambda q, c: pe.matmul(mp[q // 2][:, q % 2, :], osT[:, q, :], wo[:, q, :], start=True, stop=True))


def unslice(nc, G, I, wT, M4):
    with ExitStack() as ctx:
        L = Kit(nc, ctx, "t3")
        st = L.sb("st", [P, 2, PR, P])
        bo = L.sb("bo", [P, D])
        y = [L.ps(f"y{s}", [P, D]) for s in range(2)]
        loaded = L.sem("loaded")
        us = range(GT)
        A = L.steps("act_staged", " ".join(f"st{u}" for u in us))
        M = L.steps("pe_out", " ".join(f"mm{u}" for u in us))
        V = L.steps("dve_out", "bias " + " ".join(f"x{u}" for u in us))
        with nc.Block() as block:
            @block.sync
            def _(sp):
                L.open(sp)
                sp.dma_start(bo[:], spread(I["L3_ffn_b_out"], D)).then_inc(loaded, 16)

            @block.scalar
            def _(act):
                with act.Fori(0, NG) as i:
                    for u in us:
                        act.wait_ge(*(M.at(f"mm{u - 2}", i) if u >= 2 else M.ended(i)))
                        act.copy(st[:, u % 2], wT[:, :, bass.ds(i * (GT * P) + u * P, P)]).then_inc(*A.step(f"st{u}"))

            @block.tensor
            def _(pe):
                with pe.Fori(0, NG) as i:
                    for u in us:
                        pe.wait_ge(*A.at(f"st{u}", i))
                        pe.wait_ge(*(V.at(f"x{u - 2}", i) if u >= 2 else V.ended(i)))
                        for q in range(PR):
                            ins = pe.matmul(y[u % 2], st[:, u % 2, q, :], M4[:, q, :], start=(q == 0), stop=(q == PR - 1))
                        ins.then_inc(*M.step(f"mm{u}"))

            @block.vector
            def _(dve):
                dve.wait_ge(loaded, 16)
                with dve.Fori(0, NG) as i:
                    xs = G.x[:, bass.ds(i * GT, GT), :]
                    dve.tensor_tensor(xs, xs, bo[:].unsqueeze(1).broadcast_to([P, GT, D]), ALU.add).then_inc(*V.step("bias"))
                    dve.wait_ge(*V.at("bias", i))
                    for u in us:
                        dve.wait_ge(*M.at(f"mm{u}", i))
                        xt = G.x[:, bass.ds(i * GT + u, 1), :].rearrange("p a d -> p (a d)")
                        dve.tensor_tensor(xt, xt, y[u % 2], ALU.add).then_inc(*V.step(f"x{u}"))


def program(nc, I, out):
    with ExitStack() as ctx:
        K = Kit(nc, ctx, "")
        K.row_sems()
        G = Globals()
        constants(nc, K, G, I["src"][0:8].rearrange("(o n) -> o n", o=1))
        X = Edges(K, "g_", NCH)
        R = Edges(K, "r_", FNC)

        def dram(name, shape):
            return nc.dram_tensor(name, shape, F32, kind="Internal").ap()

        g_rows, r_rows = dram("g_rows", [P * NCH, REC]), dram("r_rows", [P * FNC, 2])
        with ExitStack() as sorting:
            S = Kit(nc, sorting, "so")
            graph = GraphRecords(nc, S, I, g_rows)
            router = S.sb("router", [P, FEJ, 2])
            router_pad = S.sb("router_pad", [P, 32, 2])
            graph.prepare("pg", router_pad)
            fill_router(nc, G, I, router, router_pad, r_rows)
            sort_edges(nc, G, "sr", FEJ, 2, router, r_rows, R, meanwhile=graph.load)
            graph.convert("cg")
            sort_edges(nc, G, "sg", EJ, REC, graph.rec, g_rows, X)
        field = K.sb("field", [P, NCH, 9])
        load_edges(nc, "lr", R, r_rows, 2)
        load_edges(nc, "lg", X, g_rows, REC, field)
        G.x = K.sb("x_sb", [P, NT, D])
        xin = K.sem("xin")
        full = N // P
        with nc.Block() as block:
            @block.vector
            def _(dve):
                dve.memset(G.x[:, full, :], 0.0).then_inc(xin, 1)

            @block.sync
            def _(sp):
                sp.wait_ge(xin, 1)
                sp.dma_start(G.x[:, 0:full, :], I["x"][0:full * P, :].rearrange("(t p) d -> p t d", p=P)).then_inc(xin, 16)
                sp.dma_start(G.x[0:N - full * P, full, :], I["x"][full * P:N, :]).then_inc(xin, 16)
                sp.wait_ge(xin, 33)
        T = Tables(dram)
        for sublayer in SUBLAYERS:
            sublayer(nc, G, I, X, R, field, g_rows, T)
        stored = K.sem("stored")
        with nc.Block() as block:
            @block.sync
            def _(sp):
                sp.dma_start(out[0:full * P, :].rearrange("(t p) d -> p t d", p=P), G.x[:, 0:full, :]).then_inc(stored, 16)
                sp.dma_start(out[full * P:N, :], G.x[0:N - full * P, full, :]).then_inc(stored, 16)
                sp.wait_ge(stored, 32)


class Tables:

    def __init__(self, dram):
        self.rows = dram("rows", [NP, D])
        self.logit = dram("logit", [NP, 8])
        self.router = dram("router", [NP, 20])
        self.counted = dram("counted", [NP, D + 1])


def layer0_gnn(nc, G, I, X, R, field, g_rows, T):
    H = 8
    with ExitStack() as ctx:
        L = Kit(nc, ctx, "l0")
        acc = L.sb("acc", [P, NT, D + H])
        alpha = L.sb("alpha", [P, NCH, H])
        ar = L.sb("ar", [P, NT, H])
        clear(nc, "c0", acc[:])
        gat_nodes(nc, G, I, "a0", I["L0_gnn_W_lin"], I["L0_gnn_W_res"],
                  I["L0_gnn_att_l"].rearrange("a h c -> (a h c)"), I["L0_gnn_att_r"].rearrange("a h c -> (a h c)"),
                  T.rows, T.logit, lambda i: ar[:, bass.ds(i * GT, GT), :])
        attention_pass(nc, G, "b0", X, H, T.logit, H, 0, ar, alpha, weight=field[:, :, R_EW])
        softmax_pass(nc, G, "s0", X, H, alpha[:])
        message_pass(nc, G, "m0", X, H, 32, T.rows, alpha, acc)
        finish_l0_gnn(nc, G, acc)


def layer0_experts(nc, G, I, X, R, field, g_rows, T):
    with ExitStack() as ctx:
        L = Kit(nc, ctx, "l0f")
        gates = L.sb("gates", [P, NT, 4])
        b2 = L.sb("b2", [4, D])
        with ExitStack() as inner:
            L2 = Kit(nc, inner, "l0r")
            acc = L2.sb("acc", [P, NT, 20])
            alpha = L2.sb("alpha", [P, FNC, 4])
            hrow = L2.sb("hrow", [P, FNC, 16])
            ad = L2.sb("ad", [P, NT, 4])
            clear(nc, "c1", acc[:])
            router_nodes(nc, G, I, T.router, ad)
            attention_pass(nc, G, "b1", R, 4, T.router, 20, 16, ad, alpha, keep=hrow)
            softmax_pass(nc, G, "s1", R, 4, alpha[:])
            message_pass(nc, G, "m1", R, 4, 4, None, alpha, acc, rows=hrow)
            router_gates(nc, G, I, acc, gates)
        gelu_experts(nc, G, "e0", I["L0_ffn_W1"], I["L0_ffn_b1"], I["L0_ffn_W2"], gates, 4)
        load(nc, "lb0", b2[:], I["L0_ffn_b2"])
        gate_bias(nc, G, "gb0", gates, 4, b2)


def layer1_gnn(nc, G, I, X, R, field, g_rows, T):
    with ExitStack() as ctx:
        L = Kit(nc, ctx, "l1")
        acc = L.sb("acc", [P, NT, D])
        types, weight = field[:, :, R_TYPE], field[:, :, R_EW1]
        conv_nodes(nc, G, "n1", I["L1_gnn_loop_w1"], I["L1_gnn_b1"], T.rows, acc)
        conv_pass(nc, G, "v1", X, T.rows, types, weight, I["L1_gnn_w1"], acc)
        conv_nodes(nc, G, "n2", I["L1_gnn_loop_w2"], I["L1_gnn_b2"], T.rows, acc, relu_of=acc)
        conv_pass(nc, G, "v2", X, T.rows, types, weight, I["L1_gnn_w2"], acc)
        add_to_x(nc, G, "x1", acc[:])


def layer1_experts(nc, G, I, X, R, field, g_rows, T):
    with ExitStack() as ctx:
        L = Kit(nc, ctx, "l1f")
        gates = L.sb("gates", [P, NT, 8])
        b2 = L.sb("b2", [8, D])
        affine = (I["L1_ffn_gamma"], I["L1_ffn_beta"])
        scores_of(nc, G, "g1", I["L1_ffn_Wr"], 8, I["L1_ffn_br"], gates, affine)
        gelu_experts(nc, G, "e1", I["L1_ffn_W1"], I["L1_ffn_b1"], I["L1_ffn_W2"], gates, 8, affine)
        load(nc, "lb1", b2[:], I["L1_ffn_b2"])
        gate_bias(nc, G, "gb1", gates, 8, b2)


def layer2_gnn(nc, G, I, X, R, field, g_rows, T):
    H = 8
    with ExitStack() as ctx:
        L = Kit(nc, ctx, "l2")
        acc = L.sb("acc", [P, NT, D + H])
        alpha = L.sb("alpha", [P, NCH, H])
        with ExitStack() as inner:
            L2 = Kit(nc, inner, "l2h")
            hh = L2.sb("hh", [P, NT, D + H])
            clear(nc, "c2", acc[:])
            gat_nodes(nc, G, I, "a2", I["L2_gnn_W"], None, I["L2_gnn_a_src"].rearrange("h c -> (h c)"),
                      I["L2_gnn_a_dst"].rearrange("h c -> (h c)"), T.rows, T.logit,
                      lambda i: hh[:, bass.ds(i * GT, GT), D:D + H], keep=hh, transposed=True)
            hparts = L2.sb("hparts", [P, NT, 3, D + H], BF16)
            split_rows(nc, "sp2", hh[:], hparts, hh[:])
            edge_attention_pass(nc, G, "b2", X, T.logit, hparts, field[:, :, R_EA3:R_EA3 + 4],
                                (I["L2_gnn_edge_W"].rearrange("n f -> f n"),
                                 I["L2_gnn_edge_b"].rearrange("(o n) -> o n", o=1)), alpha)
        softmax_pass(nc, G, "s2", X, H, alpha[:])
        message_pass(nc, G, "m2", X, H, 32, T.rows, alpha, acc)
        finish_l2_gnn(nc, G, acc, I["L2_gnn_bias"])


def layer2_experts(nc, G, I, X, R, field, g_rows, T):
    with ExitStack() as ctx:
        L = Kit(nc, ctx, "l2f")
        gates = L.sb("gates", [P, NT, 5])
        b3 = L.sb("b3", [5, D])
        clear(nc, "c3", gates[:], 1.0)
        scores_of(nc, G, "g2", I["L2_ffn_gW"], 4, I["L2_ffn_gb"], gates, soft=True)
        relu_experts(nc, G, I, gates)
        load(nc, "lb2", b3[0:4, :], I["L2_ffn_eb3"], b3[4:5, :], I["L2_ffn_sb3"].rearrange("(o n) -> o n", o=1))
        gate_bias(nc, G, "gb2", gates, 5, b3)


def layer3_gnn(nc, G, I, X, R, field, g_rows, T):
    with ExitStack() as ctx:
        L = Kit(nc, ctx, "l3")
        h0 = L.sb("h0", [P, NT, D])
        counted_nodes(nc, G, T.counted)
        with ExitStack() as inner:
            L2 = Kit(nc, inner, "l3a")
            acc = L2.sb("acc", [P, NT, 2, D + 1])
            clear(nc, "c4", acc[:])
            gine_pass(nc, G, I, "v3", X, T.counted, g_rows, acc)
            gine_nodes(nc, G, I, T.counted, acc, h0)
        gine_mlp(nc, G, I, T.counted, h0)


def layer3_ffn(nc, G, I, X, R, field, g_rows, T):
    with ExitStack() as ctx:
        L = Kit(nc, ctx, "l3f")
        wl = L.sb("wl", [P, 2, FULL])
        bl = L.sb("bl", [P, FULL])
        wT = L.sb("wT", [P, PR, NP])
        tok = L.sb("tok", [P, PR, P + 1])
        M4 = L.sb("M4", [P, PR, D])
        slice_logits_weights(nc, G, I, wl, bl)
        slice_pass(nc, G, I, wl, bl, wT, tok)
        slice_attention(nc, G, I, tok, M4)
        unslice(nc, G, I, wT, M4)


SUBLAYERS = [layer0_gnn, layer0_experts, layer1_gnn, layer1_experts, layer2_gnn, layer2_experts, layer3_gnn,
             layer3_ffn]


INPUTS = ("x", "src", "dst", "edge_attr_3", "edge_attr_64", "edge_type_16", "edge_weight", "edge_weight1",
          "L0_gnn_W_lin", "L0_gnn_att_l", "L0_gnn_att_r", "L0_gnn_W_res", "L0_ffn_W_gat", "L0_ffn_att_src",
          "L0_ffn_att_dst", "L0_ffn_b_gat", "L0_ffn_ln_gamma", "L0_ffn_ln_beta", "L0_ffn_W1", "L0_ffn_b1",
          "L0_ffn_W2", "L0_ffn_b2", "L0_ffn_edge_index", "L1_gnn_w1", "L1_gnn_loop_w1", "L1_gnn_b1",
          "L1_gnn_w2", "L1_gnn_loop_w2", "L1_gnn_b2", "L1_ffn_gamma", "L1_ffn_beta", "L1_ffn_Wr", "L1_ffn_br",
          "L1_ffn_W1", "L1_ffn_b1", "L1_ffn_W2", "L1_ffn_b2", "L2_gnn_W", "L2_gnn_a_src", "L2_gnn_a_dst",
          "L2_gnn_edge_W", "L2_gnn_edge_b", "L2_gnn_bias", "L2_ffn_sW1", "L2_ffn_sb1", "L2_ffn_sW2",
          "L2_ffn_sb2", "L2_ffn_sW3", "L2_ffn_sb3", "L2_ffn_eW1", "L2_ffn_eb1", "L2_ffn_eW2", "L2_ffn_eb2",
          "L2_ffn_eW3", "L2_ffn_eb3", "L2_ffn_gW", "L2_ffn_gb", "L3_gnn_eps", "L3_gnn_ee_w1", "L3_gnn_ee_b1",
          "L3_gnn_ee_w2", "L3_gnn_ee_b2", "L3_gnn_w1", "L3_gnn_b1", "L3_gnn_g1", "L3_gnn_be1", "L3_gnn_w2",
          "L3_gnn_b2", "L3_gnn_g2", "L3_gnn_be2", "L3_gnn_w3", "L3_gnn_b3", "L3_gnn_bn_g", "L3_gnn_bn_b",
          "L3_ffn_W_fx", "L3_ffn_b_fx", "L3_ffn_W_x", "L3_ffn_b_x", "L3_ffn_W_slice", "L3_ffn_b_slice",
          "L3_ffn_W_q", "L3_ffn_W_k", "L3_ffn_W_v", "L3_ffn_W_out", "L3_ffn_b_out", "L3_ffn_temperature")


def kernel(**inputs):
    import numpy as np
    import concourse.bacc as bacc
    from concourse.bass_utils import run_bass_kernel_spmd

    nc = bacc.Bacc("TRN2", target_bir_lowering=False, num_devices=1)
    arrays, aps = {}, {}
    for name in INPUTS:
        a = np.ascontiguousarray(inputs[name])
        arrays["in_" + name] = a = a.reshape(a.shape or (1,))
        aps[name] = nc.dram_tensor("in_" + name, a.shape, mybir.dt.from_np(a.dtype), kind="ExternalInput").ap()
    out = nc.dram_tensor("out_x", (N, D), F32, kind="ExternalOutput").ap()
    program(nc, aps, out)
    return run_bass_kernel_spmd(nc, [arrays], core_ids=[0]).results[0]["out_x"]
```
